# Optimizing a Trainium2 kernel written in Bass

```python
import numpy as np
import jax
import jax.numpy as jnp

def _softmax(x, axis=-1):
    return jax.nn.softmax(x, axis=axis)

def _gelu(x):
    return jax.nn.gelu(x, approximate=True)

def _silu(x):
    return jax.nn.silu(x)

def _sigmoid(x):
    return jax.nn.sigmoid(x)

def _layernorm(x, axis=-1, eps=1e-05):
    m = jnp.mean(x, axis=axis, keepdims=True)
    v = jnp.var(x, axis=axis, keepdims=True)
    return (x - m) / jnp.sqrt(v + eps)

def _scatter_add(tgt, idx, src, axis=0):
    return tgt.at[idx].add(src)

def _segment_sum(src, seg, n):
    return jax.ops.segment_sum(src, seg, n)
kernel_name = 'mk_seq_preln_d1_jaxref_r4_446417'

def setup_inputs(seed: int=0):
    np.random.seed(seed)
    _w = jnp.asarray

    def _L0_attn_setup():
        import jax, jax.numpy as jnp
        import numpy as np
        from functools import partial
        B, S, D, H, DK, DV, DFF = (4, 512, 256, 8, 128, 128, 1024)
        EPS = 1e-06

        def rms_norm(x):
            return x * jax.lax.rsqrt(jnp.mean(x * x, axis=-1, keepdims=True) + EPS)

        def l2norm(x):
            return x * jax.lax.rsqrt(jnp.sum(x * x, axis=-1, keepdims=True) + EPS)

        def gated_delta_net(h, Wq, Wk, Wv, Wb, Wa, A_log, dt_bias, Wg, o_norm_w, Wo):
            b, s, _ = h.shape
            q = l2norm(jax.nn.silu(h @ Wq).reshape(b, s, H, DK))
            k = l2norm(jax.nn.silu(h @ Wk).reshape(b, s, H, DK))
            v = jax.nn.silu(h @ Wv).reshape(b, s, H, DV)
            beta = jax.nn.sigmoid(h @ Wb)
            g = -jnp.exp(A_log) * jax.nn.softplus(h @ Wa + dt_bias)
            alpha = jnp.exp(g)
            scale = DK ** (-0.5)
            tm = lambda a: jnp.moveaxis(a, 1, 0)
            qs, ks_, vs, als, bts = (tm(q), tm(k), tm(v), tm(alpha), tm(beta))

            def step(Sst, inp):
                q_t, k_t, v_t, a_t, b_t = inp
                Sst = Sst * a_t[..., None, None]
                kv = jnp.einsum('bhd,bhde->bhe', k_t, Sst)
                delta = (v_t - kv) * b_t[..., None]
                Sst = Sst + jnp.einsum('bhd,bhe->bhde', k_t, delta)
                o_t = jnp.einsum('bhd,bhde->bhe', q_t, Sst) * scale
                return (Sst, o_t)
            S0 = jnp.zeros((b, H, DK, DV), dtype=h.dtype)
            _, o = jax.lax.scan(step, S0, (qs, ks_, vs, als, bts))
            o = jnp.moveaxis(o, 0, 1)
            gate = (h @ Wg).reshape(b, s, H, DV)
            o = rms_norm(o) * o_norm_w * jax.nn.silu(gate)
            return o.reshape(b, s, H * DV) @ Wo
        key = jax.random.key(seed)
        ks = jax.random.split(key, 16)
        w = lambda k, shp: jax.random.normal(k, shp, dtype=jnp.float32) * 0.02
        return {'x': jax.random.normal(ks[0], (B, S, D), dtype=jnp.float32), 'Wq': w(ks[1], (D, H * DK)), 'Wk': w(ks[2], (D, H * DK)), 'Wv': w(ks[3], (D, H * DV)), 'Wb': w(ks[4], (D, H)), 'Wa': w(ks[5], (D, H)), 'A_log': jnp.log(jnp.linspace(1.0, 8.0, H).astype(jnp.float32)), 'dt_bias': jax.random.normal(ks[6], (H,), dtype=jnp.float32) * 0.1, 'Wg': w(ks[7], (D, H * DV)), 'o_norm_w': jnp.ones((DV,), dtype=jnp.float32), 'Wo': w(ks[8], (H * DV, D)), 'W_fc': w(ks[9], (D, DFF)), 'W_proj': w(ks[10], (DFF, D))}
    _L0_attn_in = _L0_attn_setup()

    def _L0_ffn_setup():
        import jax, jax.numpy as jnp
        import numpy as np
        EPS = 0.05
        N_ITERS = 20
        TOP_K = 2

        def _sinkhorn(cost, n_iters=N_ITERS, epsilon=EPS):
            la = cost / epsilon
            for _ in range(n_iters):
                la = la - jax.scipy.special.logsumexp(la, axis=-1, keepdims=True)
                la = la - jax.scipy.special.logsumexp(la, axis=-2, keepdims=True)
            return jnp.exp(la)
        key = jax.random.key(seed)
        k0, k1, k2, k3, k4 = jax.random.split(key, 5)
        B, T, D, F, E = (2, 512, 256, 1024, 8)
        x = jax.random.normal(k0, (B, T, D), dtype=jnp.float32)
        gate_W = jax.random.normal(k1, (E, D), dtype=jnp.float32) * 0.02
        W_gate = jax.random.normal(k2, (E, F, D), dtype=jnp.float32) * 0.02
        W_up = jax.random.normal(k3, (E, F, D), dtype=jnp.float32) * 0.02
        W_down = jax.random.normal(k4, (E, D, F), dtype=jnp.float32) * 0.02
        return {'x': x, 'gate_W': gate_W, 'W_gate': W_gate, 'W_up': W_up, 'W_down': W_down}
    _L0_ffn_in = _L0_ffn_setup()
    _d = {'L0_attn_x': _L0_attn_in['x'], 'L0_attn_Wq': _L0_attn_in['Wq'], 'L0_attn_Wk': _L0_attn_in['Wk'], 'L0_attn_Wv': _L0_attn_in['Wv'], 'L0_attn_Wb': _L0_attn_in['Wb'], 'L0_attn_Wa': _L0_attn_in['Wa'], 'L0_attn_A_log': _L0_attn_in['A_log'], 'L0_attn_dt_bias': _L0_attn_in['dt_bias'], 'L0_attn_Wg': _L0_attn_in['Wg'], 'L0_attn_o_norm_w': _L0_attn_in['o_norm_w'], 'L0_attn_Wo': _L0_attn_in['Wo'], 'L0_attn_W_fc': _L0_attn_in['W_fc'], 'L0_attn_W_proj': _L0_attn_in['W_proj'], 'L0_ffn_gate_W': _L0_ffn_in['gate_W'], 'L0_ffn_W_gate': _L0_ffn_in['W_gate'], 'L0_ffn_W_up': _L0_ffn_in['W_up'], 'L0_ffn_W_down': _L0_ffn_in['W_down']}
    _x0 = _d['L0_attn_x']
    _d['L0_attn_x'] = jax.random.normal(jax.random.fold_in(jax.random.key(seed), 1), (8, 512, 256), dtype=_x0.dtype)
    del _x0
    return _d

def reference(L0_attn_x, L0_attn_Wq, L0_attn_Wk, L0_attn_Wv, L0_attn_Wb, L0_attn_Wa, L0_attn_A_log, L0_attn_dt_bias, L0_attn_Wg, L0_attn_o_norm_w, L0_attn_Wo, L0_attn_W_fc, L0_attn_W_proj, L0_ffn_gate_W, L0_ffn_W_gate, L0_ffn_W_up, L0_ffn_W_down):

    def _L0_attn_ref(x, Wq, Wk, Wv, Wb, Wa, A_log, dt_bias, Wg, o_norm_w, Wo, W_fc, W_proj):
        import jax, jax.numpy as jnp
        import numpy as np
        from functools import partial
        B, S, D, H, DK, DV, DFF = (4, 512, 256, 8, 128, 128, 1024)
        EPS = 1e-06

        def rms_norm(x):
            return x * jax.lax.rsqrt(jnp.mean(x * x, axis=-1, keepdims=True) + EPS)

        def l2norm(x):
            return x * jax.lax.rsqrt(jnp.sum(x * x, axis=-1, keepdims=True) + EPS)

        def gated_delta_net(h, Wq, Wk, Wv, Wb, Wa, A_log, dt_bias, Wg, o_norm_w, Wo):
            b, s, _ = h.shape
            q = l2norm(jax.nn.silu(h @ Wq).reshape(b, s, H, DK))
            k = l2norm(jax.nn.silu(h @ Wk).reshape(b, s, H, DK))
            v = jax.nn.silu(h @ Wv).reshape(b, s, H, DV)
            beta = jax.nn.sigmoid(h @ Wb)
            g = -jnp.exp(A_log) * jax.nn.softplus(h @ Wa + dt_bias)
            alpha = jnp.exp(g)
            scale = DK ** (-0.5)
            tm = lambda a: jnp.moveaxis(a, 1, 0)
            qs, ks_, vs, als, bts = (tm(q), tm(k), tm(v), tm(alpha), tm(beta))

            def step(Sst, inp):
                q_t, k_t, v_t, a_t, b_t = inp
                Sst = Sst * a_t[..., None, None]
                kv = jnp.einsum('bhd,bhde->bhe', k_t, Sst)
                delta = (v_t - kv) * b_t[..., None]
                Sst = Sst + jnp.einsum('bhd,bhe->bhde', k_t, delta)
                o_t = jnp.einsum('bhd,bhde->bhe', q_t, Sst) * scale
                return (Sst, o_t)
            S0 = jnp.zeros((b, H, DK, DV), dtype=h.dtype)
            _, o = jax.lax.scan(step, S0, (qs, ks_, vs, als, bts))
            o = jnp.moveaxis(o, 0, 1)
            gate = (h @ Wg).reshape(b, s, H, DV)
            o = rms_norm(o) * o_norm_w * jax.nn.silu(gate)
            return o.reshape(b, s, H * DV) @ Wo
        ln_scale = 1.0
        h = gated_delta_net(ln_scale * rms_norm(x), Wq, Wk, Wv, Wb, Wa, A_log, dt_bias, Wg, o_norm_w, Wo)
        x = x + h
        m = ln_scale * rms_norm(x)
        y = jnp.square(jax.nn.relu(m @ W_fc)) @ W_proj
        return x + y

    def _L0_ffn_ref(x, gate_W, W_gate, W_up, W_down):
        import jax, jax.numpy as jnp
        import numpy as np
        EPS = 0.05
        N_ITERS = 20
        TOP_K = 2

        def _sinkhorn(cost, n_iters=N_ITERS, epsilon=EPS):
            la = cost / epsilon
            for _ in range(n_iters):
                la = la - jax.scipy.special.logsumexp(la, axis=-1, keepdims=True)
                la = la - jax.scipy.special.logsumexp(la, axis=-2, keepdims=True)
            return jnp.exp(la)
        B, T, D = x.shape
        xf = x.reshape(B * T, D)
        logits = xf @ gate_W.T
        pi = _sinkhorn(-logits)
        _, top_idx = jax.lax.top_k(pi, TOP_K)
        g = jnp.einsum('nd,efd->enf', xf, W_gate)
        u = jnp.einsum('nd,efd->enf', xf, W_up)
        y = jnp.einsum('enf,edf->end', jax.nn.silu(g) * u, W_down)
        n_ar = jnp.arange(xf.shape[0])
        out = jnp.zeros_like(xf)
        for k in range(TOP_K):
            out = out + y[top_idx[:, k], n_ar] * pi[:, k:k + 1]
        return out.reshape(B, T, D)
    x = L0_attn_x
    x = x + _L0_attn_ref(_layernorm(x, axis=-1), L0_attn_Wq, L0_attn_Wk, L0_attn_Wv, L0_attn_Wb, L0_attn_Wa, L0_attn_A_log, L0_attn_dt_bias, L0_attn_Wg, L0_attn_o_norm_w, L0_attn_Wo, L0_attn_W_fc, L0_attn_W_proj)
    x = x + _L0_ffn_ref(_layernorm(x, axis=-1), L0_ffn_gate_W, L0_ffn_W_gate, L0_ffn_W_up, L0_ffn_W_down)
    return x

_drawn_inputs = setup_inputs


def setup_inputs(seed=0):
    import zlib

    import numpy as np

    out = dict(_drawn_inputs(seed))
    spreads = {'L0_attn_o_norm_w': (1.0, 0.6)}
    factors = {'L0_attn_Wb': 27.306,
     'L0_attn_Wa': 64.0,
     'L0_attn_A_log': 57.698,
     'L0_attn_dt_bias': 64.0,
     'L0_ffn_gate_W': 43.434,
     'L0_ffn_W_gate': 47.303,
     'L0_ffn_W_up': 41.235,
     'L0_ffn_W_down': 41.272}
    for name, (base, spread) in spreads.items():
        noise = np.random.default_rng([zlib.crc32(name.encode()), seed]).standard_normal(out[name].shape)
        drawn = base * np.exp(spread * noise) if base else spread * noise
        out[name] = jnp.asarray(drawn.astype(out[name].dtype))
    for name, factor in factors.items():
        out[name] = (out[name] * factor).astype(out[name].dtype)
    return out
```

```python
from contextlib import ExitStack

import numpy as np
import concourse.bass as bass
from concourse import mybir

F32 = mybir.dt.float32
I32 = mybir.dt.int32
ALU = mybir.AluOpType
ACT = mybir.ActivationFunctionType
X = mybir.AxisListType.X

P = 128
BATCH, SEQ, D = 8, 512, 256
H, DK, F = 8, 128, 1024
E, TOPK, ROUNDS, EPSILON = 8, 2, 20, 0.05
KD = D // P
CHUNKS = SEQ // P
TILES = BATCH * CHUNKS
TOKENS = BATCH * SEQ
HD = H * DK
G = 2
HG = H // G
GW = HG * DK
LEVELS = 7
FB = F // P
WCOLS = 3 * KD * F
ROWS = 256
RB = ROWS // P
ETILES = (TOKENS * TOPK + E * (ROWS - 1)) // ROWS
MAXT = TOKENS // ROWS
LN_EPS, RMS_EPS = 1e-5, 1e-6
DEAD = 110.0
EXP_ZERO = -87.33654

BETA, GAM, NGAM, GTOT, DEND, GLOG = (8 * n for n in range(6))
NSC = 48

FU_PROJ, FU_D, FU_K, FU_KB, FU_Q, FU_KKQ, FU = 0, 8, 10, 12, 14, 16, 20
BU_KBS, BU_QS, BU_U, BU_PU, BU_KDU, BU_PREP, BU_OT, BU_WO, BU_MT, BU_FC, BU_PROJ, BU_XT, BU_LG, BU = (
    0, 2, 4, 6, 8, 10, 13, 15, 16, 17, 19, 20, 21, 22)


class Chain:

    def __init__(self, eng, sem, base=0):
        self.eng, self.sem, self.base, self.n = eng, sem, base, 0

    def link(self, ins):
        self.n += 1
        ins.then_inc(self.sem, 1)
        self.eng.wait_ge(self.sem, self.base + self.n)


def over_heads(m, n=HG):
    return m.unsqueeze(1).to_broadcast([m.shape[0], n, m.shape[1]])


def per_head(s, k=DK):
    return s.unsqueeze(2).to_broadcast([s.shape[0], s.shape[1], k])


def program(nc, x, Wq, Wk, Wv, Wb, Wa, A_log, dt_bias, Wg, o_norm_w, Wo, W_fc, W_proj,
            gate_W, W_gate, W_up, W_down, out):
    x_tiles = x.rearrange("b (c p) d -> (b c) p d", p=P)
    out_tiles = out.rearrange("b (c p) d -> (b c) p d", p=P)
    hT_d = nc.dram_tensor("hT_d", [TILES, P, D], F32)
    xln_d = nc.dram_tensor("xln_d", [TILES, P, D], F32)
    x1_d = nc.dram_tensor("x1_d", [TILES, P, D], F32)
    xf_d = nc.dram_tensor("xf_d", [TILES, P, D], F32)
    wts_d = nc.dram_tensor("wts_d", [E, P, WCOLS], F32)
    xs_d = nc.dram_tensor("xs_d", [ETILES * ROWS, D], F32)
    ys_d = nc.dram_tensor("ys_d", [ETILES * ROWS, D], F32)

    with ExitStack() as ctx:
        def sb(name, shape, dt=F32):
            return ctx.enter_context(nc.sbuf_tensor(name, shape, dt))

        def sem(name):
            return ctx.enter_context(nc.semaphore(name))

        ident = sb("ident", [P, P])
        ones = sb("ones", [P, P])
        incl = sb("incl", [P, P])
        upper = sb("upper", [P, P])
        lower = sb("lower", [P, P])
        xor = sb("xor", [P, P])
        iota_i = sb("iota_i", [P, 2, P], I32)
        level_mask = sb("level_mask", [P, LEVELS, P])
        neg_m0t = sb("neg_m0t", [P, P])
        tile_iota = sb("tile_iota", [1, ETILES])
        thresholds = sb("thresholds", [P, MAXT])
        rank_w = sb("rank_w", [P, E])
        weights = sb("weights", [P, 7 * KD * HD])
        wqkvg = weights[:, 0:4 * KD * HD].rearrange("p (w k n) -> p w k n", w=4, k=KD)
        wo = weights[:, 4 * KD * HD:5 * KD * HD].rearrange("p (h n) -> p h n", h=H)
        wfc = weights[:, 5 * KD * HD:6 * KD * HD].rearrange("p (k n) -> p k n", k=KD)
        wproj = weights[:, 6 * KD * HD:7 * KD * HD].rearrange("p (f n) -> p f n", f=FB)
        wba = sb("wba", [P, KD, 2 * H])
        gwT = sb("gwT", [P, KD, E])
        onorm = sb("onorm", [P, DK])
        alog = sb("alog", [P, H])
        dtb = sb("dtb", [P, H])
        ba = sb("ba", [P, TILES, 2 * H])
        dec = sb("dec", [P, TILES, NSC])
        la = sb("la", [P, TILES, E])
        hT = sb("hT", [P, 2, KD, P])
        q_s = sb("q_s", [P, HD])
        k_s = sb("k_s", [P, HD])
        v_s = sb("v_s", [P, HD])
        g_s = sb("g_s", [P, HD])
        kb = sb("kb", [P, HD])
        kT = sb("kT", [P, H, P])
        kbqT = sb("kbqT", [P, 2, H, 2, P])
        dT = sb("dT", [P, H, P])
        aP = sb("aP", [P, 2, H, 2, P])
        kd = sb("kd", [P, HD])
        vb = sb("vb", [P, HD])
        gw = sb("gw", [P, HD])
        sc = sb("sc", [P, 2, NSC])
        junk = sb("junk", [P, D])
        ss = sb("ss", [P, 2 * H])
        nv = sb("nv", [P, 2 * H])
        nl = sb("nl", [P, 2 * H])
        nr = sb("nr", [P, 2 * H])
        na = sb("na", [P, 2 * H])
        rn = sb("rn", [P, 2 * H])
        xi = sb("xi", [P, HD])
        yi = sb("yi", [P, HD])
        ti = sb("ti", [P, HD])
        state = sb("state", [P, HD])
        r_s = sb("r_s", [P, HD])
        u_s = sb("u_s", [P, HD])
        qsg = sb("qsg", [P, HD])
        o_s = sb("o_s", [P, HD])
        oT = sb("oT", [P, HD])
        hid = kb
        xin = sb("xin", [P, 2, D])
        x2 = sb("x2", [P, D])
        m_s = sb("m_s", [P, D])
        mT = sb("mT", [P, D])
        x1 = sb("x1", [P, D])
        xf = sb("xf", [P, D])
        xfT = sb("xfT", [P, D])
        bst = sb("bst", [P, 6])
        bag = sb("bag", [P, 2])
        tv = sb("tv", [P, H])
        tl = sb("tl", [P, H])
        tr = sb("tr", [P, H])
        ta = sb("ta", [P, H])
        to = sb("to", [P, H])
        ts = sb("ts", [P, H])
        wnat = sb("wnat", [P, 3, 2 * D])
        wst = sb("wst", [P, 3, 2 * D])

        psI = [[ctx.enter_context(nc.psum_tensor(f"ps_inv{n}{g}", [P, GW], F32)) for g in range(G)] for n in "ab"]
        psF = [ctx.enter_context(nc.psum_tensor(f"ps_front{n}", [P, GW], F32)) for n in range(2)]
        psB = [ctx.enter_context(nc.psum_tensor(f"ps_back{n}", [P, GW], F32)) for n in range(2)]

        w_loaded = sem("w_loaded")
        small_loaded = sem("small_loaded")
        consts = sem("consts")
        const_dve = sem("const_dve")
        zeroed = sem("zeroed")
        zero_made = sem("zero_made")
        xb_loaded, xb_free = sem("xb_loaded"), sem("xb_free")
        pre_dve, pre_act = sem("pre_dve"), sem("pre_act")
        pre_v, pre_r, pre_xln, pre_ss, pre_v2, pre_r2, pre_h = (
            sem(n) for n in ("pre_v", "pre_r", "pre_xln", "pre_ss", "pre_v2", "pre_r2", "pre_h"))
        pre_tr, pre_hT, pre_ba, ba_ready = (sem(n) for n in ("pre_tr", "pre_hT", "pre_ba", "ba_ready"))
        xln_stored, hT_stored = sem("xln_stored"), sem("hT_stored")
        dec_dve, dec_act, dec_pe = sem("dec_dve"), sem("dec_act"), sem("dec_pe")
        dec_ready = sem("dec_ready")
        hT_loaded = [sem("hT_loaded0"), sem("hT_loaded1")]
        front_filled = [sem("front_filled0"), sem("front_filled1")]
        front_evac = [sem("front_evac0"), sem("front_evac1")]
        sq_ready = sem("sq_ready")
        sc_ready, rhs_ready, ss_ready, nv_ready, nr_ready = (
            sem(n) for n in ("sc_ready", "rhs_ready", "ss_ready", "nv_ready", "nr_ready"))
        front_dve, front_act = sem("front_dve"), sem("front_act")
        kn_ready, qn_ready, kb_ready, dtm_ready = (sem(n) for n in ("kn_ready", "qn_ready", "kb_ready", "dtm_ready"))
        vb_ready, kd_ready, gw_ready = (sem(n) for n in ("vb_ready", "kd_ready", "gw_ready"))
        inv_filled = [[sem(f"inv_{n}_filled{g}") for g in range(G)] for n in "ab"]
        x_ready = [sem(f"x_ready{g}") for g in range(G)]
        y_ready = [sem(f"y_ready{g}") for g in range(G)]
        t_ready = [sem(f"t_ready{g}") for g in range(G)]
        y0_dve = sem("y0_dve")
        back_filled = [sem("back_filled0"), sem("back_filled1")]
        back_evac = [sem("back_evac0"), sem("back_evac1")]
        xin_loaded, wnat_loaded, wst_stored = sem("xin_loaded"), sem("wnat_loaded"), sem("wst_stored")
        x1_stored, xf_stored = sem("x1_stored"), sem("xf_stored")
        hid_ready = sem("hid_ready")
        tail_dve, tail_act = sem("tail_dve"), sem("tail_act")
        so_ready, ov_ready, or_ready, og_ready = (sem(n) for n in ("so_ready", "ov_ready", "or_ready", "og_ready"))
        sm_ready, mv_ready, mr_ready, m_ready = (sem(n) for n in ("sm_ready", "mv_ready", "mr_ready", "m_ready"))
        x1_ready, fv_ready, frr_ready, xf_ready = (sem(n) for n in ("x1_ready", "fv_ready", "frr_ready", "xf_ready"))

        def f_filled(f, u):
            return FU // 2 * f + u // 2 + 1

        def f_evac(f, u):
            return FU // 2 * f + u // 2 + 2

        def b_filled(t, u):
            return BU // 2 * t + u // 2 + 1

        def b_evac(t, u):
            return BU // 2 * t + u // 2 + 2

        NFD, NTD, NFA, NTA = 3, 12, 1, 3

        xb = q_s[:, :].rearrange("p (c d) -> p c d", c=CHUNKS)
        xlnb = k_s[:, :].rearrange("p (c d) -> p c d", c=CHUNKS)
        hb = v_s[:, :].rearrange("p (c d) -> p c d", c=CHUNKS)
        hTb = g_s[:, :].rearrange("p (c k n) -> p c k n", c=CHUNKS, k=KD)
        pbst = kb[:, 0:6 * CHUNKS].rearrange("p (c n) -> p c n", c=CHUNKS)
        pmv = kb[:, 32:32 + 2 * CHUNKS].rearrange("p (c n) -> p c n", c=CHUNKS)
        pv, pl, pr, pa, prr, pss, pv2, pl2, pr2, pa2, prr2 = (
            kb[:, 64 + 8 * n:64 + 8 * n + CHUNKS] for n in range(11))
        psq = dT[:, :, :].rearrange("p h n -> p (h n)")
        zero = wst[:, :, :].rearrange("p a n -> p (a n)")
        ZR = 3 * 2 * D // D

        V3 = lambda a: a.rearrange("p (t e) -> p t e", e=E)
        by_expert = lambda a: a.rearrange("p t e -> p e t")
        over_tiles = lambda s: s.unsqueeze(1).to_broadcast([P, TILES, E])
        TE = TILES * E
        z_b, az_b, tt_b, s_b, s2_b, p_b, den_b = (V3(a[:, 0:TE]) for a in (xi, yi, ti, r_s, u_s, qsg, o_s))
        al1, al2, e1, e2 = (oT[:, n * H:(n + 1) * H] for n in range(4))
        sd, se, pi = V3(xi[:, 0:TE]), V3(yi[:, 0:TE]), V3(ti[:, 0:TE])
        rowm, rows_, rowl = (r_s[:, n * TILES:(n + 1) * TILES] for n in range(3))
        colm, cmx, cdiag, cols_, coll = r_s[:, 96:104], r_s[0:E, 104:105], r_s[0:E, 112:120], r_s[:, 120:128], r_s[:, 128:136]
        cand, hot, hot2, both = (V3(a[:, 0:TE]) for a in (u_s, qsg, o_s, oT))
        cnt = [V3(hid[:, n * TE:(n + 1) * TE]) for n in range(2)]
        posf = V3(hid[:, 2 * TE:3 * TE])
        need3 = hid[:, 3 * TE:3 * TE + E * MAXT].rearrange("p (e n) -> p e n", e=E)
        need = [r_s[:, 136 + 8 * n:144 + 8 * n] for n in range(4)]
        posk = r_s[:, 256:256 + TILES * TOPK].rearrange("p (t k) -> p t k", k=TOPK)
        tef = r_s[0:1, 384:384 + ETILES]
        te3 = u_s[0:1, 512:512 + ETILES * E].rearrange("p (j e) -> p j e", e=E)
        posi = sb("posi", [P, TILES, TOPK], I32)
        te_i = sb("te_i", [1, ETILES], I32)
        pidx = sb("pidx", [P, 2, CHUNKS, TOPK], I32)
        pw = sb("pw", [P, 2, CHUNKS, TOPK])
        sk_dve, sk_act, sk_pe = sem("sinkhorn_dve"), sem("sinkhorn_act"), sem("sinkhorn_pe")
        rt_dve, rt_pe, pi_ready = sem("routing_dve"), sem("routing_pe"), sem("pi_ready")
        te_ready, pos_ready = sem("te_ready"), sem("pos_ready")
        xf4_loaded = [sem("xf4_loaded0"), sem("xf4_loaded1")]
        pidx_ready = sem("pidx_ready")
        scattered = [sem("scattered0"), sem("scattered1")]
        pool_turn, sp_turn, dve_turn = sem("pool_turn"), sem("sp_turn"), sem("dve_turn")
        NPAIR = ETILES // 2
        wbuf = [weights[:, n * WCOLS:(n + 1) * WCOLS] for n in range(2)]
        w_in = [wb_[:, 0:2 * KD * F].rearrange("p (w k f) -> p w k f", w=2, k=KD) for wb_ in wbuf]
        w_dn = [wb_[:, 2 * KD * F:].rearrange("p (f d) -> p f d", f=FB) for wb_ in wbuf]
        xrow = [q_s[:, n * RB * D:(n + 1) * RB * D].rearrange("p (r d) -> p r d", r=RB) for n in range(2)]
        xT = [k_s[:, n * KD * ROWS:(n + 1) * KD * ROWS].rearrange("p (k n) -> p k n", k=KD) for n in range(2)]
        eh = [kbqT[:, n].rearrange("p h a n -> p (h a n)").rearrange("p (f n) -> p f n", f=FB) for n in range(2)]
        sact = vb[:, :].rearrange("p (s n) -> p s n", s=4)
        ybuf = [kd[:, n * RB * D:(n + 1) * RB * D] for n in range(2)]
        psG = [psI[0][0], psI[0][1], psI[1][0], psI[1][1]]
        NSLOT = len(psG)
        wg_loaded = [sem("w_in_loaded0"), sem("w_in_loaded1")]
        wd_loaded = [sem("w_down_loaded0"), sem("w_down_loaded1")]
        xrow_loaded = [sem("xrow_loaded0"), sem("xrow_loaded1")]
        xT_filled, xT_ready = sem("xT_filled"), sem("xT_ready")
        gu_filled = [sem(f"gu_filled{n}") for n in range(NSLOT)]
        sact_ready = [sem(f"sact_ready{n}") for n in range(NSLOT)]
        eh_ready = [sem(f"eh_ready{n}") for n in range(NSLOT)]
        y_filled, y_evac = sem("y_filled"), sem("y_evac")
        y_stored = [sem("y_stored0"), sem("y_stored1")]
        x14_loaded = [sem("x14_loaded0"), sem("x14_loaded1")]
        gathered = [sem("gathered0"), sem("gathered1")]
        mix_dve, mixed = sem("mix_dve"), sem("mixed")
        out_stored = [sem("out_stored0"), sem("out_stored1")]
        xb2 = [a[:, :].rearrange("p (c d) -> p c d", c=CHUNKS) for a in (q_s, k_s)]
        yg = [kbqT[:, n].rearrange("p h a n -> p (h a n)").rearrange("p (c k d) -> p c k d", c=CHUNKS, k=TOPK) for n in range(2)]
        SOFTPLUS_TERMS = [1 / 13, 1 / 11, 1 / 9, 1 / 7, 1 / 5, 1 / 3]
        ND_DEC = 23
        SK_D, SK_A, SK_P = 10, 4, 3

        def dve_decays(dve):
            V = nc.vector
            ch = Chain(dve, dec_dve)
            dve.wait_ge(ba_ready, BATCH)
            dve.wait_ge(small_loaded, 16 * 7)
            ch.link(V.tensor_tensor(z_b, ba[:, :, H:2 * H], over_tiles(dtb[:, :]), ALU.add))
            ch.link(V.scalar_tensor_tensor(az_b, z_b, -1.0, z_b, ALU.mult, ALU.max))
            ch.link(V.tensor_scalar(al1, alog[:, :], 80.0, None, ALU.min))
            ch.link(V.tensor_scalar(al2, alog[:, :], -80.0, 0.0, ALU.add, ALU.max))
            ch.link(V.tensor_scalar(al2, al2, 80.0, None, ALU.min))
            dve.wait_ge(dec_act, 3)
            ch.link(V.tensor_scalar(den_b, tt_b, 2.0, None, ALU.add))
            ch.link(V.reciprocal(den_b, den_b))
            ch.link(V.tensor_tensor(s_b, tt_b, den_b, ALU.mult))
            ch.link(V.tensor_tensor(s2_b, s_b, s_b, ALU.mult))
            ch.link(V.tensor_scalar(p_b, s2_b, 1 / 15, None, ALU.mult))
            for c in SOFTPLUS_TERMS:
                ch.link(V.scalar_tensor_tensor(p_b, p_b, c, s2_b, ALU.add, ALU.mult))
            ch.link(V.scalar_tensor_tensor(p_b, p_b, 1.0, s_b, ALU.add, ALU.mult))
            ch.link(V.tensor_scalar(z_b, z_b, 0.0, None, ALU.max))
            ch.link(V.scalar_tensor_tensor(p_b, p_b, 2.0, z_b, ALU.mult, ALU.add))
            ch.link(V.tensor_tensor(p_b, p_b, over_tiles(e1), ALU.mult))
            ch.link(V.tensor_scalar(p_b, p_b, 1e3, None, ALU.min))
            ch.link(V.tensor_tensor(p_b, p_b, over_tiles(e2), ALU.mult))
            ch.link(V.tensor_scalar(dec[:, :, GLOG:GLOG + H], p_b, -1.0, -DEAD, ALU.mult, ALU.max))
            assert ch.n == ND_DEC
            dve.wait_ge(dec_act, 7)
            ch.link(V.tensor_scalar(dec[:, :, NGAM:NGAM + H], dec[:, :, GAM:GAM + H], -1.0, None, ALU.mult))
            V.memset(dec[:, 0:TILES:CHUNKS, GAM:GTOT + H], 0.0).then_inc(dec_ready, 1)

        def act_decays(act):
            A = nc.scalar.activation
            act.wait_ge(dec_dve, 5)
            A(tt_b, az_b, ACT.Exp, scale=-1.0).then_inc(dec_act, 1)
            A(e1, al1, ACT.Exp).then_inc(dec_act, 1)
            A(e2, al2, ACT.Exp).then_inc(dec_act, 1)
            A(dec[:, :, BETA:BETA + H], ba[:, :, 0:H], ACT.Sigmoid).then_inc(dec_act, 1)
            act.wait_ge(dec_pe, 3)
            for ps, c in ((psF[0], GAM), (psF[1], GTOT), (psB[0], DEND)):
                A(dec[:, :, c:c + H], V3(ps[:, 0:TE]), ACT.Exp).then_inc(dec_act, 1)

        def pe_decays(pe):
            pe.wait_ge(dec_dve, ND_DEC)
            for ps, mask in ((psF[0], incl), (psF[1], ones), (psB[0], lower)):
                nc.tensor.matmul(V3(ps[:, 0:TE]), mask[:, :], dec[:, :, GLOG:GLOG + H], start=True, stop=True).then_inc(dec_pe, 1)
            pe.wait_ge(dec_act, 7)

        def dve_late(dve):
            V = nc.vector
            dve.wait_ge(back_evac[1], BU // 2 * TILES + 1)
            with dve.Fori(0, ROUNDS) as r:
                ch = Chain(dve, sk_dve, SK_D * r)
                ch.link(V.tensor_reduce(rowm, la[:, :, :], X, ALU.max))
                ch.link(V.tensor_tensor(sd, la[:, :, :], per_head(rowm, E), ALU.subtract))
                dve.wait_ge(sk_act, SK_A * r + 1)
                ch.link(V.tensor_reduce(rows_, se, X, ALU.add))
                dve.wait_ge(sk_act, SK_A * r + 2)
                ch.link(V.tensor_tensor(la[:, :, :], sd, per_head(rowl, E), ALU.subtract))
                ch.link(V.tensor_reduce(colm, by_expert(la[:, :, :]), X, ALU.max))
                dve.wait_ge(sk_pe, SK_P * r + 1)
                ch.link(V.tensor_reduce(cmx, psF[0][0:E, 0:P], X, ALU.max))
                ch.link(V.tensor_scalar(cdiag, ident[0:E, 0:E], cmx, None, ALU.mult))
                dve.wait_ge(sk_pe, SK_P * r + 2)
                ch.link(V.tensor_tensor(sd, la[:, :, :], over_tiles(psF[1][:, 0:E]), ALU.subtract))
                dve.wait_ge(sk_act, SK_A * r + 3)
                ch.link(V.tensor_reduce(cols_, by_expert(se), X, ALU.add))
                dve.wait_ge(sk_act, SK_A * r + 4)
                ch.link(V.tensor_tensor(la[:, :, :], sd, over_tiles(coll), ALU.subtract))
                assert ch.n == SK_D
            ch = Chain(dve, rt_dve)
            ch.link(V.tensor_scalar(sd, la[:, :, :], EXP_ZERO, None, ALU.max))
            for n, h in enumerate((hot, hot2)):
                ch.link(V.tensor_reduce(rowm, sd, X, ALU.max))
                ch.link(V.tensor_tensor(se, sd, per_head(rowm, E), ALU.is_equal))
                ch.link(V.tensor_tensor(cand, se, over_tiles(rank_w[:, :]), ALU.mult))
                ch.link(V.tensor_reduce(rows_, cand, X, ALU.max))
                ch.link(V.tensor_tensor(h, cand, per_head(rows_, E), ALU.is_equal))
                if n == 0:
                    ch.link(V.scalar_tensor_tensor(sd, h, -1e30, sd, ALU.mult, ALU.add))
            ch.link(V.tensor_tensor(both, hot, hot2, ALU.add))
            assert ch.n == 13
            dve.wait_ge(rt_pe, 2)
            ch.link(V.tensor_copy(cnt[0], V3(psF[1][:, 0:TE])))
            cur = 0
            for s in (1, 2, 4, 8, 16):
                V.tensor_copy(cnt[1 - cur][:, 0:s], cnt[cur][:, 0:s])
                ch.link(V.tensor_tensor(cnt[1 - cur][:, s:], cnt[cur][:, s:], cnt[cur][:, 0:TILES - s], ALU.add))
                cur = 1 - cur
            ch.link(V.tensor_tensor(posf, cnt[cur], V3(psF[1][:, 0:TE]), ALU.subtract))
            ch.link(V.tensor_tensor(posf, posf, V3(psF[0][:, 0:TE]), ALU.add))
            ch.link(V.tensor_tensor(need3, per_head(cnt[cur][:, TILES - 1, :], MAXT), thresholds[:, :].unsqueeze(1).to_broadcast([P, E, MAXT]), ALU.is_gt))
            ch.link(V.tensor_reduce(need[0], need3, X, ALU.add))
            ch.link(V.tensor_copy(need[1], need[0]))
            a, b = need[1], need[2]
            for s in (1, 2, 4):
                V.tensor_copy(b[:, 0:s], a[:, 0:s])
                ch.link(V.tensor_tensor(b[:, s:], a[:, s:], a[:, 0:E - s], ALU.add))
                a, b = b, a
            ch.link(V.tensor_tensor(need[3], a, need[0], ALU.subtract))
            ch.link(V.tensor_scalar(need[3], need[3], float(ROWS), None, ALU.mult))
            ch.link(V.tensor_tensor(posf, posf, over_tiles(need[3]), ALU.add))
            for k, h in enumerate((hot, hot2)):
                ch.link(V.tensor_tensor(cand, h, posf, ALU.mult))
                ch.link(V.tensor_reduce(posk[:, :, k], cand, X, ALU.add))
            V.tensor_copy(posi[:, :, :], posk).then_inc(pos_ready, 1)
            ch.link(V.tensor_tensor(te3, tile_iota[:, :].unsqueeze(2).to_broadcast([1, ETILES, E]), a[0:1, :].unsqueeze(1).to_broadcast([1, ETILES, E]), ALU.is_ge))
            ch.link(V.tensor_reduce(tef, te3, X, ALU.add))
            ch.link(V.tensor_scalar(tef, tef, float(E - 1), None, ALU.min))
            V.tensor_copy(te_i[:, :], tef).then_inc(te_ready, 1)
            dve.wait_ge(pos_ready, 1)
            def places(b, p):
                V.tensor_copy(pidx[:, p], posi[:, bass.ds(b * CHUNKS, CHUNKS), :]).then_inc(pidx_ready, 1)

            for p in range(2):
                places(p, p)
            with dve.Fori(1, BATCH // 2) as i:
                for p in range(2):
                    dve.wait_ge(scattered[p], 128 * i)
                    places(2 * i + p, p)

            def expert(j, p):
                for fb in range(FB):
                    s, n = fb % NSLOT, FB // NSLOT * j + fb // NSLOT
                    dve.wait_ge(sact_ready[s], n + 1)
                    V.tensor_tensor(eh[p][:, fb, :], sact[:, s, :], psG[s][:, ROWS:2 * ROWS], ALU.mult).then_inc(eh_ready[s], 1)

            with dve.Fori(0, NPAIR) as i:
                for p in range(2):
                    expert(2 * i + p, p)
            expert(ETILES - 1, 0)
            dve.wait_ge(pi_ready, 1)
            for p in range(2):
                dve.wait_ge(scattered[p], 128 * (BATCH // 2))
                places(p, p)

            def mix(b, p, i):
                ch = Chain(dve, mix_dve, 2 * b)
                ch.link(V.tensor_copy(pw[:, p], pi[:, bass.ds(b * CHUNKS, CHUNKS), 0:TOPK]))
                dve.wait_ge(x14_loaded[p], 16 * i + 16)
                dve.wait_ge(gathered[p], 128 * i + 128)
                for k in range(TOPK):
                    for c in range(CHUNKS):
                        ins = V.scalar_tensor_tensor(xb2[p][:, c, :], yg[p][:, c, k, :], pw[:, p, c, k:k + 1], xb2[p][:, c, :], ALU.mult, ALU.add)
                    if k == 0:
                        ch.link(ins)
                ins.then_inc(mixed, 1)

            with dve.Fori(0, BATCH // 2 - 1) as i:
                for p in range(2):
                    mix(2 * i + p, p, i)
                    places(2 * i + p + 2, p)
            for p in range(2):
                mix(BATCH - 2 + p, p, BATCH // 2 - 1)

        def act_late(act):
            A = nc.scalar.activation
            with act.Fori(0, ROUNDS) as r:
                act.wait_ge(sk_dve, SK_D * r + 2)
                A(se, sd, ACT.Exp).then_inc(sk_act, 1)
                act.wait_ge(sk_dve, SK_D * r + 3)
                A(rowl, rows_, ACT.Ln).then_inc(sk_act, 1)
                act.wait_ge(sk_dve, SK_D * r + 8)
                A(se, sd, ACT.Exp).then_inc(sk_act, 1)
                act.wait_ge(sk_pe, SK_P * r + 3)
                A(coll, psB[0][:, 0:E], ACT.Ln).then_inc(sk_act, 1)
            act.wait_ge(sk_dve, SK_D * ROUNDS)
            A(pi, la[:, :, :], ACT.Exp).then_inc(pi_ready, 1)

            def rows_T(j, p):
                act.wait_ge(xT_filled, j + 1)
                A(xT[p].rearrange("p k n -> p (k n)"), psF[p][:, :], ACT.Copy).then_inc(xT_ready, 1)

            def expert(j, p, i, more):
                for fb in range(FB):
                    s, n = fb % NSLOT, FB // NSLOT * j + fb // NSLOT
                    act.wait_ge(eh_ready[s], n + 1)
                    act.wait_ge(gu_filled[s], n + 1)
                    A(sact[:, s, :], psG[s][:, 0:ROWS], ACT.Silu).then_inc(sact_ready[s], 1)
                if more:
                    rows_T(j + 1, 1 - p)
                act.wait_ge(y_stored[p], 16 * i + 16)
                act.wait_ge(y_filled, j + 1)
                A(ybuf[p], psB[p][:, :], ACT.Copy).then_inc(y_evac, 1)
                act.wait_ge(y_evac, j + 3)
                act.dma_start(ys_d[bass.ds(j * ROWS, ROWS), :].rearrange("(r p) d -> p r d", p=P), ybuf[p].rearrange("p (r d) -> p r d", r=RB)).then_inc(y_stored[p], 16)

            rows_T(0, 0)
            with act.Fori(0, NPAIR) as i:
                for p in range(2):
                    expert(2 * i + p, p, i, True)
            expert(ETILES - 1, 0, NPAIR, False)

        def pe_late(pe):
            MM = nc.tensor.matmul
            with pe.Fori(0, ROUNDS) as r:
                pe.wait_ge(sk_dve, SK_D * r + 5)
                nc.tensor.transpose(psF[0][0:E, 0:P], colm, ident[:, :]).then_inc(sk_pe, 1)
                pe.wait_ge(sk_dve, SK_D * r + 7)
                MM(psF[1][:, 0:E], ones[0:E, :], cdiag, start=True, stop=True).then_inc(sk_pe, 1)
                pe.wait_ge(sk_dve, SK_D * r + 9)
                MM(psB[0][:, 0:E], ones[:, :], cols_, start=True, stop=True).then_inc(sk_pe, 1)
            pe.wait_ge(rt_dve, 13)
            MM(V3(psF[0][:, 0:TE]), upper[:, :], both, start=True, stop=True).then_inc(rt_pe, 1)
            MM(V3(psF[1][:, 0:TE]), ones[:, :], both, start=True, stop=True).then_inc(rt_pe, 1)

            def rows_T(j, p, i):
                pe.wait_ge(xrow_loaded[p], 16 * i + 16)
                pe.wait_ge(xT_ready, j + 1)
                for k in range(KD):
                    for r in range(RB):
                        c = (k * RB + r) * P
                        last = nc.tensor.transpose(psF[p][:, c:c + P], xrow[p][:, r, k * P:(k + 1) * P], ident[:, :])
                last.then_inc(xT_filled, 1)

            def expert(j, p, i, more):
                pe.wait_ge(xT_ready, j + 3)
                pe.wait_ge(wg_loaded[p], 32 * i + 32)
                for fb in range(FB):
                    s, n = fb % NSLOT, FB // NSLOT * j + fb // NSLOT
                    pe.wait_ge(eh_ready[s], n + 1)
                    for w in range(2):
                        for k in range(KD):
                            last = MM(psG[s][:, w * ROWS:(w + 1) * ROWS], w_in[p][:, w, k, fb * P:(fb + 1) * P], xT[p][:, k, :], start=k == 0, stop=k == KD - 1)
                    last.then_inc(gu_filled[s], 1)
                if more:
                    rows_T(j + 1, 1 - p, i + p)
                pe.wait_ge(wd_loaded[p], 16 * i + 16)
                pe.wait_ge(y_evac, j + 1)
                for s in range(NSLOT):
                    pe.wait_ge(eh_ready[s], FB // NSLOT * (j + 1) + 1)
                for r in range(RB):
                    for fb in range(FB):
                        last = MM(psB[p][:, r * D:(r + 1) * D], eh[p][:, fb, r * P:(r + 1) * P], w_dn[p][:, fb, :], start=fb == 0, stop=fb == FB - 1)
                last.then_inc(y_filled, 1)

            pe.wait_ge(te_ready, 1)
            rows_T(0, 0, 0)
            with pe.Fori(0, NPAIR) as i:
                for p in range(2):
                    expert(2 * i + p, p, i, True)
            expert(ETILES - 1, 0, NPAIR, False)

        def pool_late(pool):
            for s in eh_ready:
                pool.sem_inc(s, 1)
            pool.sem_inc(xT_ready, 2)
            pool.sem_inc(y_evac, 2)
            for s in y_stored + out_stored:
                pool.sem_inc(s, 16)
            pool.wait_ge(zeroed, 16 * (ETILES * ROWS // (P * ZR)))
            with pool.Fori(0, BATCH // 2) as i:
                for p in range(2):
                    pool.wait_ge(xf4_loaded[p], 16 * i + 16)
                    pool.wait_ge(pidx_ready, 2 * i + p + 1)
                    pool.sem_inc(pool_turn, 1)
                    for c in range(CHUNKS):
                        for k in range(TOPK):
                            pool.indirect_dma_start(xs_d[:, :], bass.IndirectOffsetOnAxis(ap=pidx[:, p, c, k:k + 1], axis=0), xb2[p][:, c, :], None).then_inc(scattered[p], 16)
            pool.wait_ge(y_stored[0], 16 * (NPAIR + 1) + 16)
            pool.wait_ge(y_stored[1], 16 * NPAIR + 16)
            with pool.Fori(0, BATCH // 2) as i:
                for p in range(2):
                    pool.wait_ge(pidx_ready, BATCH + 2 * i + p + 1)
                    pool.sem_inc(pool_turn, 1)
                    for c in range(CHUNKS):
                        for k in range(TOPK):
                            pool.indirect_dma_start(yg[p][:, c, k, :], None, ys_d[:, :], bass.IndirectOffsetOnAxis(ap=pidx[:, p, c, k:k + 1], axis=0)).then_inc(gathered[p], 16)

        def sp_late(sp):
            def load_xf(b, p):
                sp.dma_start(xb2[p], xf_d[bass.ds(b * CHUNKS, CHUNKS)].rearrange("c p d -> p c d")).then_inc(xf4_loaded[p], 16)

            load_xf(0, 0), load_xf(1, 1)
            with sp.Fori(1, BATCH // 2) as i:
                for p in range(2):
                    sp.wait_ge(scattered[p], 128 * i)
                    sp.sem_inc(sp_turn, 1)
                    load_xf(2 * i + p, p)
            sp.wait_ge(te_ready, 1)
            for p in range(2):
                sp.wait_ge(scattered[p], 128 * (BATCH // 2))

            def expert(j, p, i, first):
                e = sp.value_load(te_i[0:1, bass.ds(j, 1)] if not isinstance(j, int) else te_i[0:1, j:j + 1], min_val=0, max_val=E - 1)
                if not first:
                    sp.wait_ge(xT_filled, j - 1)
                    sp.sem_inc(sp_turn, 1)
                sp.dma_start(xrow[p], xs_d[bass.ds(j * ROWS, ROWS), :].rearrange("(r p) d -> p r d", p=P)).then_inc(xrow_loaded[p], 16)
                if not first:
                    sp.wait_ge(y_filled, j - 1)
                    sp.sem_inc(sp_turn, 1)
                for w in range(2):
                    sp.dma_start(wbuf[p][:, w * KD * F:(w + 1) * KD * F], wts_d[bass.ds(e, 1), :, w * KD * F:(w + 1) * KD * F].rearrange("a p n -> p (a n)")).then_inc(wg_loaded[p], 16)
                sp.dma_start(wbuf[p][:, 2 * KD * F:], wts_d[bass.ds(e, 1), :, 2 * KD * F:].rearrange("a p n -> p (a n)")).then_inc(wd_loaded[p], 16)

            expert(0, 0, 0, True)
            expert(1, 1, 0, True)
            with sp.Fori(1, NPAIR) as i:
                for p in range(2):
                    expert(2 * i + p, p, i, False)
            expert(ETILES - 1, 0, NPAIR, False)
            sp.wait_ge(y_stored[0], 16 * (NPAIR + 1) + 16)
            sp.wait_ge(y_stored[1], 16 * NPAIR + 16)

            def load_x1(b, p, i):
                sp.wait_ge(out_stored[p], 16 * i + 16)
                sp.sem_inc(sp_turn, 1)
                sp.dma_start(xb2[p], x1_d[bass.ds(b * CHUNKS, CHUNKS)].rearrange("c p d -> p c d")).then_inc(x14_loaded[p], 16)

            with sp.Fori(0, BATCH // 2) as i:
                for p in range(2):
                    load_x1(2 * i + p, p, i)
                for p in range(2):
                    sp.wait_ge(mixed, 2 * i + p + 1)
                    sp.sem_inc(sp_turn, 1)
                    sp.dma_start(out_tiles[bass.ds((2 * i + p) * CHUNKS, CHUNKS)].rearrange("c p d -> p c d"), xb2[p]).then_inc(out_stored[p], 16)
            for p in range(2):
                sp.wait_ge(out_stored[p], 16 * (BATCH // 2) + 16)

        block = ctx.enter_context(nc.Block())

        @block.sync
        def _(sp):
            for n, w in enumerate((Wq, Wk, Wv, Wg)):
                sp.dma_start(wqkvg[:, n], w.rearrange("(k p) n -> p k n", p=P)).then_inc(w_loaded, 16)
            sp.dma_start(wo, Wo.rearrange("(h p) n -> p h n", p=P)).then_inc(w_loaded, 16)
            sp.dma_start(wfc, W_fc.rearrange("(k p) n -> p k n", p=P)).then_inc(w_loaded, 16)
            sp.dma_start(wproj, W_proj.rearrange("(f p) n -> p f n", p=P)).then_inc(w_loaded, 16)
            sp.dma_start(wba[:, :, 0:H], Wb.rearrange("(k p) n -> p k n", p=P)).then_inc(small_loaded, 16)
            sp.dma_start(wba[:, :, H:2 * H], Wa.rearrange("(k p) n -> p k n", p=P)).then_inc(small_loaded, 16)
            with nc.allow_non_contiguous_dma(reason="2048 elements, once"):
                for k in range(KD):
                    sp.dma_start(gwT[:, k, :], gate_W[:, k * P:(k + 1) * P].rearrange("e p -> p e")).then_inc(small_loaded, 16)
            sp.dma_start(onorm[:, :], o_norm_w.partition_broadcast(P)).then_inc(small_loaded, 16)
            sp.dma_start(alog[:, :], A_log.partition_broadcast(P)).then_inc(small_loaded, 16)
            sp.dma_start(dtb[:, :], dt_bias.partition_broadcast(P)).then_inc(small_loaded, 16)
            sp.wait_ge(zero_made, 1)
            for n in range(ETILES * ROWS // (P * ZR)):
                sp.dma_start(xs_d[n * P * ZR:(n + 1) * P * ZR, :].rearrange("(p r) d -> p (r d)", p=P), zero).then_inc(zeroed, 16)
            with sp.Fori(0, BATCH) as b:
                sp.wait_ge(pre_xln, b + 1)
                sp.sem_inc(sp_turn, 1)
                sp.dma_start(xln_d[bass.ds(CHUNKS * b, CHUNKS)].rearrange("c p d -> p c d"), xlnb).then_inc(xln_stored, 16)
                sp.wait_ge(pre_hT, 2 * b + 2)
                sp.sem_inc(sp_turn, 1)
                sp.dma_start(hT_d[bass.ds(CHUNKS * b, CHUNKS)].rearrange("c p (k n) -> p c k n", k=KD), hTb).then_inc(hT_stored, 16)
            sp.wait_ge(hT_stored, 16 * BATCH + 16)
            sp.wait_ge(xln_stored, 16 * BATCH + 16)

            def load_hT(f, q):
                sp.dma_start(hT[:, q], hT_d[f].rearrange("p (k n) -> p k n", k=KD)).then_inc(hT_loaded[q], 16)

            def step(t, p, more, e, c):
                if more:
                    sp.wait_ge(front_filled[1], f_filled(t, FU_PROJ + 7))
                    sp.sem_inc(sp_turn, 1)
                    load_hT(t + 2, p)
                sp.wait_ge(back_evac[1], BU // 2 * t + 1)
                sp.sem_inc(sp_turn, 1)
                sp.dma_start(xin[:, 0, :], x_tiles[t]).then_inc(xin_loaded, 16)
                sp.dma_start(xin[:, 1, :], xln_d[t]).then_inc(xin_loaded, 16)
                r0 = c * (F // CHUNKS)
                sp.dma_start(wnat[:, 0].rearrange("p (f d) -> p f d", f=2),
                             W_gate[e][bass.ds(r0, 2 * P)].rearrange("(f p) d -> p f d", p=P)).then_inc(wnat_loaded, 16)
                sp.dma_start(wnat[:, 1].rearrange("p (f d) -> p f d", f=2),
                             W_up[e][bass.ds(r0, 2 * P)].rearrange("(f p) d -> p f d", p=P)).then_inc(wnat_loaded, 16)
                sp.dma_start(wnat[:, 2].rearrange("p (k f) -> p k f", k=KD),
                             W_down[e][:, bass.ds(r0, 2 * P)].rearrange("(k p) f -> p k f", p=P)).then_inc(wnat_loaded, 16)
                sp.wait_ge(back_evac[1], b_evac(t, BU_PREP + 1))
                sp.sem_inc(sp_turn, 1)
                sp.wait_ge(back_evac[0], b_evac(t, BU_PREP + 2))
                sp.sem_inc(sp_turn, 1)
                for n in range(2):
                    sp.dma_start(wts_d[e][:, n * KD * F:(n + 1) * KD * F].rearrange("p (k f) -> p k f", k=KD)[:, :, bass.ds(r0, 2 * P)],
                                 wst[:, n].rearrange("p (k f) -> p k f", k=KD)).then_inc(wst_stored, 16)
                sp.dma_start(wts_d[e][:, bass.ds(2 * KD * F + c * 2 * D, 2 * D)], wst[:, 2]).then_inc(wst_stored, 16)
                sp.wait_ge(x1_ready, t + 1)
                sp.sem_inc(sp_turn, 1)
                sp.dma_start(x1_d[t], x1[:, :]).then_inc(x1_stored, 16)
                sp.wait_ge(xf_ready, t + 1)
                sp.sem_inc(sp_turn, 1)
                sp.dma_start(xf_d[t], xf[:, :]).then_inc(xf_stored, 16)

            load_hT(0, 0)
            load_hT(1, 1)
            with sp.Fori(0, TILES // 2 - 1) as i:
                for p in range(2):
                    t = 2 * i + p
                    step(t, p, True, t // CHUNKS, t % CHUNKS)
            for t in (TILES - 2, TILES - 1):
                step(t, t % 2, False, t // CHUNKS, t % CHUNKS)
            sp.wait_ge(x1_stored, 16 * TILES + 16)
            sp.wait_ge(xf_stored, 16 * TILES + 16)
            sp.wait_ge(wst_stored, 48 * TILES + 48)
            sp_late(sp)

        @block.gpsimd
        def _(pool):
            pool.memset(zero, 0.0).then_inc(zero_made, 1)
            pool.memset(ones[:, :], 1.0).then_inc(consts, 1)
            pool.memset(state[:, :], 0.0).then_inc(consts, 1)
            pool.iota(iota_i[:, 0, :], pattern=[[0, P]], base=0, channel_multiplier=1).then_inc(consts, 1)
            pool.iota(iota_i[:, 1, :], pattern=[[1, P]], base=0, channel_multiplier=0).then_inc(consts, 1)
            pool.iota(tile_iota[:, :], pattern=[[1, ETILES]], base=0, channel_multiplier=0, allow_small_or_imprecise_dtypes=True).then_inc(consts, 1)
            pool.iota(thresholds[:, :], pattern=[[ROWS, MAXT]], base=0, channel_multiplier=0, allow_small_or_imprecise_dtypes=True).then_inc(consts, 1)
            pool.iota(rank_w[:, :], pattern=[[-1, E]], base=E, channel_multiplier=0, allow_small_or_imprecise_dtypes=True).then_inc(consts, 1)
            pool.wait_ge(consts, 7)
            pool.affine_select(out=incl[:, :], in_=ones[:, :], compare_op=ALU.is_ge, fill=0.0, base=0,
                               pattern=[[1, P]], channel_multiplier=-1).then_inc(consts, 1)
            pool.affine_select(out=upper[:, :], in_=ones[:, :], compare_op=ALU.is_gt, fill=0.0, base=0,
                               pattern=[[1, P]], channel_multiplier=-1).then_inc(consts, 1)
            pool.affine_select(out=lower[:, :], in_=ones[:, :], compare_op=ALU.is_gt, fill=0.0, base=0,
                               pattern=[[-1, P]], channel_multiplier=1).then_inc(consts, 1)
            pool.affine_select(out=ident[:, :], in_=ones[:, :], compare_op=ALU.is_equal, fill=0.0, base=0,
                               pattern=[[1, P]], channel_multiplier=-1).then_inc(consts, 1)
            for s in front_evac + back_evac + [xb_free]:
                pool.sem_inc(s, 1)
            for s in (x1_stored, xf_stored, xln_stored, hT_stored):
                pool.sem_inc(s, 16)
            pool.sem_inc(wst_stored, 48)
            with pool.Fori(0, BATCH) as b:
                pool.wait_ge(xb_free, b + 1)
                pool.sem_inc(pool_turn, 1)
                pool.dma_start(xb, x_tiles[bass.ds(CHUNKS * b, CHUNKS)].rearrange("c p d -> p c d")).then_inc(xb_loaded, 16)

            def front_early(f, q, first):
                pool.tensor_copy(sc[:, q, :].unsqueeze(1), dec[:, bass.ds(f, 1), :]).then_inc(sc_ready, 1)
                if not first:
                    pool.wait_ge(front_evac[0], f_evac(f - 1, FU_KKQ + 2))
                    pool.wait_ge(front_evac[1], f_evac(f - 1, FU_KKQ + 3))
                pool.wait_ge(sc_ready, f + 1)
                pool.tensor_tensor(dT[:, :, :], over_heads(incl[:, :], H), per_head(sc[:, q, GLOG:GLOG + H]), ALU.mult).then_inc(rhs_ready, 1)

            def front_mid(f, q):
                pool.wait_ge(kn_ready, f + 1)
                pool.tensor_tensor(kb[:, :].rearrange("p (h d) -> p h d", h=H), k_s[:, :].rearrange("p (h d) -> p h d", h=H),
                                   per_head(sc[:, q, BETA:BETA + H]), ALU.mult).then_inc(kb_ready, 1)
                for n in range(G):
                    pool.wait_ge(front_evac[n], f_evac(f, FU_D + n))
                    d = dT[:, n * HG:(n + 1) * HG, :]
                    pool.tensor_tensor(d, d, over_heads(incl[:, :]), ALU.mult).then_inc(dtm_ready, 1)

            def front_late(f, q):
                r = lambda a: a[:, :].rearrange("p (h d) -> p h d", h=H)
                pool.wait_ge(front_evac[1], f_evac(f, FU_PROJ + 5))
                pool.tensor_tensor(r(vb), r(v_s), per_head(sc[:, q, BETA:BETA + H]), ALU.mult).then_inc(vb_ready, 1)
                pool.tensor_tensor(r(kd), r(k_s), per_head(sc[:, q, DEND:DEND + H]), ALU.mult).then_inc(kd_ready, 1)

            def front_gate(f):
                r = lambda a: a[:, :].rearrange("p (h d) -> p h d", h=H)
                pool.wait_ge(front_evac[1], f_evac(f, FU_PROJ + 7))
                pool.tensor_tensor(r(gw), r(g_s), over_heads(onorm[:, :], H), ALU.mult).then_inc(gw_ready, 1)

            def step(t, p, more):
                if more:
                    front_early(t + 1, 1 - p, False)
                    front_mid(t + 1, 1 - p)
                    pool.wait_ge(back_evac[0], b_evac(t, BU_KDU))
                    pool.wait_ge(back_evac[1], b_evac(t, BU_KDU + 1))
                    front_late(t + 1, 1 - p)
                    pool.wait_ge(og_ready, 2 * t + 2)
                    front_gate(t + 1)

            pool.wait_ge(dec_ready, 1)
            pool.wait_ge(small_loaded, 16 * 7)
            front_early(0, 0, True)
            front_mid(0, 0)
            front_late(0, 0)
            front_gate(0)
            with pool.Fori(0, TILES // 2 - 1) as i:
                for p in range(2):
                    step(2 * i + p, p, True)
            step(TILES - 2, 0, True)
            pool_late(pool)

        @block.scalar
        def _(act):
            A = nc.scalar.activation
            with act.Fori(0, BATCH) as b:
                ch = Chain(act, pre_act, 2 * b)
                act.wait_ge(pre_v, b + 1)
                ch.link(A(pl, pv, ACT.Ln))
                A(pr, pl, ACT.Exp, scale=-0.5).then_inc(pre_r, 1)
                act.wait_ge(pre_xln, b + 1)
                A(psq, k_s[:, :], ACT.Square).then_inc(pre_ss, 1)
                act.wait_ge(pre_v2, b + 1)
                ch.link(A(pl2, pv2, ACT.Ln))
                A(pr2, pl2, ACT.Exp, scale=-0.5).then_inc(pre_r2, 1)
                act.wait_ge(hT_stored, 16 * b + 16)
                for n in range(2):
                    act.wait_ge(pre_tr, 2 * b + n + 1)
                    A(hTb[:, 2 * n:2 * n + 2].rearrange("p c k n -> p (c k n)"), psF[n][:, :], ACT.Copy).then_inc(pre_hT, 1)
                act.wait_ge(pre_ba, b + 1)
                A(ba[:, bass.ds(CHUNKS * b, CHUNKS), :], psB[0][:, 0:CHUNKS * 2 * H].rearrange("p (c n) -> p c n", c=CHUNKS), ACT.Copy).then_inc(ba_ready, 1)
            act_decays(act)

            def silu(f, n, first):
                u = FU_PROJ + n
                if not first and n in (2, 4, 6):
                    act.wait_ge({2: kd_ready, 4: vb_ready, 6: gw_ready}[n], f)
                act.wait_ge(front_filled[u % 2], f_filled(f, u))
                A((q_s, k_s, v_s, g_s)[n // 2][:, n % 2 * GW:(n % 2 + 1) * GW], psF[u % 2][:, :], ACT.Silu).then_inc(front_evac[u % 2], 1)

            def square(f, n):
                if n == 1:
                    act.wait_ge(ss_ready, 2 * f + 1)
                act.wait_ge(front_evac[0], f_evac(f, FU_PROJ + 2 * n))
                act.wait_ge(front_evac[1], f_evac(f, FU_PROJ + 2 * n + 1))
                A(kb[:, :], (q_s, k_s)[n][:, :], ACT.Square).then_inc(sq_ready, 1)

            def norm_root(f):
                act.wait_ge(nv_ready, f + 1)
                Chain(act, front_act, NFA * f).link(A(nl[:, :], nv[:, :], ACT.Ln))
                A(nr[:, :], nl[:, :], ACT.Exp, scale=-0.5).then_inc(nr_ready, 1)

            def decay_exp(f):
                for n in range(G):
                    u = FU_D + n
                    act.wait_ge(front_filled[u % 2], f_filled(f, u))
                    A(dT[:, n * HG:(n + 1) * HG, :].rearrange("p h n -> p (h n)"), psF[u % 2][:, :], ACT.Exp).then_inc(front_evac[u % 2], 1)

            def copy_T(f, u0, dst):
                for n in range(G):
                    u = u0 + n
                    act.wait_ge(front_filled[u % 2], f_filled(f, u))
                    A(dst[:, n * HG:(n + 1) * HG, :], psF[u % 2][:, :].rearrange("p (h n) -> p h n", h=HG), ACT.Copy).then_inc(front_evac[u % 2], 1)

            def copy_x(t):
                for g in range(G):
                    act.wait_ge(inv_filled[0][g], 12 * t + 1)
                    A(xi[:, g * GW:(g + 1) * GW], psI[0][g][:, :], ACT.Copy).then_inc(x_ready[g], 1)

            def copy_y(t, l):
                for g in range(G):
                    act.wait_ge(inv_filled[0][g], 12 * t + 2 * l + 1)
                    A(yi[:, g * GW:(g + 1) * GW], psI[0][g][:, :], ACT.Copy).then_inc(y_ready[g], 1)

            def evac(t, u, dst, func=ACT.Copy):
                act.wait_ge(back_filled[u % 2], b_filled(t, u))
                A(dst, psB[u % 2][:, 0:dst.shape[1]], func).then_inc(back_evac[u % 2], 1)

            def root(ready, t, src, dst, done, ch, n):
                act.wait_ge(ready, t + 1)
                ch.link(A(tl[:, 0:n], src, ACT.Ln))
                A(dst, tl[:, 0:n], ACT.Exp, scale=-0.5).then_inc(done, 1)

            def back(t, p):
                act.wait_ge(sc_ready, t + 1)
                for g in range(G):
                    u = BU_QS + g
                    act.wait_ge(back_filled[u % 2], b_filled(t, u))
                    for h in range(HG):
                        c = g * HG + h
                        last = A(qsg[:, c * DK:(c + 1) * DK], psB[u % 2][:, h * DK:(h + 1) * DK], ACT.Copy, scale=sc[:, p, GAM + c:GAM + c + 1])
                    last.then_inc(back_evac[u % 2], 1)
                for g in range(G):
                    evac(t, BU_U + g, u_s[:, g * GW:(g + 1) * GW])
                act.wait_ge(wst_stored, 48 * t + 48)
                for n in range(3):
                    evac(t, BU_PREP + n, wst[:, n])
                ch = Chain(act, tail_act, NTA * t)
                act.wait_ge(back_evac[0], b_evac(t, BU_PU))
                act.wait_ge(back_evac[1], b_evac(t, BU_PU + 1))
                A(r_s[:, :], o_s[:, :], ACT.Square).then_inc(so_ready, 1)
                root(ov_ready, t, tv[:, :], tr[:, :], or_ready, ch, H)
                for g in range(G):
                    evac(t, BU_OT + g, oT[:, g * GW:(g + 1) * GW])
                act.wait_ge(back_evac[1], b_evac(t, BU_WO))
                A(junk[:, :], x2[:, :], ACT.Square, accum_out=ts[:, 0:1]).then_inc(sm_ready, 1)
                root(mv_ready, t, tv[:, 0:1], tr[:, 0:1], mr_ready, ch, 1)
                evac(t, BU_MT, mT[:, :])
                for n in range(2):
                    evac(t, BU_FC + n, hid[:, n * GW:(n + 1) * GW], ACT.Relu)
                root(fv_ready, t, tv[:, 0:1], tr[:, 0:1], frr_ready, ch, 1)
                evac(t, BU_XT, xfT[:, :])

            def step(t, p, more):
                f, q = t + 1, 1 - p
                copy_x(t)
                if more:
                    silu(f, 0, False), silu(f, 1, False)
                for l in range(1, LEVELS - 1):
                    if more and l <= 3:
                        silu(f, 2 * l, False), silu(f, 2 * l + 1, False)
                    if more and l <= 2:
                        square(f, l - 1)
                    if more and l == 4:
                        norm_root(f)
                        decay_exp(f)
                        copy_T(f, FU_K, kT)
                    if more and l == 5:
                        copy_T(f, FU_KB, kbqT[:, q, :, 0, :])
                        copy_T(f, FU_Q, kbqT[:, q, :, 1, :])
                    copy_y(t, l)
                back(t, p)

            act.wait_ge(w_loaded, 16 * 7)
            for n in range(8):
                silu(0, n, True)
            square(0, 0), square(0, 1)
            norm_root(0)
            decay_exp(0)
            copy_T(0, FU_K, kT)
            copy_T(0, FU_KB, kbqT[:, 0, :, 0, :])
            copy_T(0, FU_Q, kbqT[:, 0, :, 1, :])
            with act.Fori(0, TILES // 2 - 1) as i:
                for p in range(2):
                    step(2 * i + p, p, True)
            step(TILES - 2, 0, True)
            step(TILES - 1, 1, False)
            act_late(act)

        @block.vector
        def _(dve):
            V = nc.vector
            ch = Chain(dve, const_dve)
            dve.wait_ge(consts, 11)
            ch.link(V.tensor_tensor(iota_i[:, 0, :], iota_i[:, 0, :], iota_i[:, 1, :], ALU.bitwise_xor))
            ch.link(V.tensor_copy(xor[:, :], iota_i[:, 0, :]))
            for l in range(LEVELS):
                ins = V.scalar_tensor_tensor(level_mask[:, l, :], xor[:, :], float(1 << l), lower[:, :], ALU.is_ge, ALU.mult)
            ch.link(ins)
            for l in range(LEVELS - 1):
                ins = V.tensor_tensor(level_mask[:, l, :], level_mask[:, l, :], level_mask[:, l + 1, :], ALU.subtract)
            ch.link(ins)
            ch.link(V.scalar_tensor_tensor(neg_m0t[:, :], xor[:, :], 1.0, upper[:, :], ALU.is_equal, ALU.mult))
            ch.link(V.tensor_scalar(neg_m0t[:, :], neg_m0t[:, :], -1.0, None, ALU.mult))

            def refine(ch, r, v, a, dst):
                ch.link(V.scalar_tensor_tensor(a, r, -0.5, r, ALU.mult, ALU.mult))
                ch.link(V.tensor_tensor(a, a, v, ALU.mult))
                return V.scalar_tensor_tensor(dst, a, 1.5, r, ALU.add, ALU.mult)

            with dve.Fori(0, BATCH) as b:
                ch = Chain(dve, pre_dve, 9 * b)
                dve.wait_ge(xb_loaded, 16 * b + 16)
                for c in range(CHUNKS):
                    ins = V.bn_stats(pbst[:, c, :], xb[:, c, :])
                ch.link(ins)
                dve.sem_inc(dve_turn, 1)
                for c in range(CHUNKS):
                    ins = V.bn_aggr(pmv[:, c, :], pbst[:, c, :])
                ch.link(ins)
                V.tensor_scalar(pv, pmv[:, :, 1], LN_EPS, None, ALU.add).then_inc(pre_v, 1)
                dve.wait_ge(pre_r, b + 1)
                ch.link(refine(ch, pr, pv, pa, prr))
                dve.wait_ge(xln_stored, 16 * b + 16)
                for c in range(CHUNKS):
                    ins = V.tensor_scalar(xlnb[:, c, :], xb[:, c, :], pmv[:, c, 0:1], prr[:, c:c + 1], ALU.subtract, ALU.mult)
                ins.then_inc(pre_xln, 1)
                dve.wait_ge(pre_xln, b + 1)
                dve.sem_inc(xb_free, 1)
                dve.wait_ge(pre_ss, b + 1)
                ch.link(V.tensor_reduce(pss, psq.rearrange("p (c d) -> p c d", c=CHUNKS), X, ALU.add))
                V.tensor_scalar(pv2, pss, 1.0 / D, RMS_EPS, ALU.mult, ALU.add).then_inc(pre_v2, 1)
                dve.wait_ge(pre_r2, b + 1)
                ch.link(refine(ch, pr2, pv2, pa2, prr2))
                for c in range(CHUNKS):
                    ins = V.tensor_scalar(hb[:, c, :], xlnb[:, c, :], prr2[:, c:c + 1], None, ALU.mult)
                ins.then_inc(pre_h, 1)
            dve_decays(dve)

            H3 = lambda a: a[:, :].rearrange("p (h d) -> p h d", h=H)

            def norm_sum(f, n):
                dve.wait_ge(sq_ready, 2 * f + n + 1)
                V.tensor_reduce(ss[:, n * H:(n + 1) * H], H3(kb), X, ALU.add).then_inc(ss_ready, 1)

            def norm_var(f):
                dve.wait_ge(ss_ready, 2 * f + 2)
                V.tensor_scalar(nv[:, :], ss[:, :], RMS_EPS, None, ALU.add).then_inc(nv_ready, 1)

            def norms(f):
                ch = Chain(dve, front_dve, NFD * f)
                dve.wait_ge(nr_ready, f + 1)
                ch.link(refine(ch, nr[:, :], nv[:, :], na[:, :], rn[:, :]))
                V.tensor_tensor(H3(k_s), H3(k_s), per_head(rn[:, H:2 * H]), ALU.mult).then_inc(kn_ready, 1)
                V.scalar_tensor_tensor(H3(q_s), H3(q_s), DK ** -0.5, per_head(rn[:, 0:H]), ALU.mult, ALU.mult).then_inc(qn_ready, 1)

            def delta_products(f, q, n):
                u = FU_KKQ + n
                if n % 2 == 0:
                    dve.wait_ge(dtm_ready, 2 * f + n // 2 + 1)
                dve.wait_ge(front_filled[u % 2], f_filled(f, u))
                d = dT[:, 2 * n:2 * n + 2, :].unsqueeze(2).to_broadcast([P, 2, 2, P])
                V.tensor_tensor(aP[:, q, 2 * n:2 * n + 2], psF[u % 2][:, :].rearrange("p (h a n) -> p h a n", h=2, a=2), d, ALU.mult).then_inc(front_evac[u % 2], 1)

            GV = lambda a, g: a[:, g * GW:(g + 1) * GW].rearrange("p (h n) -> p h n", h=HG)

            def inverse_start(t, p):
                dve.wait_ge(front_evac[0], f_evac(t, FU_KKQ + 2))
                dve.wait_ge(front_evac[1], f_evac(t, FU_KKQ + 3))
                for g in range(G):
                    ins = V.tensor_tensor(GV(yi, g), aP[:, p, g * HG:(g + 1) * HG, 0, :], over_heads(neg_m0t[:, :]), ALU.mult)
                Chain(dve, y0_dve, t).link(ins)
                for g in range(G):
                    V.tensor_tensor(GV(yi, g), GV(yi, g), over_heads(ident[:, :]), ALU.add).then_inc(y_ready[g], 1)

            def level_t(t, l):
                for g in range(G):
                    dve.wait_ge(inv_filled[0][g], 12 * t + 2 * l)
                    V.tensor_tensor(GV(ti, g), psI[0][g][:, :].rearrange("p (h n) -> p h n", h=HG), over_heads(level_mask[:, l, :]), ALU.mult).then_inc(t_ready[g], 1)

            def level_x(t, l):
                a, ready = (xi, x_ready) if l < LEVELS - 1 else (yi, y_ready)
                for g in range(G):
                    dve.wait_ge(inv_filled[1][g], 6 * t + l)
                    V.tensor_tensor(a[:, g * GW:(g + 1) * GW], a[:, g * GW:(g + 1) * GW], psI[1][g][:, :], ALU.subtract).then_inc(ready[g], 1)

            def back(t, p):
                dve.wait_ge(vb_ready, t + 1)
                for g in range(G):
                    u = BU_KBS + g
                    dve.wait_ge(back_filled[u % 2], b_filled(t, u))
                    for h in range(HG):
                        c = g * HG + h
                        s = slice(c * DK, (c + 1) * DK)
                        ins = V.scalar_tensor_tensor(r_s[:, s], psB[u % 2][:, h * DK:(h + 1) * DK], sc[:, p, NGAM + c:NGAM + c + 1], vb[:, s], ALU.mult, ALU.add)
                    ins.then_inc(back_evac[u % 2], 1)
                for g in range(G):
                    u = BU_PU + g
                    dve.wait_ge(back_evac[(BU_QS + g) % 2], b_evac(t, BU_QS + g))
                    dve.wait_ge(back_filled[u % 2], b_filled(t, u))
                    s = slice(g * GW, (g + 1) * GW)
                    V.tensor_tensor(o_s[:, s], qsg[:, s], psB[u % 2][:, :], ALU.add).then_inc(back_evac[u % 2], 1)
                for g in range(G):
                    u = BU_KDU + g
                    dve.wait_ge(back_filled[u % 2], b_filled(t, u))
                    for h in range(HG):
                        c = g * HG + h
                        s = slice(c * DK, (c + 1) * DK)
                        ins = V.scalar_tensor_tensor(state[:, s], state[:, s], sc[:, p, GTOT + c:GTOT + c + 1], psB[u % 2][:, h * DK:(h + 1) * DK], ALU.mult, ALU.add)
                    ins.then_inc(back_evac[u % 2], 1)
                ch = Chain(dve, tail_dve, NTD * t)
                dve.wait_ge(so_ready, t + 1)
                ch.link(V.tensor_reduce(ts[:, :], H3(r_s), X, ALU.add))
                V.tensor_scalar(tv[:, :], ts[:, :], 1.0 / DK, RMS_EPS, ALU.mult, ALU.add).then_inc(ov_ready, 1)
                dve.wait_ge(or_ready, t + 1)
                ch.link(refine(ch, tr[:, :], tv[:, :], ta[:, :], to[:, :]))
                V.tensor_tensor(H3(o_s), H3(o_s), per_head(to[:, :]), ALU.mult).then_inc(og_ready, 1)

            def tail(t):
                ch = Chain(dve, tail_dve, NTD * t)
                ch.n = 4
                dve.wait_ge(xin_loaded, 32 * t + 32)
                dve.wait_ge(back_filled[1], b_filled(t, BU_WO))
                V.tensor_tensor(x2[:, :], xin[:, 1, :], psB[1][:, 0:D], ALU.add).then_inc(back_evac[1], 1)
                dve.wait_ge(sm_ready, t + 1)
                V.tensor_scalar(tv[:, 0:1], ts[:, 0:1], 1.0 / D, RMS_EPS, ALU.mult, ALU.add).then_inc(mv_ready, 1)
                dve.wait_ge(mr_ready, t + 1)
                ch.link(refine(ch, tr[:, 0:1], tv[:, 0:1], ta[:, 0:1], to[:, 0:1]))
                V.tensor_scalar(m_s[:, :], x2[:, :], to[:, 0:1], None, ALU.mult).then_inc(m_ready, 1)
                for n in range(2):
                    u = BU_FC + n
                    dve.wait_ge(back_evac[u % 2], b_evac(t, u))
                    V.tensor_tensor(hid[:, n * GW:(n + 1) * GW], hid[:, n * GW:(n + 1) * GW], hid[:, n * GW:(n + 1) * GW], ALU.mult).then_inc(hid_ready, 1)
                dve.wait_ge(x1_stored, 16 * t + 16)
                dve.wait_ge(back_filled[1], b_filled(t, BU_PROJ))
                V.tensor_tensor(x1[:, :], x2[:, :], psB[1][:, 0:D], ALU.add).then_inc(back_evac[1], 1)
                dve.wait_ge(back_evac[1], b_evac(t, BU_PROJ))
                V.tensor_tensor(x1[:, :], x1[:, :], xin[:, 0, :], ALU.add).then_inc(x1_ready, 1)
                dve.wait_ge(x1_ready, t + 1)
                ch.link(V.bn_stats(bst[:, :], x1[:, :]))
                dve.sem_inc(dve_turn, 1)
                ch.link(V.bn_aggr(bag[:, :], bst[:, :]))
                V.tensor_scalar(tv[:, 0:1], bag[:, 1:2], LN_EPS, None, ALU.add).then_inc(fv_ready, 1)
                dve.wait_ge(frr_ready, t + 1)
                ch.link(refine(ch, tr[:, 0:1], tv[:, 0:1], ta[:, 0:1], to[:, 0:1]))
                dve.wait_ge(xf_stored, 16 * t + 16)
                V.tensor_scalar(xf[:, :], x1[:, :], bag[:, 0:1], to[:, 0:1], ALU.subtract, ALU.mult).then_inc(xf_ready, 1)
                dve.wait_ge(back_filled[1], b_filled(t, BU_LG))
                V.tensor_scalar(la[:, bass.ds(t, 1), :], psB[1][:, 0:E].unsqueeze(1), -1.0 / EPSILON, None, ALU.mult).then_inc(back_evac[1], 1)

            def gated(t):
                dve.wait_ge(gw_ready, t + 1)
                dve.wait_ge(og_ready, 2 * t + 1)
                V.tensor_tensor(o_s[:, :], o_s[:, :], gw[:, :], ALU.mult).then_inc(og_ready, 1)

            def step(t, p, more):
                f, q = t + 1, 1 - p
                inverse_start(t, p)
                for l in range(1, LEVELS):
                    level_t(t, l)
                    if more and l == 2:
                        norm_sum(f, 0)
                    if more and l == 3:
                        norm_sum(f, 1)
                        norm_var(f)
                    if more and l == 4:
                        norms(f)
                    if more and l == 6:
                        delta_products(f, q, 0), delta_products(f, q, 1)
                    level_x(t, l)
                if more:
                    delta_products(f, q, 2), delta_products(f, q, 3)
                back(t, p)
                gated(t)
                tail(t)

            norm_sum(0, 0), norm_sum(0, 1)
            norm_var(0)
            norms(0)
            for n in range(4):
                delta_products(0, 0, n)
            with dve.Fori(0, TILES // 2 - 1) as i:
                for p in range(2):
                    step(2 * i + p, p, True)
            step(TILES - 2, 0, True)
            step(TILES - 1, 1, False)
            dve_late(dve)

        @block.tensor
        def _(pe):
            MM = nc.tensor.matmul
            pe.wait_ge(const_dve, 6)
            pe.wait_ge(small_loaded, 16 * 7)
            with pe.Fori(0, BATCH) as b:
                pe.wait_ge(pre_h, b + 1)
                for n in range(2):
                    for c in range(2):
                        for k in range(KD):
                            j = (c * KD + k) * P
                            last = nc.tensor.transpose(psF[n][:, j:j + P], hb[:, 2 * n + c, k * P:(k + 1) * P], ident[:, :])
                    last.then_inc(pre_tr, 1)
                pe.wait_ge(pre_hT, 2 * b + 2)
                for c in range(CHUNKS):
                    for k in range(KD):
                        last = MM(psB[0][:, c * 2 * H:(c + 1) * 2 * H], hTb[:, c, k, :], wba[:, k, :], start=k == 0, stop=k == KD - 1)
                last.then_inc(pre_ba, 1)
                pe.wait_ge(ba_ready, b + 1)
            pe_decays(pe)

            def front_bank(f, u):
                pe.wait_ge(front_evac[u % 2], f_evac(f, u) - 1)
                return psF[u % 2], front_filled[u % 2]

            def back_bank(t, u):
                pe.wait_ge(back_evac[u % 2], b_evac(t, u) - 1)
                return psB[u % 2], back_filled[u % 2]

            def project(f, q, n):
                ps, filled = front_bank(f, FU_PROJ + n)
                for k in range(KD):
                    last = MM(ps[:, :], hT[:, q, k, :], wqkvg[:, n // 2, k, n % 2 * GW:(n % 2 + 1) * GW], start=k == 0, stop=k == KD - 1)
                last.then_inc(filled, 1)

            def decay_sums(f, n):
                ps, filled = front_bank(f, FU_D + n)
                MM(ps[:, :], lower[:, :], dT[:, n * HG:(n + 1) * HG, :].rearrange("p h n -> p (h n)"), start=True, stop=True).then_inc(filled, 1)

            def transposes(f, u0, src):
                for n in range(G):
                    ps, filled = front_bank(f, u0 + n)
                    for h in range(HG):
                        c = n * HG + h
                        last = nc.tensor.transpose(ps[:, h * P:(h + 1) * P], src[:, c * DK:(c + 1) * DK], ident[:, :])
                    last.then_inc(filled, 1)

            def delta_products(f, q, n):
                ps, filled = front_bank(f, FU_KKQ + n)
                for h in range(2):
                    c = 2 * n + h
                    last = MM(ps[:, h * 2 * P:(h + 1) * 2 * P], kT[:, c, :], kbqT[:, q, c].rearrange("p a n -> p (a n)"), start=True, stop=True)
                last.then_inc(filled, 1)

            cols = lambda a, c: a[:, c * DK:(c + 1) * DK]

            def start_x(t):
                for g in range(G):
                    pe.wait_ge(y_ready[g], 7 * t + 1)
                    for h in range(HG):
                        last = nc.tensor.transpose(psI[0][g][:, h * P:(h + 1) * P], cols(yi, g * HG + h), ident[:, :])
                    last.then_inc(inv_filled[0][g], 1)

            def level_t(t, p, l):
                for g in range(G):
                    pe.wait_ge(x_ready[g], 6 * t + l)
                    pe.wait_ge(y_ready[g], 7 * t + l)
                    for h in range(HG):
                        last = MM(psI[0][g][:, h * P:(h + 1) * P], aP[:, p, g * HG + h, 0, :], cols(xi, g * HG + h), start=True, stop=True)
                    last.then_inc(inv_filled[0][g], 1)

            def level_x(t, l):
                for g in range(G):
                    pe.wait_ge(t_ready[g], 6 * t + l)
                    for h in range(HG):
                        c = g * HG + h
                        a, b = (yi, ti) if l < LEVELS - 1 else (ti, yi)
                        last = MM(psI[1][g][:, h * P:(h + 1) * P], cols(a, c), cols(b, c), start=True, stop=True)
                    last.then_inc(inv_filled[1][g], 1)

            def level_y(t, l):
                for g in range(G):
                    pe.wait_ge(x_ready[g], 6 * t + l + 1)
                    for h in range(HG):
                        last = nc.tensor.transpose(psI[0][g][:, h * P:(h + 1) * P], cols(xi, g * HG + h), ident[:, :])
                    last.then_inc(inv_filled[0][g], 1)

            def heads(t, u, g, left, right):
                ps, filled = back_bank(t, u)
                for h in range(HG):
                    last = MM(ps[:, h * DK:(h + 1) * DK], left(g * HG + h), right(g * HG + h), start=True, stop=True)
                last.then_inc(filled, 1)

            def back(t, p):
                for g in range(G):
                    heads(t, BU_KBS + g, g, lambda c: kbqT[:, p, c, 0, :], lambda c: cols(state, c))
                for g in range(G):
                    heads(t, BU_QS + g, g, lambda c: kbqT[:, p, c, 1, :], lambda c: cols(state, c))
                for g in range(G):
                    pe.wait_ge(y_ready[g], 7 * t + 7)
                    heads(t, BU_U + g, g, lambda c: cols(yi, c), lambda c: cols(r_s, c))
                for g in range(G):
                    heads(t, BU_PU + g, g, lambda c: aP[:, p, c, 1, :], lambda c: cols(u_s, c))
                pe.wait_ge(kd_ready, t + 1)
                for g in range(G):
                    heads(t, BU_KDU + g, g, lambda c: cols(kd, c), lambda c: cols(u_s, c))
                pe.wait_ge(wnat_loaded, 48 * t + 48)
                for n in range(3):
                    ps, filled = back_bank(t, BU_PREP + n)
                    for a in range(2):
                        for b in range(2):
                            j = (b * 2 + a) * P
                            last = nc.tensor.transpose(ps[:, j:j + P], wnat[:, n, a * D + b * P:a * D + (b + 1) * P], ident[:, :])
                    last.then_inc(filled, 1)
                pe.wait_ge(og_ready, 2 * t + 2)
                for g in range(G):
                    ps, filled = back_bank(t, BU_OT + g)
                    for h in range(HG):
                        last = nc.tensor.transpose(ps[:, h * P:(h + 1) * P], cols(o_s, g * HG + h), ident[:, :])
                    last.then_inc(filled, 1)
                ps, filled = back_bank(t, BU_WO)
                for h in range(H):
                    if h == HG:
                        pe.wait_ge(back_evac[(BU_OT + 1) % 2], b_evac(t, BU_OT + 1))
                    last = MM(ps[:, 0:D], cols(oT, h), wo[:, h, :], start=h == 0, stop=h == H - 1)
                last.then_inc(filled, 1)
                pe.wait_ge(m_ready, t + 1)
                ps, filled = back_bank(t, BU_MT)
                for k in range(KD):
                    last = nc.tensor.transpose(ps[:, k * P:(k + 1) * P], m_s[:, k * P:(k + 1) * P], ident[:, :])
                last.then_inc(filled, 1)
                pe.wait_ge(back_evac[BU_MT % 2], b_evac(t, BU_MT))
                for n in range(2):
                    ps, filled = back_bank(t, BU_FC + n)
                    for fb in range(FB // 2):
                        for k in range(KD):
                            c = (n * (FB // 2) + fb) * P
                            last = MM(ps[:, fb * P:(fb + 1) * P], wfc[:, k, c:c + P], mT[:, k * P:(k + 1) * P], start=k == 0, stop=k == KD - 1)
                    last.then_inc(filled, 1)
                ps, filled = back_bank(t, BU_PROJ)
                for fb in range(FB):
                    if fb % (FB // 2) == 0:
                        pe.wait_ge(hid_ready, 2 * t + fb // (FB // 2) + 1)
                    last = MM(ps[:, 0:D], hid[:, fb * P:(fb + 1) * P], wproj[:, fb, :], start=fb == 0, stop=fb == FB - 1)
                last.then_inc(filled, 1)
                pe.wait_ge(xf_ready, t + 1)
                ps, filled = back_bank(t, BU_XT)
                for k in range(KD):
                    last = nc.tensor.transpose(ps[:, k * P:(k + 1) * P], xf[:, k * P:(k + 1) * P], ident[:, :])
                last.then_inc(filled, 1)
                pe.wait_ge(back_evac[BU_XT % 2], b_evac(t, BU_XT))
                ps, filled = back_bank(t, BU_LG)
                for k in range(KD):
                    last = MM(ps[:, 0:E], xfT[:, k * P:(k + 1) * P], gwT[:, k, :], start=k == 0, stop=k == KD - 1)
                last.then_inc(filled, 1)

            def front_k(f):
                pe.wait_ge(kn_ready, f + 1)
                transposes(f, FU_K, k_s)

            def front_kb(f):
                pe.wait_ge(kb_ready, f + 1)
                transposes(f, FU_KB, kb)

            def front_q(f):
                pe.wait_ge(qn_ready, f + 1)
                transposes(f, FU_Q, q_s)

            def step(t, p, more, turn):
                f, q = t + 1, 1 - p
                start_x(t)
                if more:
                    pe.wait_ge(hT_loaded[q], 16 * turn + 16)
                    project(f, q, 0), project(f, q, 1)
                for l in range(1, LEVELS):
                    level_t(t, p, l)
                    if more and l <= 3:
                        project(f, q, 2 * l)
                    if more and l == 4:
                        pe.wait_ge(rhs_ready, f + 1)
                        decay_sums(f, 0), decay_sums(f, 1)
                    if more and l == 5:
                        front_kb(f)
                    if more and l == 6:
                        delta_products(f, q, 0), delta_products(f, q, 1)
                    level_x(t, l)
                    if more and l <= 3:
                        project(f, q, 2 * l + 1)
                    if more and l == 4:
                        front_k(f)
                    if more and l == 5:
                        front_q(f)
                    if l < LEVELS - 1:
                        level_y(t, l)
                if more:
                    delta_products(f, q, 2), delta_products(f, q, 3)
                back(t, p)

            pe.wait_ge(w_loaded, 16 * 7)
            pe.wait_ge(hT_loaded[0], 16)
            for n in range(8):
                project(0, 0, n)
            pe.wait_ge(rhs_ready, 1)
            decay_sums(0, 0), decay_sums(0, 1)
            front_k(0)
            front_kb(0)
            front_q(0)
            for n in range(4):
                delta_products(0, 0, n)
            with pe.Fori(0, TILES // 2 - 1) as i:
                for p in range(2):
                    step(2 * i + p, p, True, i + p)
            step(TILES - 2, 0, True, TILES // 2 - 1)
            step(TILES - 1, 1, False, 0)
            pe_late(pe)


_INS = ["L0_attn_x", "L0_attn_Wq", "L0_attn_Wk", "L0_attn_Wv", "L0_attn_Wb", "L0_attn_Wa", "L0_attn_A_log",
        "L0_attn_dt_bias", "L0_attn_Wg", "L0_attn_o_norm_w", "L0_attn_Wo", "L0_attn_W_fc", "L0_attn_W_proj",
        "L0_ffn_gate_W", "L0_ffn_W_gate", "L0_ffn_W_up", "L0_ffn_W_down"]


def kernel(**inputs):
    import concourse.bacc as _bacc
    from concourse.bass_utils import run_bass_kernel_spmd as _run

    nc = _bacc.Bacc("TRN2", target_bir_lowering=False, num_devices=1)
    arrays, args = {}, []
    for name in _INS:
        a = np.ascontiguousarray(inputs[name])
        arrays[f"{name}_dram"] = a
        args.append(nc.dram_tensor(f"{name}_dram", a.shape, mybir.dt.from_np(a.dtype), kind="ExternalInput").ap())
    o = nc.dram_tensor("out_dram", (BATCH, SEQ, D), F32, kind="ExternalOutput").ap()
    program(nc, *args, o)
    r = _run(nc, [arrays], core_ids=[0])
    return r.results[0]["out_dram"]
```

```python
from contextlib import ExitStack

import numpy as np
import concourse.bass as bass
from concourse import mybir

F32 = mybir.dt.float32
F32R = mybir.dt.float32r
I32 = mybir.dt.int32
ALU = mybir.AluOpType
ACT = mybir.ActivationFunctionType
X = mybir.AxisListType.X

P = 128
BATCH, SEQ, D = 8, 512, 256
H, DK, F = 8, 128, 1024
E, TOPK, ROUNDS, EPSILON = 8, 2, 20, 0.05
KD = D // P
CHUNKS = SEQ // P
TILES = BATCH * CHUNKS
PAIRS = TILES // 2 - 1
TOKENS = BATCH * SEQ
HD = H * DK
G = 2
HG = H // G
GW = HG * DK
LEVELS = 7
FB = F // P
WCOLS = 3 * KD * F
ROWS = 256
RB = ROWS // P
ETILES = (TOKENS * TOPK + E * (ROWS - 1)) // ROWS
MAXT = TOKENS // ROWS
XPARTS = 4
LN_EPS, RMS_EPS = 1e-5, 1e-6
DEAD = 110.0
EXP_ZERO = -87.33654
ROOT_MAGIC = 1597463007.0

BETA, GAM, NGAM, GTOT, DEND, GLOG, MEAN = (8 * n for n in range(7))
RINV = MEAN + 1
NSC = MEAN + 2

FU_PROJ, FU_D, FU_K, FU_KB, FU_Q, FU_KKQ, FU = 0, 8, 10, 12, 14, 16, 20
(BU_OT, BU_WO, BU_MT, BU_FC, BU_KBS, BU_PROJ, BU_U, BU_QS, BU_PU, BU_KDU, BU_XT, BU_LG, BU_PREP, BU) = (
    0, 2, 3, 4, 6, 8, 9, 11, 13, 15, 17, 18, 19, 22)
TAIL_USES = (0, 1, 2, 3, 4, 5, 8, 17, 18)
STATE_USES = tuple(u for u in range(BU) if u not in TAIL_USES)


class Chain:

    def __init__(self, eng, sem, base=0):
        self.eng, self.sem, self.base, self.n = eng, sem, base, 0

    def link(self, ins):
        self.n += 1
        ins.then_inc(self.sem, 1)
        self.eng.wait_ge(self.sem, self.base + self.n)


def over_heads(m, n=HG):
    return m.unsqueeze(1).to_broadcast([m.shape[0], n, m.shape[1]])


def left(a, l, halves=2):
    w = 1 << l
    return a.rearrange("p (b s) -> p b s", s=halves * w)[:, :, 0:w]


def per_head(s, k=DK):
    return s.unsqueeze(2).to_broadcast([s.shape[0], s.shape[1], k])


def program(nc, x, Wq, Wk, Wv, Wb, Wa, A_log, dt_bias, Wg, o_norm_w, Wo, W_fc, W_proj,
            gate_W, W_gate, W_up, W_down, out):
    x_tiles = x.rearrange("b (c p) d -> (b c) p d", p=P)
    out_tiles = out.rearrange("b (c p) d -> (b c) p d", p=P)
    hT_d = nc.dram_tensor("hT_d", [TILES, P, D], F32)
    x1_d = nc.dram_tensor("x1_d", [TILES, P, D], F32)
    xf_d = nc.dram_tensor("xf_d", [TILES, P, D], F32)
    wts_d = nc.dram_tensor("wts_d", [E, P, WCOLS], F32)
    xs_d = nc.dram_tensor("xs_d", [ETILES * ROWS, D], F32)
    ys_d = nc.dram_tensor("ys_d", [ETILES * ROWS, D], F32)

    with ExitStack() as ctx:
        def sb(name, shape, dt=F32):
            return ctx.enter_context(nc.sbuf_tensor(name, shape, dt))

        def sem(name):
            return ctx.enter_context(nc.semaphore(name))

        ident = sb("ident", [P, P])
        ones = sb("ones", [P, P])
        incl = sb("incl", [P, P])
        upper = sb("upper", [P, P])
        lower = sb("lower", [P, P])
        xor = sb("xor", [P, P])
        iota_i = sb("iota_i", [P, 2, P], I32)
        level_mask = sb("level_mask", [P, LEVELS, P // 2])
        neg_m0t = sb("neg_m0t", [P, P])
        tile_iota = sb("tile_iota", [1, ETILES])
        thresholds = sb("thresholds", [P, MAXT])
        rank_w = sb("rank_w", [P, E])
        wba = sb("wba", [P, KD, 2 * H])
        gwT = sb("gwT", [P, KD, E])
        onorm = sb("onorm", [P, DK])
        alog = sb("alog", [P, H])
        dtb = sb("dtb", [P, H])
        ba = sb("ba", [P, TILES, 2 * H])
        dec = sb("dec", [P, TILES, NSC])
        la = sb("la", [P, TILES, E])
        sc = sb("sc", [P, 2, NSC])
        msc = sb("msc", [P, 2])
        ss = sb("ss", [P, 2 * H])
        nv = sb("nv", [P, 2 * H])
        na = sb("na", [P, 2 * H])
        rn = sb("rn", [P, 2 * H])
        bst = sb("bst", [P, 6])
        bag = sb("bag", [P, 2])
        xrow_v = sb("xrow_v", [P, 2])
        xrow_r = sb("xrow_r", [P, 2])
        mrow_v = sb("mrow_v", [P, 2])
        mrow_r = sb("mrow_r", [P, 2])
        os_ = sb("os", [P, 2, H])
        or_ = sb("or", [P, 2, H])

        pi_t = sb("pi_t", [P, TILES * E])
        posi = sb("posi", [P, TILES, TOPK], I32)
        te_i = sb("te_i", [1, ETILES], I32)
        pidx = sb("pidx", [P, 2, CHUNKS, TOPK], I32)
        pw = sb("pw", [P, 2, CHUNKS, TOPK])
        with nc.sbuf_tensor("x_all", [P, TILES, D], F32) as x_all:
            pass
        attention = ExitStack()

        def at(name, shape):
            return attention.enter_context(nc.sbuf_tensor(name, shape, F32))

        kbqT = at("kbqT", [P, 2, H, 2, P])
        aP = at("aP", [P, 2, H, 2, P])
        weights = at("weights", [P, 7 * KD * HD])
        kT = at("kT", [P, H, P])
        dT = at("dT", [P, H, P])
        kd, vb, kb, v_s, g_s = (at(n, [P, HD]) for n in ("kd", "vb", "kb", "v_s", "g_s"))
        hT = at("hT", [P, 2, KD, P])
        xin = at("xin", [P, 2, D])
        x2, m_s, mT, x1, xf, xfT = (at(n, [P, D]) for n in ("x2", "m_s", "mT", "x1", "xf", "xfT"))
        wnat = at("wnat", [P, 3, 2 * D])
        wst = at("wst", [P, 3, 2 * D])
        q_s, k_s = (at(n, [P, HD]) for n in ("q_s", "k_s"))
        xi, yi, state, r_s, u_s, qsg, o_s, oT, gw = (at(n, [P, HD]) for n in ("xi", "yi", "state", "r_s", "u_s", "qsg", "o_s", "oT", "gw"))
        ti = at("ti", [P, HD // 2])
        wqkvg = weights[:, 0:4 * KD * HD].rearrange("p (w k n) -> p w k n", w=4, k=KD)
        wo = weights[:, 4 * KD * HD:5 * KD * HD].rearrange("p (h n) -> p h n", h=H)
        wfc = weights[:, 5 * KD * HD:6 * KD * HD].rearrange("p (k n) -> p k n", k=KD)
        wproj = weights[:, 6 * KD * HD:7 * KD * HD].rearrange("p (f n) -> p f n", f=FB)
        hid = oT
        attention.close()

        psI = [[ctx.enter_context(nc.psum_tensor(f"ps_inv{n}{g}", [P, GW], F32)) for g in range(G)] for n in "ab"]
        psF = [ctx.enter_context(nc.psum_tensor(f"ps_front{n}", [P, GW], F32)) for n in range(2)]
        psB = [ctx.enter_context(nc.psum_tensor(f"ps_back{n}", [P, GW], F32)) for n in range(2)]

        w_loaded = sem("w_loaded")
        small_loaded = sem("small_loaded")
        consts = sem("consts")
        const_dve = sem("const_dve")
        zeroed = sem("zeroed")
        zero_made = sem("zero_made")
        x_loaded = [sem(f"x_loaded{n}") for n in range(XPARTS)]
        pre_dve, pre_h = sem("pre_dve"), sem("pre_h")
        pre_tr, pre_hT, pre_ba, ba_ready = (sem(n) for n in ("pre_tr", "pre_hT", "pre_ba", "ba_ready"))
        hT_stored = [sem(f"hT_stored{n}") for n in range(4)]
        wba_loaded, gate_loaded = sem("wba_loaded"), sem("gate_loaded")
        msc_ready, xln_ready = sem("msc_ready"), sem("xln_ready")
        dec_dve, dec_act, dec_pe = sem("dec_dve"), sem("dec_act"), sem("dec_pe")
        dec_ready = sem("dec_ready")
        hT_loaded = [sem("hT_loaded0"), sem("hT_loaded1")]
        front_filled = [sem("front_filled0"), sem("front_filled1")]
        front_evac = [sem("front_evac0"), sem("front_evac1")]
        sq_ready = sem("sq_ready")
        sc_ready, rhs_ready, ss_ready, rn_ready = (sem(n) for n in ("sc_ready", "rhs_ready", "ss_ready", "rn_ready"))
        norm_pool = sem("norm_pool")
        kn_ready, qn_ready, kb_ready, dtm_ready = (sem(n) for n in ("kn_ready", "qn_ready", "kb_ready", "dtm_ready"))
        vb_ready, kd_ready, gw_ready = (sem(n) for n in ("vb_ready", "kd_ready", "gw_ready"))
        inv_filled = [[sem(f"inv_{n}_filled{g}") for g in range(G)] for n in "ab"]
        x_ready = [sem(f"x_ready{g}") for g in range(G)]
        y_ready = [sem(f"y_ready{g}") for g in range(G)]
        t_ready = [sem(f"t_ready{g}") for g in range(G)]
        y0_dve = sem("y0_dve")
        back_filled = [sem("back_filled0"), sem("back_filled1")]
        back_evac = [sem("back_evac0"), sem("back_evac1")]
        xin_loaded, wnat_loaded, wst_stored = sem("xin_loaded"), sem("wnat_loaded"), sem("wst_stored")
        x1_stored, xf_stored = sem("x1_stored"), sem("xf_stored")
        hid_ready = sem("hid_ready")
        tail_dve, m_pool, x_pool, o_pool = (sem(n) for n in ("tail_dve", "m_pool", "x_pool", "o_pool"))
        so_ready, os_ready, or_ready, og_ready = (sem(n) for n in ("so_ready", "os_ready", "or_ready", "og_ready"))
        mv_ready, mr_ready, m_ready = (sem(n) for n in ("mv_ready", "mr_ready", "m_ready"))
        x1_ready, xv_ready, xr_ready, xf_ready = (sem(n) for n in ("x1_ready", "xv_ready", "xr_ready", "xf_ready"))

        def f_filled(f, u):
            return FU // 2 * f + u // 2 + 1

        def f_evac(f, u):
            return FU // 2 * f + u // 2 + 2

        def b_filled(s, u):
            before = lambda uses, last: sum(1 for n in uses if n % 2 == u % 2 and n <= last)
            if isinstance(s, int) and s == 0:
                return before(STATE_USES, u)
            inner = before(STATE_USES, BU) + BU // 2 * (s - 1)
            return inner + (before(TAIL_USES, u) if isinstance(s, int) and s == TILES else u // 2 + 1)

        def b_evac(s, u):
            return b_filled(s, u) + 1

        N_NORM, N_ROW, N_O = 13, 8, 13

        hb = [a[:, :].rearrange("p (c d) -> p c d", c=CHUNKS) for a in (v_s, g_s)]
        hTb = [a[:, :].rearrange("p (c k n) -> p c k n", c=CHUNKS, k=KD) for a in (kb, kd, vb, q_s)]
        NB = len(hTb)
        pbst4 = yi[:, 0:6 * CHUNKS].rearrange("p (t n) -> p t n", t=CHUNKS)
        pmv4 = yi[:, 64:64 + 2 * CHUNKS].rearrange("p (t n) -> p t n", t=CHUNKS)
        pmv = yi[:, 256:256 + 2 * TILES].rearrange("p (t n) -> p t n", t=TILES)
        pv, pr, pa, pms, pr2, phs = (r_s[:, n * TILES:(n + 1) * TILES] for n in range(6))
        pmean4, phs4 = r_s[:, 256:256 + CHUNKS], r_s[:, 260:260 + CHUNKS]
        pre_ps = psI
        zero = pi_t[:, :]
        ZR = 6

        V3 = lambda a: a.rearrange("p (t e) -> p t e", e=E)
        by_expert = lambda a: a.rearrange("p t e -> p e t")
        over_tiles = lambda s: s.unsqueeze(1).to_broadcast([P, TILES, E])
        TE = TILES * E
        z_b, az_b, tt_b, s_b, s2_b, p_b, den_b = (V3(a[:, 0:TE]) for a in (xi, yi, ti, r_s, u_s, qsg, o_s))
        al1, al2, e1, e2 = (oT[:, n * H:(n + 1) * H] for n in range(4))
        sd, se, pi = V3(xi[:, 0:TE]), V3(yi[:, 0:TE]), V3(pi_t[:, :])
        rowm, rows_, rowl = (r_s[:, n * TILES:(n + 1) * TILES] for n in range(3))
        colm, cmx, cdiag, cols_, coll = r_s[:, 96:104], r_s[0:E, 104:105], r_s[0:E, 112:120], r_s[:, 120:128], r_s[:, 128:136]
        cand, hot, hot2, both = (V3(a[:, 0:TE]) for a in (u_s, qsg, o_s, gw))
        cnt = [V3(hid[:, n * TE:(n + 1) * TE]) for n in range(2)]
        posf = V3(hid[:, 2 * TE:3 * TE])
        need3 = hid[:, 3 * TE:3 * TE + E * MAXT].rearrange("p (e n) -> p e n", e=E)
        need = [r_s[:, 136 + 8 * n:144 + 8 * n] for n in range(4)]
        posk = r_s[:, 256:256 + TILES * TOPK].rearrange("p (t k) -> p t k", k=TOPK)
        tef = r_s[0:1, 384:384 + ETILES]
        te3 = u_s[0:1, 512:512 + ETILES * E].rearrange("p (j e) -> p j e", e=E)
        sk_dve, sk_act, sk_pe = sem("sinkhorn_dve"), sem("sinkhorn_act"), sem("sinkhorn_pe")
        rt_dve, rt_pe, pi_ready = sem("routing_dve"), sem("routing_pe"), sem("pi_ready")
        te_ready, pos_ready = sem("te_ready"), sem("pos_ready")
        xf4_loaded = [sem("xf4_loaded0"), sem("xf4_loaded1")]
        pidx_ready = sem("pidx_ready")
        scattered = [sem("scattered0"), sem("scattered1")]
        pool_turn, sp_turn, dve_turn = sem("pool_turn"), sem("sp_turn"), sem("dve_turn")
        NPAIR = ETILES // 2
        w_raw = sb("w_raw", [P, 3, KD * F])
        w_hi, w_lo = ([sb(f"w_{n}{p}", [P, 3, KD * F]) for p in range(2)] for n in ("hi", "lo"))
        eh_hi, eh_lo = ([sb(f"eh_{n}{p}", [P, FB, ROWS]) for p in range(2)] for n in ("hi", "lo"))
        eh = sb("eh", [P, 4, ROWS])
        sact = sb("sact", [P, 4, ROWS])
        xT_hi, xT_lo = ([sb(f"xT_{n}{p}", [P, KD, ROWS]) for p in range(2)] for n in ("hi", "lo"))
        xrow = [sb(f"xrow{p}", [P, RB, D]) for p in range(2)]
        ybuf = [sb(f"ybuf{p}", [P, RB * D]) for p in range(2)]
        psG = [psI[0][0], psI[0][1], psI[1][0], psI[1][1]]
        NSLOT = len(psG)
        QUARTERS = 4
        PIECES = 2 * QUARTERS
        EARLY = PIECES - 2
        piece = lambda a, m: a[:, m // QUARTERS, m % QUARTERS * (KD * F // QUARTERS):(m % QUARTERS + 1) * (KD * F // QUARTERS)]
        flat = lambda a: a[:, :, :].rearrange("p a b -> p (a b)")
        expert_loaded = [sem(f"expert_{n}_loaded") for n in ("gate", "up", "down")]
        hi_ready = [sem(f"expert_{n}_hi_ready") for n in ("gate", "up", "down")]
        split = [sem(f"expert_{n}_split") for n in ("gate", "up", "down")]
        xrow_loaded = [sem("xrow_loaded0"), sem("xrow_loaded1")]
        xT_filled, xT_hi_ready, xT_ready = sem("xT_filled"), sem("xT_hi_ready"), sem("xT_ready")
        gu_filled = [sem(f"gu_filled{n}") for n in range(NSLOT)]
        sact_ready = [sem(f"sact_ready{n}") for n in range(NSLOT)]
        eh_ready = [sem(f"eh_ready{n}") for n in range(NSLOT)]
        eh_hi_ready = [sem(f"eh_hi_ready{n}") for n in range(NSLOT)]
        eh_split = [sem(f"eh_split{n}") for n in range(NSLOT)]
        y_filled, y_evac = sem("y_filled"), sem("y_evac")
        y_stored = [sem("y_stored0"), sem("y_stored1")]
        x14_loaded = [sem("x14_loaded0"), sem("x14_loaded1")]
        gathered = [sem("gathered0"), sem("gathered1")]
        mix_dve, mixed = sem("mix_dve"), sem("mixed")
        out_stored = [sem("out_stored0"), sem("out_stored1")]
        xb2 = [a[:, :].rearrange("p (c d) -> p c d", c=CHUNKS) for a in (q_s, k_s)]
        yg = [kbqT[:, n].rearrange("p h a n -> p (h a n)").rearrange("p (c k d) -> p c k d", c=CHUNKS, k=TOPK) for n in range(2)]
        SOFTPLUS_TERMS = [1 / 13, 1 / 11, 1 / 9, 1 / 7, 1 / 5, 1 / 3]
        ND_DEC = 23
        SK_D, SK_A, SK_P = 10, 4, 3

        def dve_decays(dve):
            V = nc.vector
            ch = Chain(dve, dec_dve)
            dve.wait_ge(ba_ready, BATCH + 2)
            dve.wait_ge(small_loaded, 16 * 3)
            ch.link(V.tensor_tensor(z_b, ba[:, :, H:2 * H], over_tiles(dtb[:, :]), ALU.add))
            ch.link(V.scalar_tensor_tensor(az_b, z_b, -1.0, z_b, ALU.mult, ALU.max))
            ch.link(V.tensor_scalar(al1, alog[:, :], 80.0, None, ALU.min))
            ch.link(V.tensor_scalar(al2, alog[:, :], -80.0, 0.0, ALU.add, ALU.max))
            ch.link(V.tensor_scalar(al2, al2, 80.0, None, ALU.min))
            dve.wait_ge(dec_act, 3)
            ch.link(V.tensor_scalar(den_b, tt_b, 2.0, None, ALU.add))
            ch.link(V.reciprocal(den_b, den_b))
            ch.link(V.tensor_tensor(s_b, tt_b, den_b, ALU.mult))
            ch.link(V.tensor_tensor(s2_b, s_b, s_b, ALU.mult))
            ch.link(V.tensor_scalar(p_b, s2_b, 1 / 15, None, ALU.mult))
            for c in SOFTPLUS_TERMS:
                ch.link(V.scalar_tensor_tensor(p_b, p_b, c, s2_b, ALU.add, ALU.mult))
            ch.link(V.scalar_tensor_tensor(p_b, p_b, 1.0, s_b, ALU.add, ALU.mult))
            ch.link(V.tensor_scalar(z_b, z_b, 0.0, None, ALU.max))
            ch.link(V.scalar_tensor_tensor(p_b, p_b, 2.0, z_b, ALU.mult, ALU.add))
            ch.link(V.tensor_tensor(p_b, p_b, over_tiles(e1), ALU.mult))
            ch.link(V.tensor_scalar(p_b, p_b, 1e3, None, ALU.min))
            ch.link(V.tensor_tensor(p_b, p_b, over_tiles(e2), ALU.mult))
            ch.link(V.tensor_scalar(dec[:, :, GLOG:GLOG + H], p_b, -1.0, -DEAD, ALU.mult, ALU.max))
            assert ch.n == ND_DEC
            dve.wait_ge(dec_act, 7)
            ch.link(V.tensor_scalar(dec[:, :, NGAM:NGAM + H], dec[:, :, GAM:GAM + H], -1.0, None, ALU.mult))
            V.memset(dec[:, 0:TILES:CHUNKS, GAM:GTOT + H], 0.0).then_inc(dec_ready, 1)

        def act_decays_in(act):
            A = nc.scalar.activation
            act.wait_ge(dec_dve, 5)
            A(tt_b, az_b, ACT.Exp, scale=-1.0).then_inc(dec_act, 1)
            A(e1, al1, ACT.Exp).then_inc(dec_act, 1)
            A(e2, al2, ACT.Exp).then_inc(dec_act, 1)
            A(dec[:, :, BETA:BETA + H], ba[:, :, 0:H], ACT.Sigmoid).then_inc(dec_act, 1)

        def act_decays_out(act):
            A = nc.scalar.activation
            act.wait_ge(dec_pe, 3)
            for ps, c in ((psI[0][0], GAM), (psI[0][1], GTOT), (psI[1][0], DEND)):
                A(dec[:, :, c:c + H], V3(ps[:, 0:TE]), ACT.Exp).then_inc(dec_act, 1)

        def pe_decays(pe):
            pe.wait_ge(dec_dve, ND_DEC)
            for ps, mask in ((psI[0][0], incl), (psI[0][1], ones), (psI[1][0], lower)):
                nc.tensor.matmul(V3(ps[:, 0:TE]), mask[:, :], dec[:, :, GLOG:GLOG + H], start=True, stop=True).then_inc(dec_pe, 1)
            pe.wait_ge(dec_act, 7)

        def dve_late(dve):
            V = nc.vector
            dve.wait_ge(back_evac[BU_LG % 2], b_evac(TILES, BU_LG))
            with dve.Fori(0, ROUNDS) as r:
                ch = Chain(dve, sk_dve, SK_D * r)
                ch.link(V.tensor_reduce(rowm, la[:, :, :], X, ALU.max))
                ch.link(V.tensor_tensor(sd, la[:, :, :], per_head(rowm, E), ALU.subtract))
                dve.wait_ge(sk_act, SK_A * r + 1)
                ch.link(V.tensor_reduce(rows_, se, X, ALU.add))
                dve.wait_ge(sk_act, SK_A * r + 2)
                ch.link(V.tensor_tensor(la[:, :, :], sd, per_head(rowl, E), ALU.subtract))
                ch.link(V.tensor_reduce(colm, by_expert(la[:, :, :]), X, ALU.max))
                dve.wait_ge(sk_pe, SK_P * r + 1)
                ch.link(V.tensor_reduce(cmx, psF[0][0:E, 0:P], X, ALU.max))
                ch.link(V.tensor_scalar(cdiag, ident[0:E, 0:E], cmx, None, ALU.mult))
                dve.wait_ge(sk_pe, SK_P * r + 2)
                ch.link(V.tensor_tensor(sd, la[:, :, :], over_tiles(psF[1][:, 0:E]), ALU.subtract))
                dve.wait_ge(sk_act, SK_A * r + 3)
                ch.link(V.tensor_reduce(cols_, by_expert(se), X, ALU.add))
                dve.wait_ge(sk_act, SK_A * r + 4)
                ch.link(V.tensor_tensor(la[:, :, :], sd, over_tiles(coll), ALU.subtract))
                assert ch.n == SK_D
            ch = Chain(dve, rt_dve)
            ch.link(V.tensor_scalar(sd, la[:, :, :], EXP_ZERO, None, ALU.max))
            for n, h in enumerate((hot, hot2)):
                ch.link(V.tensor_reduce(rowm, sd, X, ALU.max))
                ch.link(V.tensor_tensor(se, sd, per_head(rowm, E), ALU.is_equal))
                ch.link(V.tensor_tensor(cand, se, over_tiles(rank_w[:, :]), ALU.mult))
                ch.link(V.tensor_reduce(rows_, cand, X, ALU.max))
                ch.link(V.tensor_tensor(h, cand, per_head(rows_, E), ALU.is_equal))
                if n == 0:
                    ch.link(V.scalar_tensor_tensor(sd, h, -1e30, sd, ALU.mult, ALU.add))
            ch.link(V.tensor_tensor(both, hot, hot2, ALU.add))
            assert ch.n == 13
            dve.wait_ge(rt_pe, 2)
            ch.link(V.tensor_copy(cnt[0], V3(psF[1][:, 0:TE])))
            cur = 0
            for s in (1, 2, 4, 8, 16):
                V.tensor_copy(cnt[1 - cur][:, 0:s], cnt[cur][:, 0:s])
                ch.link(V.tensor_tensor(cnt[1 - cur][:, s:], cnt[cur][:, s:], cnt[cur][:, 0:TILES - s], ALU.add))
                cur = 1 - cur
            ch.link(V.tensor_tensor(posf, cnt[cur], V3(psF[1][:, 0:TE]), ALU.subtract))
            ch.link(V.tensor_tensor(posf, posf, V3(psF[0][:, 0:TE]), ALU.add))
            ch.link(V.tensor_tensor(need3, per_head(cnt[cur][:, TILES - 1, :], MAXT), thresholds[:, :].unsqueeze(1).to_broadcast([P, E, MAXT]), ALU.is_gt))
            ch.link(V.tensor_reduce(need[0], need3, X, ALU.add))
            ch.link(V.tensor_copy(need[1], need[0]))
            a, b = need[1], need[2]
            for s in (1, 2, 4):
                V.tensor_copy(b[:, 0:s], a[:, 0:s])
                ch.link(V.tensor_tensor(b[:, s:], a[:, s:], a[:, 0:E - s], ALU.add))
                a, b = b, a
            ch.link(V.tensor_tensor(need[3], a, need[0], ALU.subtract))
            ch.link(V.tensor_scalar(need[3], need[3], float(ROWS), None, ALU.mult))
            ch.link(V.tensor_tensor(posf, posf, over_tiles(need[3]), ALU.add))
            for k, h in enumerate((hot, hot2)):
                ch.link(V.tensor_tensor(cand, h, posf, ALU.mult))
                ch.link(V.tensor_reduce(posk[:, :, k], cand, X, ALU.add))
            V.tensor_copy(posi[:, :, :], posk).then_inc(pos_ready, 1)
            ch.link(V.tensor_tensor(te3, tile_iota[:, :].unsqueeze(2).to_broadcast([1, ETILES, E]), a[0:1, :].unsqueeze(1).to_broadcast([1, ETILES, E]), ALU.is_ge))
            ch.link(V.tensor_reduce(tef, te3, X, ALU.add))
            ch.link(V.tensor_scalar(tef, tef, float(E - 1), None, ALU.min))
            V.tensor_copy(te_i[:, :], tef).then_inc(te_ready, 1)
            dve.wait_ge(pos_ready, 1)
            def places(b, p):
                V.tensor_copy(pidx[:, p], posi[:, bass.ds(b * CHUNKS, CHUNKS), :]).then_inc(pidx_ready, 1)

            for p in range(2):
                places(p, p)
            with dve.Fori(1, BATCH // 2) as i:
                for p in range(2):
                    dve.wait_ge(scattered[p], 128 * i)
                    places(2 * i + p, p)

            def low(m, j, p):
                n = m // QUARTERS
                dve.wait_ge(hi_ready[n], QUARTERS * j + m % QUARTERS + 1)
                V.tensor_tensor(piece(w_lo[p], m).bitcast(F32R), piece(w_raw, m), piece(w_hi[p], m), ALU.subtract).then_inc(split[n], 1)

            def rows_T(j, p):
                dve.wait_ge(xT_hi_ready, j + 1)
                V.tensor_tensor(flat(xT_lo[p]).bitcast(F32R), psF[p][:, :], flat(xT_hi[p]), ALU.subtract).then_inc(xT_ready, 1)

            def low_h(j, p, fb):
                s, n = fb % NSLOT, FB // NSLOT * j + fb // NSLOT
                dve.wait_ge(eh_hi_ready[s], n + 1)
                V.tensor_tensor(eh_lo[p][:, fb, :].bitcast(F32R), eh[:, s, :], eh_hi[p][:, fb, :], ALU.subtract).then_inc(eh_split[s], 1)

            def expert(j, p, more):
                for fb in range(FB):
                    s, n = fb % NSLOT, FB // NSLOT * j + fb // NSLOT
                    dve.wait_ge(sact_ready[s], n + 1)
                    V.tensor_tensor(eh[:, s, :], sact[:, s, :], psG[s][:, ROWS:2 * ROWS], ALU.mult).then_inc(eh_ready[s], 1)
                    if fb > 0:
                        low_h(j, p, fb - 1)
                    if more and fb < EARLY:
                        low(fb, j + 1, 1 - p)
                low_h(j, p, FB - 1)
                if more:
                    rows_T(j + 1, 1 - p)
                    for m in range(EARLY, PIECES):
                        low(m, j + 1, 1 - p)

            for m in range(PIECES):
                low(m, 0, 0)
            rows_T(0, 0)
            with dve.Fori(0, NPAIR) as i:
                for p in range(2):
                    expert(2 * i + p, p, True)
            expert(ETILES - 1, 0, False)
            dve.wait_ge(pi_ready, 1)
            for p in range(2):
                dve.wait_ge(scattered[p], 128 * (BATCH // 2))
                places(p, p)

            def mix(b, p, i):
                ch = Chain(dve, mix_dve, 2 * b)
                ch.link(V.tensor_copy(pw[:, p], pi[:, bass.ds(b * CHUNKS, CHUNKS), 0:TOPK]))
                dve.wait_ge(x14_loaded[p], 16 * i + 16)
                dve.wait_ge(gathered[p], 128 * i + 128)
                for k in range(TOPK):
                    for c in range(CHUNKS):
                        ins = V.scalar_tensor_tensor(xb2[p][:, c, :], yg[p][:, c, k, :], pw[:, p, c, k:k + 1], xb2[p][:, c, :], ALU.mult, ALU.add)
                    if k == 0:
                        ch.link(ins)
                ins.then_inc(mixed, 1)

            with dve.Fori(0, BATCH // 2 - 1) as i:
                for p in range(2):
                    mix(2 * i + p, p, i)
                    places(2 * i + p + 2, p)
            for p in range(2):
                mix(BATCH - 2 + p, p, BATCH // 2 - 1)

        def act_late(act):
            A = nc.scalar.activation
            act.preload_act_table_set("natural_log_exp_and_others")
            with act.Fori(0, ROUNDS) as r:
                act.wait_ge(sk_dve, SK_D * r + 2)
                A(se, sd, ACT.Exp).then_inc(sk_act, 1)
                act.wait_ge(sk_dve, SK_D * r + 3)
                A(rowl, rows_, ACT.Ln).then_inc(sk_act, 1)
                act.wait_ge(sk_dve, SK_D * r + 8)
                A(se, sd, ACT.Exp).then_inc(sk_act, 1)
                act.wait_ge(sk_pe, SK_P * r + 3)
                A(coll, psB[0][:, 0:E], ACT.Ln).then_inc(sk_act, 1)
            act.wait_ge(sk_dve, SK_D * ROUNDS)
            A(pi, la[:, :, :], ACT.Exp).then_inc(pi_ready, 1)

            def rows_T(j, p):
                act.wait_ge(xT_filled, j + 1)
                A(flat(xT_hi[p]).bitcast(F32R), psF[p][:, :], ACT.Copy).then_inc(xT_hi_ready, 1)

            def high(m, j, p, first):
                n = m // QUARTERS
                act.wait_ge(expert_loaded[n], 16 * j + 16)
                if not first:
                    act.wait_ge(y_filled, j - 1)
                A(piece(w_hi[p], m).bitcast(F32R), piece(w_raw, m), ACT.Copy).then_inc(hi_ready[n], 1)

            def high_h(j, p, fb):
                s, n = fb % NSLOT, FB // NSLOT * j + fb // NSLOT
                act.wait_ge(eh_ready[s], n + 2)
                A(eh_hi[p][:, fb, :].bitcast(F32R), eh[:, s, :], ACT.Copy).then_inc(eh_hi_ready[s], 1)

            def expert(j, p, i, more):
                for fb in range(FB):
                    s, n = fb % NSLOT, FB // NSLOT * j + fb // NSLOT
                    act.wait_ge(eh_ready[s], n + 1)
                    act.wait_ge(gu_filled[s], n + 1)
                    A(sact[:, s, :], psG[s][:, 0:ROWS], ACT.Silu).then_inc(sact_ready[s], 1)
                    if fb > 0:
                        high_h(j, p, fb - 1)
                    if more and fb < EARLY:
                        high(fb, j + 1, 1 - p, False)
                high_h(j, p, FB - 1)
                if more:
                    rows_T(j + 1, 1 - p)
                    for m in range(EARLY, PIECES):
                        high(m, j + 1, 1 - p, False)
                act.wait_ge(y_stored[p], 16 * i + 16)
                act.wait_ge(y_filled, j + 1)
                A(ybuf[p][:, :], psB[p][:, :], ACT.Copy).then_inc(y_evac, 1)
                act.wait_ge(y_evac, j + 3)
                act.dma_start(ys_d[bass.ds(j * ROWS, ROWS), :].rearrange("(r p) d -> p r d", p=P), ybuf[p][:, :].rearrange("p (r d) -> p r d", r=RB)).then_inc(y_stored[p], 16)

            for m in range(PIECES):
                high(m, 0, 0, True)
            rows_T(0, 0)
            with act.Fori(0, NPAIR) as i:
                for p in range(2):
                    expert(2 * i + p, p, i, True)
            expert(ETILES - 1, 0, NPAIR, False)

        def pe_late(pe):
            MM = nc.tensor.matmul
            with pe.Fori(0, ROUNDS) as r:
                pe.wait_ge(sk_dve, SK_D * r + 5)
                nc.tensor.transpose(psF[0][0:E, 0:P], colm, ident[:, :]).then_inc(sk_pe, 1)
                pe.wait_ge(sk_dve, SK_D * r + 7)
                MM(psF[1][:, 0:E], ones[0:E, :], cdiag, start=True, stop=True).then_inc(sk_pe, 1)
                pe.wait_ge(sk_dve, SK_D * r + 9)
                MM(psB[0][:, 0:E], ones[:, :], cols_, start=True, stop=True).then_inc(sk_pe, 1)
            pe.wait_ge(rt_dve, 13)
            MM(V3(psF[0][:, 0:TE]), upper[:, :], both, start=True, stop=True).then_inc(rt_pe, 1)
            MM(V3(psF[1][:, 0:TE]), ones[:, :], both, start=True, stop=True).then_inc(rt_pe, 1)

            def rows_T(j, p, i):
                pe.wait_ge(xrow_loaded[p], 16 * i + 16)
                pe.wait_ge(xT_ready, j + 1)
                for k in range(KD):
                    for r in range(RB):
                        c = (k * RB + r) * P
                        last = nc.tensor.transpose(psF[p][:, c:c + P], xrow[p][:, r, k * P:(k + 1) * P], ident[:, :])
                last.then_inc(xT_filled, 1)

            def exact(out_, w, x, start, stop):
                for n, (a, b) in enumerate(((0, 0), (0, 1), (1, 0))):
                    ins = MM(out_, w[a].bitcast(F32R), x[b].bitcast(F32R), start=start and n == 0, stop=stop and n == 2)
                return ins

            def expert(j, p, i, more):
                pe.wait_ge(xT_ready, j + 3)
                for w in range(2):
                    pe.wait_ge(split[w], QUARTERS * (j + 1))
                for fb in range(FB):
                    s, n = fb % NSLOT, FB // NSLOT * j + fb // NSLOT
                    pe.wait_ge(eh_ready[s], n + 1)
                    for w in range(2):
                        for k in range(KD):
                            c = k * F + fb * P
                            last = exact(psG[s][:, w * ROWS:(w + 1) * ROWS], [a[p][:, w, c:c + P] for a in (w_hi, w_lo)],
                                         [a[p][:, k, :] for a in (xT_hi, xT_lo)], k == 0, k == KD - 1)
                    last.then_inc(gu_filled[s], 1)
                if more:
                    rows_T(j + 1, 1 - p, i + p)
                pe.wait_ge(split[2], j + 1)
                pe.wait_ge(y_evac, j + 1)
                for r in range(RB):
                    for fb in range(FB):
                        if r == 0:
                            s, n = fb % NSLOT, FB // NSLOT * j + fb // NSLOT
                            pe.wait_ge(eh_split[s], n + 1)
                        last = exact(psB[p][:, r * D:(r + 1) * D], [a[p][:, fb, r * P:(r + 1) * P] for a in (eh_hi, eh_lo)],
                                     [a[p][:, 2, fb * D:(fb + 1) * D] for a in (w_hi, w_lo)], fb == 0, fb == FB - 1)
                last.then_inc(y_filled, 1)

            pe.wait_ge(te_ready, 1)
            rows_T(0, 0, 0)
            with pe.Fori(0, NPAIR) as i:
                for p in range(2):
                    expert(2 * i + p, p, i, True)
            expert(ETILES - 1, 0, NPAIR, False)

        def pool_late(pool):
            for s in eh_ready:
                pool.sem_inc(s, 1)
            pool.sem_inc(xT_ready, 2)
            pool.sem_inc(y_evac, 2)
            for s in y_stored + out_stored:
                pool.sem_inc(s, 16)
            pool.wait_ge(zeroed, 16 * (ETILES * ROWS // (P * ZR)))
            with pool.Fori(0, BATCH // 2) as i:
                for p in range(2):
                    pool.wait_ge(xf4_loaded[p], 16 * i + 16)
                    pool.wait_ge(pidx_ready, 2 * i + p + 1)
                    pool.sem_inc(pool_turn, 1)
                    for c in range(CHUNKS):
                        for k in range(TOPK):
                            pool.indirect_dma_start(xs_d[:, :], bass.IndirectOffsetOnAxis(ap=pidx[:, p, c, k:k + 1], axis=0), xb2[p][:, c, :], None).then_inc(scattered[p], 16)
            def split_down(j, p, first):
                pool.wait_ge(expert_loaded[2], 16 * j + 16)
                pool.sem_inc(pool_turn, 1)
                if not first:
                    pool.wait_ge(y_filled, j - 1)
                    pool.sem_inc(pool_turn, 1)
                pool.tensor_copy(w_hi[p][:, 2].bitcast(F32R), w_raw[:, 2]).then_inc(hi_ready[2], 1)
                pool.wait_ge(hi_ready[2], j + 1)
                pool.tensor_tensor(w_lo[p][:, 2].bitcast(F32R), w_raw[:, 2], w_hi[p][:, 2], ALU.subtract).then_inc(split[2], 1)

            split_down(0, 0, True)
            split_down(1, 1, True)
            with pool.Fori(1, NPAIR) as i:
                for p in range(2):
                    split_down(2 * i + p, p, False)
            split_down(ETILES - 1, 0, False)
            pool.wait_ge(y_stored[0], 16 * (NPAIR + 1) + 16)
            pool.wait_ge(y_stored[1], 16 * NPAIR + 16)
            with pool.Fori(0, BATCH // 2) as i:
                for p in range(2):
                    pool.wait_ge(pidx_ready, BATCH + 2 * i + p + 1)
                    pool.sem_inc(pool_turn, 1)
                    for c in range(CHUNKS):
                        for k in range(TOPK):
                            pool.indirect_dma_start(yg[p][:, c, k, :], None, ys_d[:, :], bass.IndirectOffsetOnAxis(ap=pidx[:, p, c, k:k + 1], axis=0)).then_inc(gathered[p], 16)

        def sp_late(sp):
            def load_xf(b, p):
                sp.dma_start(xb2[p], xf_d[bass.ds(b * CHUNKS, CHUNKS)].rearrange("c p d -> p c d")).then_inc(xf4_loaded[p], 16)

            def load_weights(j, first):
                e = sp.value_load(te_i[0:1, bass.ds(j, 1)] if not isinstance(j, int) else te_i[0:1, j:j + 1], min_val=0, max_val=E - 1)
                for n in range(3):
                    if not first:
                        sp.wait_ge(split[n], (QUARTERS if n < 2 else 1) * j)
                        sp.sem_inc(sp_turn, 1)
                    sp.dma_start(w_raw[:, n], wts_d[bass.ds(e, 1), :, n * KD * F:(n + 1) * KD * F].rearrange("a p n -> p (a n)")).then_inc(expert_loaded[n], 16)

            def load_rows(j, p, first):
                if not first:
                    sp.wait_ge(xT_filled, j - 1)
                    sp.sem_inc(sp_turn, 1)
                sp.dma_start(xrow[p][:, :, :], xs_d[bass.ds(j * ROWS, ROWS), :].rearrange("(r p) d -> p r d", p=P)).then_inc(xrow_loaded[p], 16)

            load_xf(0, 0), load_xf(1, 1)
            sp.wait_ge(te_ready, 1)
            load_weights(0, True)
            with sp.Fori(1, BATCH // 2) as i:
                for p in range(2):
                    sp.wait_ge(scattered[p], 128 * i)
                    sp.sem_inc(sp_turn, 1)
                    load_xf(2 * i + p, p)
            for p in range(2):
                sp.wait_ge(scattered[p], 128 * (BATCH // 2))
            load_rows(0, 0, True)
            load_rows(1, 1, True)
            load_weights(1, False)
            with sp.Fori(1, NPAIR) as i:
                for p in range(2):
                    load_rows(2 * i + p, p, False)
                    load_weights(2 * i + p, False)
            load_rows(ETILES - 1, 0, False)
            load_weights(ETILES - 1, False)
            sp.wait_ge(y_stored[0], 16 * (NPAIR + 1) + 16)
            sp.wait_ge(y_stored[1], 16 * NPAIR + 16)

            def load_x1(b, p, i):
                sp.wait_ge(out_stored[p], 16 * i + 16)
                sp.sem_inc(sp_turn, 1)
                sp.dma_start(xb2[p], x1_d[bass.ds(b * CHUNKS, CHUNKS)].rearrange("c p d -> p c d")).then_inc(x14_loaded[p], 16)

            with sp.Fori(0, BATCH // 2) as i:
                for p in range(2):
                    load_x1(2 * i + p, p, i)
                for p in range(2):
                    sp.wait_ge(mixed, 2 * i + p + 1)
                    sp.sem_inc(sp_turn, 1)
                    sp.dma_start(out_tiles[bass.ds((2 * i + p) * CHUNKS, CHUNKS)].rearrange("c p d -> p c d"), xb2[p]).then_inc(out_stored[p], 16)
            for p in range(2):
                sp.wait_ge(out_stored[p], 16 * (BATCH // 2) + 16)

        block = ctx.enter_context(nc.Block())

        @block.sync
        def _(sp):
            sp.dma_start(wba[:, :, 0:H], Wb.rearrange("(k p) n -> p k n", p=P)).then_inc(wba_loaded, 16)
            sp.dma_start(wba[:, :, H:2 * H], Wa.rearrange("(k p) n -> p k n", p=P)).then_inc(wba_loaded, 16)
            for n in range(XPARTS):
                s = slice(n * TILES // XPARTS, (n + 1) * TILES // XPARTS)
                sp.dma_start(x_all[:, s, :], x_tiles[s].rearrange("c p d -> p c d")).then_inc(x_loaded[n], 16)
            sp.dma_start(alog[:, :], A_log.partition_broadcast(P)).then_inc(small_loaded, 16)
            sp.dma_start(dtb[:, :], dt_bias.partition_broadcast(P)).then_inc(small_loaded, 16)
            sp.dma_start(onorm[:, :], o_norm_w.partition_broadcast(P)).then_inc(small_loaded, 16)
            for n, w in enumerate((Wq, Wk, Wv, Wg)):
                sp.dma_start(wqkvg[:, n], w.rearrange("(k p) n -> p k n", p=P)).then_inc(w_loaded, 16)
            with sp.Fori(0, BATCH // NB) as i:
                for p in range(NB):
                    b = NB * i + p
                    sp.wait_ge(pre_hT, 2 * b + 2)
                    sp.sem_inc(sp_turn, 1)
                    sp.dma_start(hT_d[bass.ds(CHUNKS * b, CHUNKS)].rearrange("c p (k n) -> p c k n", k=KD), hTb[p]).then_inc(hT_stored[p], 16)
            for p in range(NB):
                sp.wait_ge(hT_stored[p], 16 * (BATCH // NB) + 16)

            def load_hT(f, q):
                sp.dma_start(hT[:, q], hT_d[f].rearrange("p (k n) -> p k n", k=KD)).then_inc(hT_loaded[q], 16)

            def tail(t):
                sp.wait_ge(x1_ready, t + 1)
                sp.sem_inc(sp_turn, 1)
                sp.dma_start(x1_d[t], x1[:, :]).then_inc(x1_stored, 16)
                sp.wait_ge(xf_ready, t + 1)
                sp.sem_inc(sp_turn, 1)
                sp.dma_start(xf_d[t], xf[:, :]).then_inc(xf_stored, 16)

            def step(t, p, ahead, before, e, c):
                if ahead:
                    sp.wait_ge(front_filled[1], f_filled(t, FU_PROJ + 7))
                    sp.sem_inc(sp_turn, 1)
                    load_hT(t + 2, p)
                r0 = c * (F // CHUNKS)
                if before:
                    sp.wait_ge(back_evac[(BU_PREP + 2) % 2], b_evac(t - 1, BU_PREP + 2))
                    sp.sem_inc(sp_turn, 1)
                sp.dma_start(wnat[:, 0].rearrange("p (f d) -> p f d", f=2),
                             W_gate[e][bass.ds(r0, 2 * P)].rearrange("(f p) d -> p f d", p=P)).then_inc(wnat_loaded, 16)
                sp.dma_start(wnat[:, 1].rearrange("p (f d) -> p f d", f=2),
                             W_up[e][bass.ds(r0, 2 * P)].rearrange("(f p) d -> p f d", p=P)).then_inc(wnat_loaded, 16)
                sp.dma_start(wnat[:, 2].rearrange("p (k f) -> p k f", k=KD),
                             W_down[e][:, bass.ds(r0, 2 * P)].rearrange("(k p) f -> p k f", p=P)).then_inc(wnat_loaded, 16)
                if before:
                    tail(t - 1)
                sp.dma_start(xin[:, 0, :], x_tiles[t]).then_inc(xin_loaded, 16)
                sp.wait_ge(back_evac[(BU_PREP + 1) % 2], b_evac(t, BU_PREP + 1))
                sp.sem_inc(sp_turn, 1)
                sp.wait_ge(back_evac[(BU_PREP + 2) % 2], b_evac(t, BU_PREP + 2))
                sp.sem_inc(sp_turn, 1)
                for n in range(2):
                    sp.dma_start(wts_d[e][:, n * KD * F:(n + 1) * KD * F].rearrange("p (k f) -> p k f", k=KD)[:, :, bass.ds(r0, 2 * P)],
                                 wst[:, n].rearrange("p (k f) -> p k f", k=KD)).then_inc(wst_stored, 16)
                sp.dma_start(wts_d[e][:, bass.ds(2 * KD * F + c * 2 * D, 2 * D)], wst[:, 2]).then_inc(wst_stored, 16)

            load_hT(0, 0)
            load_hT(1, 1)
            sp.dma_start(wo, Wo.rearrange("(h p) n -> p h n", p=P)).then_inc(w_loaded, 16)
            sp.dma_start(wfc, W_fc.rearrange("(k p) n -> p k n", p=P)).then_inc(w_loaded, 16)
            sp.dma_start(wproj, W_proj.rearrange("(f p) n -> p f n", p=P)).then_inc(w_loaded, 16)
            with nc.allow_non_contiguous_dma(reason="2048 elements, once"):
                for k in range(KD):
                    sp.dma_start(gwT[:, k, :], gate_W[:, k * P:(k + 1) * P].rearrange("e p -> p e")).then_inc(gate_loaded, 16)
            sp.wait_ge(zero_made, 1)
            for n in range(ETILES * ROWS // (P * ZR)):
                sp.dma_start(xs_d[n * P * ZR:(n + 1) * P * ZR, :].rearrange("(p r) d -> p r d", p=P), zero.unsqueeze(1).to_broadcast([P, ZR, D])).then_inc(zeroed, 16)
            step(0, 0, True, False, 0, 0)
            with sp.Fori(0, PAIRS - 1) as i:
                for p in range(2):
                    t = 2 * i + p + 1
                    step(t, 1 - p, True, True, t // CHUNKS, t % CHUNKS)
            for t in range(2 * PAIRS - 1, TILES):
                step(t, t % 2, t + 2 < TILES, True, t // CHUNKS, t % CHUNKS)
            tail(TILES - 1)
            sp.wait_ge(x1_stored, 16 * TILES + 16)
            sp.wait_ge(xf_stored, 16 * TILES + 16)
            sp.wait_ge(wst_stored, 48 * TILES + 48)
            sp_late(sp)

        @block.gpsimd
        def _(pool):
            pool.memset(zero, 0.0).then_inc(zero_made, 1)
            pool.memset(ones[:, :], 1.0).then_inc(consts, 1)
            pool.memset(state[:, :], 0.0).then_inc(consts, 1)
            pool.iota(iota_i[:, 0, :], pattern=[[0, P]], base=0, channel_multiplier=1).then_inc(consts, 1)
            pool.iota(iota_i[:, 1, :], pattern=[[1, P]], base=0, channel_multiplier=0).then_inc(consts, 1)
            pool.iota(tile_iota[:, :], pattern=[[1, ETILES]], base=0, channel_multiplier=0, allow_small_or_imprecise_dtypes=True).then_inc(consts, 1)
            pool.iota(thresholds[:, :], pattern=[[ROWS, MAXT]], base=0, channel_multiplier=0, allow_small_or_imprecise_dtypes=True).then_inc(consts, 1)
            pool.iota(rank_w[:, :], pattern=[[-1, E]], base=E, channel_multiplier=0, allow_small_or_imprecise_dtypes=True).then_inc(consts, 1)
            pool.wait_ge(consts, 7)
            pool.affine_select(out=incl[:, :], in_=ones[:, :], compare_op=ALU.is_ge, fill=0.0, base=0,
                               pattern=[[1, P]], channel_multiplier=-1).then_inc(consts, 1)
            pool.affine_select(out=upper[:, :], in_=ones[:, :], compare_op=ALU.is_gt, fill=0.0, base=0,
                               pattern=[[1, P]], channel_multiplier=-1).then_inc(consts, 1)
            pool.affine_select(out=lower[:, :], in_=ones[:, :], compare_op=ALU.is_gt, fill=0.0, base=0,
                               pattern=[[-1, P]], channel_multiplier=1).then_inc(consts, 1)
            pool.affine_select(out=ident[:, :], in_=ones[:, :], compare_op=ALU.is_equal, fill=0.0, base=0,
                               pattern=[[1, P]], channel_multiplier=-1).then_inc(consts, 1)
            for s in front_evac + back_evac:
                pool.sem_inc(s, 1)
            pool.sem_inc(ba_ready, 2)
            pool.sem_inc(pre_tr, 4)
            for s in [x1_stored, xf_stored] + hT_stored:
                pool.sem_inc(s, 16)
            pool.sem_inc(wst_stored, 48)
            def front_early(f, q, first):
                pool.tensor_copy(sc[:, q, :].unsqueeze(1), dec[:, bass.ds(f, 1), :]).then_inc(sc_ready, 1)
                if not first:
                    pool.wait_ge(front_evac[0], f_evac(f - 1, FU_KKQ + 2))
                    pool.wait_ge(front_evac[1], f_evac(f - 1, FU_KKQ + 3))
                pool.wait_ge(sc_ready, f + 1)
                pool.tensor_tensor(dT[:, :, :], over_heads(incl[:, :], H), per_head(sc[:, q, GLOG:GLOG + H]), ALU.mult).then_inc(rhs_ready, 1)

            def link(ins, chain, n):
                ins.then_inc(chain, 1)
                pool.wait_ge(chain, n)
                pool.sem_inc(pool_turn, 1)

            def first_root(v, r, chain, n):
                link(pool.tensor_scalar(r.bitcast(I32), v.bitcast(I32), -0.5, ROOT_MAGIC, ALU.mult, ALU.add), chain, n)

            def roots(v, r, a, chain, n, ready):
                first_root(v, r, chain, n + 1)
                for k in range(3):
                    m = n + 4 * k + 1
                    link(pool.tensor_tensor(a, r, r, ALU.mult), chain, m + 1)
                    link(pool.tensor_tensor(a, a, v, ALU.mult), chain, m + 2)
                    link(pool.tensor_scalar(a, a, -0.5, 1.5, ALU.mult, ALU.add), chain, m + 3)
                    last = pool.tensor_tensor(r, a, r, ALU.mult)
                    if k < 2:
                        link(last, chain, m + 4)
                last.then_inc(ready, 1)

            def row_root(v, r, a, chain, n, ready):
                first_root(v, r, chain, n + 1)
                c = 1.0
                for k in range(3):
                    m = n + 2 * k + 1
                    link(pool.tensor_scalar(a, r, r, v, ALU.mult, ALU.mult), chain, m + 1)
                    link(pool.tensor_scalar(r, a, -3.0 * c * c, r, ALU.add, ALU.mult), chain, m + 2)
                    c *= -2.0 * c * c
                pool.tensor_scalar(r, r, 1.0 / c, None, ALU.mult).then_inc(ready, 1)

            def norm_roots(f):
                pool.wait_ge(ss_ready, 2 * f + 2)
                pool.sem_inc(pool_turn, 1)
                link(pool.tensor_scalar(nv[:, :], ss[:, :], RMS_EPS, None, ALU.add), norm_pool, N_NORM * f + 1)
                roots(nv[:, :], rn[:, :], na[:, :], norm_pool, N_NORM * f + 1, rn_ready)

            def m_root(t):
                pool.wait_ge(mv_ready, t + 1)
                pool.sem_inc(pool_turn, 1)
                n = N_ROW * t + 1
                link(pool.tensor_scalar(mrow_v[:, 1:2], mrow_v[:, 0:1], 1.0 / D, RMS_EPS, ALU.mult, ALU.add), m_pool, n)
                row_root(mrow_v[:, 1:2], mrow_r[:, 0:1], mrow_r[:, 1:2], m_pool, n, mr_ready)

            def x_root(t):
                pool.wait_ge(xv_ready, t + 1)
                pool.sem_inc(pool_turn, 1)
                n = N_ROW * t + 1
                link(pool.tensor_scalar(xrow_v[:, 0:1], bag[:, 1:2], LN_EPS, None, ALU.add), x_pool, n)
                row_root(xrow_v[:, 0:1], xrow_r[:, 0:1], xrow_r[:, 1:2], x_pool, n, xr_ready)

            def o_roots(t):
                pool.wait_ge(os_ready, t + 1)
                pool.sem_inc(pool_turn, 1)
                link(pool.tensor_scalar(os_[:, 1, :], os_[:, 0, :], 1.0 / DK, RMS_EPS, ALU.mult, ALU.add), o_pool, N_O * t + 1)
                roots(os_[:, 1, :], or_[:, 0, :], or_[:, 1, :], o_pool, N_O * t + 1, or_ready)

            def front_mid(f, q):
                pool.wait_ge(kn_ready, f + 1)
                pool.tensor_tensor(kb[:, :].rearrange("p (h d) -> p h d", h=H), k_s[:, :].rearrange("p (h d) -> p h d", h=H),
                                   per_head(sc[:, q, BETA:BETA + H]), ALU.mult).then_inc(kb_ready, 1)
                for n in range(G):
                    pool.wait_ge(front_evac[n], f_evac(f, FU_D + n))
                    d = dT[:, n * HG:(n + 1) * HG, :]
                    pool.tensor_tensor(d, d, over_heads(incl[:, :]), ALU.mult).then_inc(dtm_ready, 1)

            heads = lambda a: a[:, :].rearrange("p (h d) -> p h d", h=H)

            def decayed_k(f, q):
                pool.wait_ge(kn_ready, f + 1)
                pool.tensor_tensor(heads(kd), heads(k_s), per_head(sc[:, q, DEND:DEND + H]), ALU.mult).then_inc(kd_ready, 1)

            def beta_v(f, q):
                pool.wait_ge(front_evac[1], f_evac(f, FU_PROJ + 5))
                pool.tensor_tensor(heads(vb), heads(v_s), per_head(sc[:, q, BETA:BETA + H]), ALU.mult).then_inc(vb_ready, 1)

            def front_gate(f):
                pool.wait_ge(front_evac[1], f_evac(f, FU_PROJ + 7))
                pool.tensor_tensor(heads(gw), heads(g_s), over_heads(onorm[:, :], H), ALU.mult).then_inc(gw_ready, 1)

            def step(t, p, more, tail):
                f, q = t + 1, 1 - p
                if more:
                    front_early(f, q, False)
                if tail:
                    m_root(t - 1)
                if more:
                    norm_roots(f)
                    front_mid(f, q)
                if tail:
                    x_root(t - 1)
                if more:
                    pool.wait_ge(back_evac[BU_KDU % 2], b_evac(t, BU_KDU))
                    pool.wait_ge(back_evac[(BU_KDU + 1) % 2], b_evac(t, BU_KDU + 1))
                    decayed_k(f, q)
                o_roots(t)
                if more:
                    beta_v(f, q)
                    pool.wait_ge(og_ready, t + 1)
                    front_gate(f)

            pool.wait_ge(dec_ready, 1)
            pool.wait_ge(small_loaded, 16 * 3)
            front_early(0, 0, True)
            norm_roots(0)
            front_mid(0, 0)
            decayed_k(0, 0)
            beta_v(0, 0)
            front_gate(0)
            step(0, 0, True, False)
            with pool.Fori(0, PAIRS) as i:
                for p in range(2):
                    step(2 * i + p + 1, 1 - p, True, True)
            step(TILES - 1, 1, False, True)
            m_root(TILES - 1)
            x_root(TILES - 1)
            pool_late(pool)

        @block.scalar
        def _(act):
            A = nc.scalar.activation
            with act.Fori(0, BATCH // NB) as i:
                for p in range(NB + 1):
                    if p < NB:
                        b = NB * i + p
                        act.wait_ge(hT_stored[p], 16 * i + 16)
                        for n in range(2):
                            act.wait_ge(pre_tr, 2 * b + n + 5)
                            A(hTb[p][:, 2 * n:2 * n + 2].rearrange("p c k n -> p (c k n)"), pre_ps[p % 2][n][:, :], ACT.Copy).then_inc(pre_hT, 1)
                    if p > 0:
                        b = NB * i + p - 1
                        act.wait_ge(pre_ba, b + 1)
                        A(ba[:, bass.ds(CHUNKS * b, CHUNKS), :], psB[(p - 1) % 2][:, 0:CHUNKS * 2 * H].rearrange("p (c n) -> p c n", c=CHUNKS), ACT.Copy).then_inc(ba_ready, 1)
            act_decays_in(act)

            def silu(f, n, first):
                u = FU_PROJ + n
                if not first and n in (2, 4, 6):
                    act.wait_ge({2: kd_ready, 4: vb_ready, 6: gw_ready}[n], f)
                act.wait_ge(front_filled[u % 2], f_filled(f, u))
                A((q_s, k_s, v_s, g_s)[n // 2][:, n % 2 * GW:(n % 2 + 1) * GW], psF[u % 2][:, :], ACT.Silu).then_inc(front_evac[u % 2], 1)

            def square(f, n):
                if n == 1:
                    act.wait_ge(ss_ready, 2 * f + 1)
                act.wait_ge(front_evac[0], f_evac(f, FU_PROJ + 2 * n))
                act.wait_ge(front_evac[1], f_evac(f, FU_PROJ + 2 * n + 1))
                A(kb[:, :], (q_s, k_s)[n][:, :], ACT.Square).then_inc(sq_ready, 1)

            def decay_exp(f):
                for n in range(G):
                    u = FU_D + n
                    act.wait_ge(front_filled[u % 2], f_filled(f, u))
                    A(dT[:, n * HG:(n + 1) * HG, :].rearrange("p h n -> p (h n)"), psF[u % 2][:, :], ACT.Exp).then_inc(front_evac[u % 2], 1)

            def copy_T(f, u0, dst):
                for n in range(G):
                    u = u0 + n
                    act.wait_ge(front_filled[u % 2], f_filled(f, u))
                    A(dst[:, n * HG:(n + 1) * HG, :], psF[u % 2][:, :].rearrange("p (h n) -> p h n", h=HG), ACT.Copy).then_inc(front_evac[u % 2], 1)

            def copy_x(t):
                for g in range(G):
                    act.wait_ge(inv_filled[0][g], 7 * t + 1)
                    A(xi[:, g * GW:(g + 1) * GW], psI[0][g][:, :], ACT.Copy).then_inc(x_ready[g], 1)

            def copy_y(t, l):
                for g in range(G):
                    act.wait_ge(inv_filled[1][g], 11 * t + 2 * l)
                    A(yi[:, g * GW:(g + 1) * GW], psI[1][g][:, :], ACT.Copy).then_inc(y_ready[g], 1)

            def evac(s, u, dst, func=ACT.Copy):
                act.wait_ge(back_filled[u % 2], b_filled(s, u))
                A(dst, psB[u % 2][:, 0:dst.shape[1]], func).then_inc(back_evac[u % 2], 1)

            def back(t, p):
                for g in range(G):
                    evac(t, BU_U + g, u_s[:, g * GW:(g + 1) * GW])
                act.wait_ge(sc_ready, t + 1)
                for g in range(G):
                    u = BU_QS + g
                    act.wait_ge(back_filled[u % 2], b_filled(t, u))
                    for h in range(HG):
                        c = g * HG + h
                        last = A(qsg[:, c * DK:(c + 1) * DK], psB[u % 2][:, h * DK:(h + 1) * DK], ACT.Copy, scale=sc[:, p, GAM + c:GAM + c + 1])
                    last.then_inc(back_evac[u % 2], 1)
                for g in range(G):
                    u = BU_PU + g
                    act.wait_ge(back_evac[u % 2], b_evac(t, u))
                    s = slice(g * GW, (g + 1) * GW)
                    A(r_s[:, s], o_s[:, s], ACT.Square).then_inc(so_ready, 1)

            def tail_o(t):
                for g in range(G):
                    evac(t + 1, BU_OT + g, oT[:, g * GW:(g + 1) * GW])

            def tail_m(t):
                evac(t + 1, BU_MT, mT[:, :])

            def tail_fc(t):
                for n in range(2):
                    evac(t + 1, BU_FC + n, hid[:, n * GW:(n + 1) * GW], ACT.Relu)

            def tail_x(t):
                evac(t + 1, BU_XT, xfT[:, :])

            def prepare(t):
                act.wait_ge(wst_stored, 48 * t + 48)
                for n in range(3):
                    evac(t, BU_PREP + n, wst[:, n])

            def step(t, p, more, tail):
                f, q = t + 1, 1 - p
                if more:
                    silu(f, 0, False)
                copy_x(t)
                if more:
                    silu(f, 1, False)
                for l in range(1, LEVELS):
                    if more and l <= 3:
                        silu(f, 2 * l, False)
                    if tail and l == 2:
                        tail_o(t - 1)
                    if more and l <= 3:
                        silu(f, 2 * l + 1, False)
                    if more and l <= 2:
                        square(f, l - 1)
                    if more and l == 4:
                        decay_exp(f)
                    if tail and l == 4:
                        tail_m(t - 1)
                    if more and l == 4:
                        copy_T(f, FU_K, kT)
                    if tail and l == 4:
                        tail_fc(t - 1)
                    if more and l == 5:
                        copy_T(f, FU_KB, kbqT[:, q, :, 0, :])
                        copy_T(f, FU_Q, kbqT[:, q, :, 1, :])
                    if l < LEVELS - 1:
                        copy_y(t, l)
                back(t, p)
                if tail:
                    tail_x(t - 1)
                prepare(t)

            for n in range(8):
                silu(0, n, True)
            act_decays_out(act)
            square(0, 0), square(0, 1)
            decay_exp(0)
            copy_T(0, FU_K, kT)
            copy_T(0, FU_KB, kbqT[:, 0, :, 0, :])
            copy_T(0, FU_Q, kbqT[:, 0, :, 1, :])
            step(0, 0, True, False)
            with act.Fori(0, PAIRS) as i:
                for p in range(2):
                    step(2 * i + p + 1, 1 - p, True, True)
            step(TILES - 1, 1, False, True)
            for part in (tail_o, tail_m, tail_fc, tail_x):
                part(TILES - 1)
            act_late(act)

        @block.vector
        def _(dve):
            V = nc.vector
            ch = Chain(dve, const_dve)
            dve.wait_ge(consts, 11)
            ch.link(V.tensor_tensor(iota_i[:, 0, :], iota_i[:, 0, :], iota_i[:, 1, :], ALU.bitwise_xor))
            ch.link(V.tensor_copy(xor[:, :], iota_i[:, 0, :]))
            wide = xi[:, 0:LEVELS * P].rearrange("p (l n) -> p l n", l=LEVELS)
            for l in range(LEVELS):
                ins = V.scalar_tensor_tensor(wide[:, l, :], xor[:, :], float(1 << l), lower[:, :], ALU.is_ge, ALU.mult)
            ch.link(ins)
            for l in range(LEVELS - 1):
                ins = V.tensor_tensor(left(level_mask[:, l, :], l, 1), left(wide[:, l, :], l), left(wide[:, l + 1, :], l), ALU.subtract)
            ins = V.tensor_copy(level_mask[:, l + 1, :], left(wide[:, l + 1, :], l + 1)[:, 0, :])
            ch.link(ins)
            ch.link(V.scalar_tensor_tensor(neg_m0t[:, :], xor[:, :], 1.0, upper[:, :], ALU.is_equal, ALU.mult))
            ch.link(V.tensor_scalar(neg_m0t[:, :], neg_m0t[:, :], -1.0, None, ALU.mult))

            def root(ch, v, r, a):
                ch.link(V.tensor_scalar(r.bitcast(I32), v.bitcast(I32), -0.5, ROOT_MAGIC, ALU.mult, ALU.add))
                for _ in range(3):
                    ch.link(V.scalar_tensor_tensor(a, r, -0.5, r, ALU.mult, ALU.mult))
                    ch.link(V.tensor_tensor(a, a, v, ALU.mult))
                    ch.link(V.scalar_tensor_tensor(r, a, 1.5, r, ALU.add, ALU.mult))

            for n in range(XPARTS):
                dve.wait_ge(x_loaded[n], 16)
                with dve.Fori(n * BATCH // XPARTS, (n + 1) * BATCH // XPARTS) as b:
                    ch = Chain(dve, pre_dve, 3 * b)
                    for c in range(CHUNKS):
                        ins = V.bn_stats(pbst4[:, c, :], x_all[:, bass.ds(CHUNKS * b + c, 1), :].rearrange("p t d -> p (t d)"))
                    ch.link(ins)
                    dve.sem_inc(dve_turn, 1)
                    for c in range(CHUNKS):
                        ins = V.bn_aggr(pmv4[:, c, :], pbst4[:, c, :])
                    ch.link(ins)
                    ch.link(V.tensor_copy(pmv[:, bass.ds(CHUNKS * b, CHUNKS), :], pmv4))
            ch = Chain(dve, pre_dve, 3 * BATCH)
            V.tensor_copy(dec[:, :, MEAN], pmv[:, :, 0])
            ch.link(V.tensor_scalar(pv, pmv[:, :, 1], LN_EPS, None, ALU.add))
            root(ch, pv, pr, pa)
            V.tensor_copy(dec[:, :, RINV], pr)
            ch.link(V.tensor_tensor(pms, pmv[:, :, 1], pr, ALU.mult))
            ch.link(V.tensor_tensor(pms, pms, pr, ALU.mult))
            ch.link(V.tensor_scalar(pms, pms, RMS_EPS, None, ALU.add))
            root(ch, pms, pr2, pa)
            ch.link(V.tensor_tensor(phs, pr, pr2, ALU.mult))
            n0 = 3 * BATCH + ch.n
            with dve.Fori(0, BATCH // 2) as i:
                for p in range(2):
                    b = 2 * i + p
                    V.tensor_copy(pmean4, pmv[:, bass.ds(CHUNKS * b, CHUNKS), 0])
                    Chain(dve, pre_dve, n0 + b).link(V.tensor_copy(phs4, phs[:, bass.ds(CHUNKS * b, CHUNKS)]))
                    dve.wait_ge(pre_tr, 2 * b + 2)
                    for c in range(CHUNKS):
                        ins = V.tensor_scalar(hb[p][:, c, :], x_all[:, bass.ds(CHUNKS * b + c, 1), :].rearrange("p t d -> p (t d)"), pmean4[:, c:c + 1], phs4[:, c:c + 1], ALU.subtract, ALU.mult)
                    ins.then_inc(pre_h, 1)
                    dve.wait_ge(pre_h, b + 1)
            dve_decays(dve)

            H3 = lambda a: a[:, :].rearrange("p (h d) -> p h d", h=H)

            def norm_sum(f, n):
                dve.wait_ge(sq_ready, 2 * f + n + 1)
                V.tensor_reduce(ss[:, n * H:(n + 1) * H], H3(kb), X, ALU.add).then_inc(ss_ready, 1)

            def norms(f):
                dve.wait_ge(rn_ready, f + 1)
                V.tensor_tensor(H3(k_s), H3(k_s), per_head(rn[:, H:2 * H]), ALU.mult).then_inc(kn_ready, 1)
                V.scalar_tensor_tensor(H3(q_s), H3(q_s), DK ** -0.5, per_head(rn[:, 0:H]), ALU.mult, ALU.mult).then_inc(qn_ready, 1)

            def delta_products(f, q, n):
                u = FU_KKQ + n
                if n % 2 == 0:
                    dve.wait_ge(dtm_ready, 2 * f + n // 2 + 1)
                dve.wait_ge(front_filled[u % 2], f_filled(f, u))
                d = dT[:, 2 * n:2 * n + 2, :].unsqueeze(2).to_broadcast([P, 2, 2, P])
                V.tensor_tensor(aP[:, q, 2 * n:2 * n + 2], psF[u % 2][:, :].rearrange("p (h a n) -> p h a n", h=2, a=2), d, ALU.mult).then_inc(front_evac[u % 2], 1)

            GV = lambda a, g: a[:, g * GW:(g + 1) * GW].rearrange("p (h n) -> p h n", h=HG)

            def inverse_start(t, p):
                dve.wait_ge(front_evac[0], f_evac(t, FU_KKQ + 2))
                dve.wait_ge(front_evac[1], f_evac(t, FU_KKQ + 3))
                for g in range(G):
                    ins = V.tensor_tensor(GV(yi, g), aP[:, p, g * HG:(g + 1) * HG, 0, :], over_heads(neg_m0t[:, :]), ALU.mult)
                Chain(dve, y0_dve, t).link(ins)
                for g in range(G):
                    V.tensor_tensor(GV(yi, g), GV(yi, g), over_heads(ident[:, :]), ALU.add).then_inc(y_ready[g], 1)

            HW = GW // 2
            half = lambda a, g: a[:, g * HW:(g + 1) * HW]

            def level_t(t, l):
                for g in range(G):
                    dve.wait_ge(inv_filled[0][g], 7 * t + l + 1)
                    V.tensor_tensor(half(ti, g).rearrange("p (h n) -> p h n", h=HG), psI[0][g][:, 0:HW].rearrange("p (h n) -> p h n", h=HG),
                                    over_heads(level_mask[:, l, :]), ALU.mult).then_inc(t_ready[g], 1)

            def level_x(t, l):
                for g in range(G):
                    dve.wait_ge(inv_filled[1][g], 11 * t + 2 * l - 1)
                    if l < LEVELS - 1:
                        a = left(xi[:, g * GW:(g + 1) * GW], l)
                        V.tensor_tensor(a, a, left(psI[1][g][:, 0:HW], l, 1), ALU.subtract).then_inc(x_ready[g], 1)
                    else:
                        a = GV(yi, g)[0:P // 2, :, P // 2:P]
                        V.tensor_tensor(a, a, psI[1][g][0:P // 2, 0:HW].rearrange("p (h n) -> p h n", h=HG), ALU.subtract).then_inc(y_ready[g], 1)

            def state_in(t, p):
                dve.wait_ge(vb_ready, t + 1)
                dve.wait_ge(sc_ready, t + 1)
                for g in range(G):
                    u = BU_KBS + g
                    dve.wait_ge(back_filled[u % 2], b_filled(t, u))
                    for h in range(HG):
                        c = g * HG + h
                        s = slice(c * DK, (c + 1) * DK)
                        ins = V.scalar_tensor_tensor(r_s[:, s], psB[u % 2][:, h * DK:(h + 1) * DK], sc[:, p, NGAM + c:NGAM + c + 1], vb[:, s], ALU.mult, ALU.add)
                    ins.then_inc(back_evac[u % 2], 1)

            def state_out(t, p):
                for g in range(G):
                    u = BU_PU + g
                    dve.wait_ge(back_evac[(BU_QS + g) % 2], b_evac(t, BU_QS + g))
                    dve.wait_ge(back_filled[u % 2], b_filled(t, u))
                    s = slice(g * GW, (g + 1) * GW)
                    V.tensor_tensor(o_s[:, s], qsg[:, s], psB[u % 2][:, :], ALU.add).then_inc(back_evac[u % 2], 1)
                for g in range(G):
                    u = BU_KDU + g
                    dve.wait_ge(back_filled[u % 2], b_filled(t, u))
                    for h in range(HG):
                        c = g * HG + h
                        s = slice(c * DK, (c + 1) * DK)
                        ins = V.scalar_tensor_tensor(state[:, s], state[:, s], sc[:, p, GTOT + c:GTOT + c + 1], psB[u % 2][:, h * DK:(h + 1) * DK], ALU.mult, ALU.add)
                    ins.then_inc(back_evac[u % 2], 1)

            def tail_xln(t):
                dve.wait_ge(msc_ready, t + 1)
                dve.wait_ge(xin_loaded, 16 * t + 16)
                V.tensor_scalar(xin[:, 1, :], xin[:, 0, :], msc[:, 0:1], msc[:, 1:2], ALU.subtract, ALU.mult).then_inc(xln_ready, 1)

            def square_sums(t, p):
                V.tensor_copy(msc[:, :], sc[:, p, MEAN:MEAN + 2]).then_inc(msc_ready, 1)
                dve.wait_ge(so_ready, 2 * t + 2)
                V.tensor_reduce(os_[:, 0, :], H3(r_s), X, ALU.add).then_inc(os_ready, 1)

            def tail_o(t):
                dve.wait_ge(or_ready, t + 1)
                dve.wait_ge(gw_ready, t + 1)
                for h in range(H):
                    s = slice(h * DK, (h + 1) * DK)
                    ins = V.scalar_tensor_tensor(o_s[:, s], o_s[:, s], or_[:, 0, h:h + 1], gw[:, s], ALU.mult, ALU.mult)
                ins.then_inc(og_ready, 1)

            def tail_x2(t):
                dve.wait_ge(xln_ready, t + 1)
                b = BU_WO % 2
                dve.wait_ge(back_filled[b], b_filled(t + 1, BU_WO))
                V.tensor_tensor(x2[:, :], xin[:, 1, :], psB[b][:, 0:D], ALU.add).then_inc(back_evac[b], 1)
                dve.wait_ge(back_evac[b], b_evac(t + 1, BU_WO))
                V.tensor_tensor_reduce(out=m_s[:, :], in0=x2[:, :], in1=x2[:, :], scale=1.0, scalar=0.0, op0=ALU.mult, op1=ALU.add,
                                       accum_out=mrow_v[:, 0:1]).then_inc(mv_ready, 1)

            def tail_m(t):
                dve.wait_ge(mr_ready, t + 1)
                V.tensor_scalar(m_s[:, :], x2[:, :], mrow_r[:, 0:1], None, ALU.mult).then_inc(m_ready, 1)

            def tail_fc(t):
                for n in range(2):
                    u = BU_FC + n
                    dve.wait_ge(back_evac[u % 2], b_evac(t + 1, u))
                    s = slice(n * GW, (n + 1) * GW)
                    V.tensor_tensor(hid[:, s], hid[:, s], hid[:, s], ALU.mult).then_inc(hid_ready, 1)

            def tail_x1(t):
                b = BU_PROJ % 2
                dve.wait_ge(x1_stored, 16 * t + 16)
                dve.wait_ge(back_filled[b], b_filled(t + 1, BU_PROJ))
                V.tensor_tensor(x1[:, :], x2[:, :], psB[b][:, 0:D], ALU.add).then_inc(back_evac[b], 1)
                dve.wait_ge(back_evac[b], b_evac(t + 1, BU_PROJ))
                V.tensor_tensor(x1[:, :], x1[:, :], xin[:, 0, :], ALU.add).then_inc(x1_ready, 1)
                dve.wait_ge(x1_ready, t + 1)
                Chain(dve, tail_dve, t).link(V.bn_stats(bst[:, :], x1[:, :]))
                dve.sem_inc(dve_turn, 1)
                V.bn_aggr(bag[:, :], bst[:, :]).then_inc(xv_ready, 1)

            def tail_xf(t):
                dve.wait_ge(xr_ready, t + 1)
                dve.wait_ge(xf_stored, 16 * t + 16)
                V.tensor_scalar(xf[:, :], x1[:, :], bag[:, 0:1], xrow_r[:, 0:1], ALU.subtract, ALU.mult).then_inc(xf_ready, 1)

            def tail_logits(t):
                b = BU_LG % 2
                dve.wait_ge(back_filled[b], b_filled(t + 1, BU_LG))
                V.tensor_scalar(la[:, bass.ds(t, 1), :], psB[b][:, 0:E].unsqueeze(1), -1.0 / EPSILON, None, ALU.mult).then_inc(back_evac[b], 1)

            def step(t, p, more, tail):
                f, q = t + 1, 1 - p
                for l in range(1, LEVELS):
                    level_t(t, l)
                    if tail and l == 3:
                        tail_x2(t - 1)
                    if more and l in (2, 3):
                        norm_sum(f, l - 2)
                    if more and l == 4:
                        norms(f)
                    if tail and l == 5:
                        tail_fc(t - 1)
                    if more and l == 6:
                        delta_products(f, q, 0), delta_products(f, q, 1)
                    level_x(t, l)
                    if tail and l == 1:
                        tail_o(t - 1)
                        tail_xln(t - 1)
                    if tail and l == 3:
                        tail_m(t - 1)
                    if l == 5:
                        state_in(t, p)
                        if tail:
                            tail_x1(t - 1)
                if more:
                    delta_products(f, q, 2), delta_products(f, q, 3)
                    for g in range(G):
                        u = BU_U + g
                        dve.wait_ge(back_filled[u % 2], b_filled(t, u))
                    inverse_start(f, q)
                if tail:
                    tail_xf(t - 1)
                state_out(t, p)
                square_sums(t, p)
                if tail:
                    tail_logits(t - 1)

            norm_sum(0, 0), norm_sum(0, 1)
            norms(0)
            for n in range(4):
                delta_products(0, 0, n)
            inverse_start(0, 0)
            step(0, 0, True, False)
            with dve.Fori(0, PAIRS) as i:
                for p in range(2):
                    step(2 * i + p + 1, 1 - p, True, True)
            step(TILES - 1, 1, False, True)
            for part in (tail_o, tail_xln, tail_x2, tail_m, tail_fc, tail_x1, tail_xf, tail_logits):
                part(TILES - 1)
            dve_late(dve)

        @block.tensor
        def _(pe):
            MM = nc.tensor.matmul
            pe.wait_ge(const_dve, 6)
            pe.wait_ge(wba_loaded, 16 * 2)
            def pre_transposes(b, p):
                pe.wait_ge(pre_h, b + 1)
                for n in range(2):
                    for c in range(2):
                        for k in range(KD):
                            j = (c * KD + k) * P
                            last = nc.tensor.transpose(pre_ps[p % 2][n][:, j:j + P], hb[p % 2][:, 2 * n + c, k * P:(k + 1) * P], ident[:, :])
                    last.then_inc(pre_tr, 1)

            def pre_small(b, p):
                pe.wait_ge(pre_hT, 2 * b + 2)
                pe.wait_ge(ba_ready, b + 1)
                for c in range(CHUNKS):
                    for k in range(KD):
                        last = MM(psB[p % 2][:, c * 2 * H:(c + 1) * 2 * H], hTb[p][:, c, k, :], wba[:, k, :], start=k == 0, stop=k == KD - 1)
                last.then_inc(pre_ba, 1)

            with pe.Fori(0, BATCH // NB) as i:
                for p in range(NB + 1):
                    if p < NB:
                        pre_transposes(NB * i + p, p)
                    if p > 0:
                        pre_small(NB * i + p - 1, p - 1)

            def front_bank(f, u):
                pe.wait_ge(front_evac[u % 2], f_evac(f, u) - 1)
                return psF[u % 2], front_filled[u % 2]

            def back_bank(t, u):
                pe.wait_ge(back_evac[u % 2], b_evac(t, u) - 1)
                return psB[u % 2], back_filled[u % 2]

            def project(f, q, n):
                ps, filled = front_bank(f, FU_PROJ + n)
                for k in range(KD):
                    last = MM(ps[:, :], hT[:, q, k, :], wqkvg[:, n // 2, k, n % 2 * GW:(n % 2 + 1) * GW], start=k == 0, stop=k == KD - 1)
                last.then_inc(filled, 1)

            def decay_sums(f, n):
                ps, filled = front_bank(f, FU_D + n)
                MM(ps[:, :], lower[:, :], dT[:, n * HG:(n + 1) * HG, :].rearrange("p h n -> p (h n)"), start=True, stop=True).then_inc(filled, 1)

            def transposes(f, u0, src):
                for n in range(G):
                    ps, filled = front_bank(f, u0 + n)
                    for h in range(HG):
                        c = n * HG + h
                        last = nc.tensor.transpose(ps[:, h * P:(h + 1) * P], src[:, c * DK:(c + 1) * DK], ident[:, :])
                    last.then_inc(filled, 1)

            def delta_products(f, q, n):
                ps, filled = front_bank(f, FU_KKQ + n)
                for h in range(2):
                    c = 2 * n + h
                    last = MM(ps[:, h * 2 * P:(h + 1) * 2 * P], kT[:, c, :], kbqT[:, q, c].rearrange("p a n -> p (a n)"), start=True, stop=True)
                last.then_inc(filled, 1)

            cols = lambda a, c: a[:, c * DK:(c + 1) * DK]
            HP = P // 2

            def start_x(t):
                for g in range(G):
                    pe.wait_ge(y_ready[g], 7 * t + 1)
                    for h in range(HG):
                        last = nc.tensor.transpose(psI[0][g][:, h * P:(h + 1) * P], cols(yi, g * HG + h), ident[:, :])
                    last.then_inc(inv_filled[0][g], 1)

            def level_t(t, p, l):
                for g in range(G):
                    pe.wait_ge(x_ready[g], 6 * t + l)
                    for h in range(HG):
                        last = MM(left(psI[0][g][:, h * HP:(h + 1) * HP], l, 1), aP[:, p, g * HG + h, 0, :], left(cols(xi, g * HG + h), l), start=True, stop=True)
                    last.then_inc(inv_filled[0][g], 1)

            def level_x(t, l):
                for g in range(G):
                    pe.wait_ge(t_ready[g], 6 * t + l)
                    pe.wait_ge(y_ready[g], 7 * t + l)
                    for h in range(HG):
                        c = g * HG + h
                        tm, out_ = ti[:, c * HP:(c + 1) * HP], psI[1][g][:, h * HP:(h + 1) * HP]
                        if l < LEVELS - 1:
                            last = MM(out_, cols(yi, c), tm, start=True, stop=True)
                        else:
                            last = MM(out_[0:HP, :], tm, cols(yi, c)[:, HP:P], start=True, stop=True)
                    last.then_inc(inv_filled[1][g], 1)

            def level_y(t, l):
                for g in range(G):
                    pe.wait_ge(x_ready[g], 6 * t + l + 1)
                    for h in range(HG):
                        last = nc.tensor.transpose(psI[1][g][:, h * P:(h + 1) * P], cols(xi, g * HG + h), ident[:, :])
                    last.then_inc(inv_filled[1][g], 1)

            def heads(t, u, g, left, right):
                ps, filled = back_bank(t, u)
                for h in range(HG):
                    last = MM(ps[:, h * DK:(h + 1) * DK], left(g * HG + h), right(g * HG + h), start=True, stop=True)
                last.then_inc(filled, 1)

            def state_in(t, p):
                for g in range(G):
                    heads(t, BU_KBS + g, g, lambda c: kbqT[:, p, c, 0, :], lambda c: cols(state, c))

            def state_u(t, p):
                for g in range(G):
                    pe.wait_ge(y_ready[g], 7 * t + 7)
                    if g == 0:
                        pe.wait_ge(back_evac[BU_KBS % 2], b_evac(t, BU_KBS))
                    heads(t, BU_U + g, g, lambda c: cols(yi, c), lambda c: cols(r_s, c))

            def state_out(t, p):
                for g in range(G):
                    heads(t, BU_QS + g, g, lambda c: kbqT[:, p, c, 1, :], lambda c: cols(state, c))
                for g in range(G):
                    heads(t, BU_PU + g, g, lambda c: aP[:, p, c, 1, :], lambda c: cols(u_s, c))
                pe.wait_ge(kd_ready, t + 1)
                for g in range(G):
                    heads(t, BU_KDU + g, g, lambda c: cols(kd, c), lambda c: cols(u_s, c))

            def prepare(t):
                pe.wait_ge(wnat_loaded, 48 * t + 48)
                for n in range(3):
                    ps, filled = back_bank(t, BU_PREP + n)
                    for a in range(2):
                        for b in range(2):
                            j = (b * 2 + a) * P
                            last = nc.tensor.transpose(ps[:, j:j + P], wnat[:, n, a * D + b * P:a * D + (b + 1) * P], ident[:, :])
                    last.then_inc(filled, 1)

            def tail_o(t):
                pe.wait_ge(og_ready, t + 1)
                for g in range(G):
                    ps, filled = back_bank(t + 1, BU_OT + g)
                    for h in range(HG):
                        last = nc.tensor.transpose(ps[:, h * P:(h + 1) * P], cols(o_s, g * HG + h), ident[:, :])
                    last.then_inc(filled, 1)

            def tail_wo(t):
                ps, filled = back_bank(t + 1, BU_WO)
                for h in range(H):
                    if h == HG:
                        pe.wait_ge(back_evac[(BU_OT + 1) % 2], b_evac(t + 1, BU_OT + 1))
                    last = MM(ps[:, 0:D], cols(oT, h), wo[:, h, :], start=h == 0, stop=h == H - 1)
                last.then_inc(filled, 1)

            def tail_m(t):
                pe.wait_ge(m_ready, t + 1)
                ps, filled = back_bank(t + 1, BU_MT)
                for k in range(KD):
                    last = nc.tensor.transpose(ps[:, k * P:(k + 1) * P], m_s[:, k * P:(k + 1) * P], ident[:, :])
                last.then_inc(filled, 1)

            def tail_fc(t):
                pe.wait_ge(back_evac[BU_MT % 2], b_evac(t + 1, BU_MT))
                for n in range(2):
                    ps, filled = back_bank(t + 1, BU_FC + n)
                    for fb in range(FB // 2):
                        for k in range(KD):
                            c = (n * (FB // 2) + fb) * P
                            last = MM(ps[:, fb * P:(fb + 1) * P], wfc[:, k, c:c + P], mT[:, k * P:(k + 1) * P], start=k == 0, stop=k == KD - 1)
                    last.then_inc(filled, 1)

            def tail_proj(t):
                ps, filled = back_bank(t + 1, BU_PROJ)
                for fb in range(FB):
                    if fb % (FB // 2) == 0:
                        pe.wait_ge(hid_ready, 2 * t + fb // (FB // 2) + 1)
                    last = MM(ps[:, 0:D], hid[:, fb * P:(fb + 1) * P], wproj[:, fb, :], start=fb == 0, stop=fb == FB - 1)
                last.then_inc(filled, 1)

            def tail_logits(t):
                pe.wait_ge(xf_ready, t + 1)
                ps, filled = back_bank(t + 1, BU_XT)
                for k in range(KD):
                    last = nc.tensor.transpose(ps[:, k * P:(k + 1) * P], xf[:, k * P:(k + 1) * P], ident[:, :])
                last.then_inc(filled, 1)
                pe.wait_ge(back_evac[BU_XT % 2], b_evac(t + 1, BU_XT))
                ps, filled = back_bank(t + 1, BU_LG)
                for k in range(KD):
                    last = MM(ps[:, 0:E], xfT[:, k * P:(k + 1) * P], gwT[:, k, :], start=k == 0, stop=k == KD - 1)
                last.then_inc(filled, 1)

            def front_k(f):
                pe.wait_ge(kn_ready, f + 1)
                transposes(f, FU_K, k_s)

            def front_kb(f):
                pe.wait_ge(kb_ready, f + 1)
                transposes(f, FU_KB, kb)

            def front_q(f):
                pe.wait_ge(qn_ready, f + 1)
                transposes(f, FU_Q, q_s)

            def step(t, p, more, tail, turn):
                f, q = t + 1, 1 - p
                if more:
                    pe.wait_ge(hT_loaded[q], 16 * turn + 16)
                    project(f, q, 0), project(f, q, 1)
                for l in range(1, LEVELS):
                    level_t(t, p, l)
                    if more and l <= 3:
                        project(f, q, 2 * l)
                    if tail and l == 2:
                        tail_o(t - 1)
                    if more and l == 4:
                        pe.wait_ge(rhs_ready, f + 1)
                        decay_sums(f, 0), decay_sums(f, 1)
                    if tail and l == 4:
                        tail_m(t - 1)
                    if more and l == 5:
                        front_kb(f)
                    if l == 5:
                        state_in(t, p)
                    if more and l == 6:
                        delta_products(f, q, 0), delta_products(f, q, 1)
                    level_x(t, l)
                    if more and l <= 3:
                        project(f, q, 2 * l + 1)
                    if tail and l == 2:
                        tail_wo(t - 1)
                    if more and l == 4:
                        front_k(f)
                    if tail and l == 4:
                        tail_fc(t - 1)
                    if more and l == 5:
                        front_q(f)
                    if tail and l == 5:
                        tail_proj(t - 1)
                    if l < LEVELS - 1:
                        level_y(t, l)
                if more:
                    delta_products(f, q, 2), delta_products(f, q, 3)
                state_u(t, p)
                state_out(t, p)
                if tail:
                    tail_logits(t - 1)
                prepare(t)
                if more:
                    start_x(t + 1)

            pe.wait_ge(w_loaded, 16 * 4)
            pe.wait_ge(hT_loaded[0], 16)
            for n in range(8):
                project(0, 0, n)
            pe_decays(pe)
            pe.wait_ge(rhs_ready, 1)
            decay_sums(0, 0), decay_sums(0, 1)
            front_k(0)
            front_kb(0)
            front_q(0)
            for n in range(4):
                delta_products(0, 0, n)
            start_x(0)
            step(0, 0, True, False, 0)
            pe.wait_ge(w_loaded, 16 * 7)
            pe.wait_ge(gate_loaded, 16 * 2)
            with pe.Fori(0, PAIRS) as i:
                for p in range(2):
                    step(2 * i + p + 1, 1 - p, True, True, i + 1)
            step(TILES - 1, 1, False, True, 0)
            for part in (tail_o, tail_wo, tail_m, tail_fc, tail_proj, tail_logits):
                part(TILES - 1)
            pe_late(pe)


_INS = ["L0_attn_x", "L0_attn_Wq", "L0_attn_Wk", "L0_attn_Wv", "L0_attn_Wb", "L0_attn_Wa", "L0_attn_A_log",
        "L0_attn_dt_bias", "L0_attn_Wg", "L0_attn_o_norm_w", "L0_attn_Wo", "L0_attn_W_fc", "L0_attn_W_proj",
        "L0_ffn_gate_W", "L0_ffn_W_gate", "L0_ffn_W_up", "L0_ffn_W_down"]


def kernel(**inputs):
    import concourse.bacc as _bacc
    from concourse.bass_utils import run_bass_kernel_spmd as _run

    nc = _bacc.Bacc("TRN2", target_bir_lowering=False, num_devices=1)
    arrays, args = {}, []
    for name in _INS:
        a = np.ascontiguousarray(inputs[name])
        arrays[f"{name}_dram"] = a
        args.append(nc.dram_tensor(f"{name}_dram", a.shape, mybir.dt.from_np(a.dtype), kind="ExternalInput").ap())
    o = nc.dram_tensor("out_dram", (BATCH, SEQ, D), F32, kind="ExternalOutput").ap()
    program(nc, *args, o)
    r = _run(nc, [arrays], core_ids=[0])
    return r.results[0]["out_dram"]
```

```python
from contextlib import ExitStack

import numpy as np
import concourse.bass as bass
from concourse import mybir

F32 = mybir.dt.float32
F32R = mybir.dt.float32r
I32 = mybir.dt.int32
ALU = mybir.AluOpType
ACT = mybir.ActivationFunctionType
X = mybir.AxisListType.X

P = 128
BATCH, SEQ, D = 8, 512, 256
H, DK, F = 8, 128, 1024
E, TOPK, ROUNDS, EPSILON = 8, 2, 20, 0.05
KD = D // P
CHUNKS = SEQ // P
TILES = BATCH * CHUNKS
PAIRS = TILES // 2 - 1
TOKENS = BATCH * SEQ
HD = H * DK
G = 2
HG = H // G
GW = HG * DK
LEVELS = 7
FB = F // P
WCOLS = 3 * KD * F
ROWS = 256
RB = ROWS // P
ETILES = (TOKENS * TOPK + E * (ROWS - 1)) // ROWS
MAXT = TOKENS // ROWS
XPARTS = 4
LN_EPS, RMS_EPS = 1e-5, 1e-6
DEAD = 110.0
ROUND = 1.5 * 2 ** 23
EXP_ZERO = -87.33654
ROOT_MAGIC = 1597463007.0

BETA, GAM, NGAM, GTOT, DEND, GLOG, MEAN = (8 * n for n in range(7))
RINV = MEAN + 1
NSC = MEAN + 2

FU_PROJ, FU_D, FU_K, FU_KB, FU_Q, FU_KKQ, FU = 0, 8, 10, 12, 14, 16, 20
(BU_OT, BU_WO, BU_MT, BU_FC, BU_KBS, BU_PROJ, BU_QS, BU_U, BU_PU, BU_KDU, BU_XT, BU_LG, BU) = (
    0, 2, 3, 4, 6, 8, 9, 11, 13, 15, 17, 18, 19)
TAIL_USES = (0, 1, 2, 3, 4, 5, 8, BU_XT, BU_LG)
STATE_USES = tuple(u for u in range(BU) if u not in TAIL_USES)


class Chain:

    def __init__(self, eng, sem, base=0):
        self.eng, self.sem, self.base, self.n = eng, sem, base, 0

    def link(self, ins):
        self.n += 1
        ins.then_inc(self.sem, 1)
        self.eng.wait_ge(self.sem, self.base + self.n)


def over_heads(m, n=HG):
    return m.unsqueeze(1).to_broadcast([m.shape[0], n, m.shape[1]])


def left(a, l, halves=2):
    w = 1 << l
    return a.rearrange("p (b s) -> p b s", s=halves * w)[:, :, 0:w]


def per_head(s, k=DK):
    return s.unsqueeze(2).to_broadcast([s.shape[0], s.shape[1], k])


def program(nc, x, Wq, Wk, Wv, Wb, Wa, A_log, dt_bias, Wg, o_norm_w, Wo, W_fc, W_proj,
            gate_W, W_gate, W_up, W_down, out):
    x_tiles = x.rearrange("b (c p) d -> (b c) p d", p=P)
    out_tiles = out.rearrange("b (c p) d -> (b c) p d", p=P)
    hT_d = nc.dram_tensor("hT_d", [TILES, P, D], F32)
    x1_d = nc.dram_tensor("x1_d", [TILES, P, D], F32)
    xf_d = nc.dram_tensor("xf_d", [TILES, P, D], F32)
    wts_d = nc.dram_tensor("wts_d", [E, P, WCOLS], F32)
    ys_d = nc.dram_tensor("ys_d", [ETILES * ROWS, D], F32)

    with ExitStack() as ctx:
        def sb(name, shape, dt=F32):
            return ctx.enter_context(nc.sbuf_tensor(name, shape, dt))

        def sem(name):
            return ctx.enter_context(nc.semaphore(name))

        ident = sb("ident", [P, P])
        ones = sb("ones", [P, P])
        incl = sb("incl", [P, P])
        upper = sb("upper", [P, P])
        lower = sb("lower", [P, P])
        xor = sb("xor", [P, P])
        iota_i = sb("iota_i", [P, 2, P], I32)
        level_mask = sb("level_mask", [P, LEVELS, P // 2])
        neg_m0t = sb("neg_m0t", [P, P])
        tile_iota = sb("tile_iota", [1, ETILES])
        thresholds = sb("thresholds", [P, MAXT])
        rank_w = sb("rank_w", [P, E])
        wba = sb("wba", [P, KD, 2 * H])
        gwT = sb("gwT", [P, KD, E])
        onorm = sb("onorm", [P, DK])
        alog = sb("alog", [P, H])
        dtb = sb("dtb", [P, H])
        dec = sb("dec", [P, TILES, NSC])
        la = sb("la", [P, TILES, E])
        sc = sb("sc", [P, 2, NSC])
        msc = sb("msc", [P, 2])
        ss = sb("ss", [P, 2 * H])
        nv = sb("nv", [P, 2 * H])
        na = sb("na", [P, 2 * H])
        rn = sb("rn", [P, 2 * H])
        bst = sb("bst", [P, 6])
        bag = sb("bag", [P, 2])
        xrow_v = sb("xrow_v", [P, 2])
        xrow_r = sb("xrow_r", [P, 2])
        mrow_v = sb("mrow_v", [P, 2])
        mrow_r = sb("mrow_r", [P, 2])
        os_ = sb("os", [P, 2, H])
        or_ = sb("or", [P, 2, H])

        pi_t = sb("pi_t", [P, TILES * E])
        posi = sb("posi", [P, TILES, TOPK], I32)
        te_i = sb("te_i", [1, ETILES], I32)
        pidx = sb("pidx", [P, 2, CHUNKS, TOPK], I32)
        list_i = sb("list_i", [P, ETILES * RB], I32)
        ridx = sb("ridx", [P, 2, RB], I32)
        pw = sb("pw", [P, 2, CHUNKS, TOPK])
        with nc.sbuf_tensor("x_all", [P, TILES, D], F32) as x_all:
            pass
        attention = ExitStack()

        def at(name, shape):
            return attention.enter_context(nc.sbuf_tensor(name, shape, F32))

        kbqT = at("kbqT", [P, 2, H, 2, P])
        aP = at("aP", [P, 2, H, 2, P])
        weights = at("weights", [P, 5 * KD * HD])
        wvg_hi, wvg_lo = (at(n, [P, 2, KD, HD]) for n in ("wvg_hi", "wvg_lo"))
        hT_hi, hT_lo = (at(n, [P, KD, P]) for n in ("hT_hi", "hT_lo"))
        kT = at("kT", [P, H, P])
        dT = at("dT", [P, H, P])
        kd, vb, kb, v_s, g_s = (at(n, [P, HD]) for n in ("kd", "vb", "kb", "v_s", "g_s"))
        hT = at("hT", [P, 2, KD, P])
        xin = at("xin", [P, 2, D])
        x2, m_s, mT, x1, xf, xfT = (at(n, [P, D]) for n in ("x2", "m_s", "mT", "x1", "xf", "xfT"))
        q_s, k_s = (at(n, [P, HD]) for n in ("q_s", "k_s"))
        xi, yi, state, r_s, u_s, qsg, o_s, oT, gw = (at(n, [P, HD]) for n in ("xi", "yi", "state", "r_s", "u_s", "qsg", "o_s", "oT", "gw"))
        ti = at("ti", [P, HD // 2])
        wqk = weights[:, 0:2 * KD * HD].rearrange("p (w k n) -> p w k n", w=2, k=KD)
        wo = weights[:, 2 * KD * HD:3 * KD * HD].rearrange("p (h n) -> p h n", h=H)
        wfc = weights[:, 3 * KD * HD:4 * KD * HD].rearrange("p (k n) -> p k n", k=KD)
        wproj = weights[:, 4 * KD * HD:5 * KD * HD].rearrange("p (f n) -> p f n", f=FB)
        wvg_raw = [k_s[:, :], kT[:, :, :].rearrange("p h n -> p (h n)"), gw[:, :], dT[:, :, :].rearrange("p h n -> p (h n)")]
        ba = oT[:, HD // 2:HD].rearrange("p (t n) -> p t n", t=TILES)
        hid = oT
        attention.close()

        psI = [[ctx.enter_context(nc.psum_tensor(f"ps_inv{n}{g}", [P, GW], F32)) for g in range(G)] for n in "ab"]
        psF = [ctx.enter_context(nc.psum_tensor(f"ps_front{n}", [P, GW], F32)) for n in range(2)]
        psB = [ctx.enter_context(nc.psum_tensor(f"ps_back{n}", [P, GW], F32)) for n in range(2)]

        w_loaded, tail_loaded = sem("w_loaded"), sem("tail_loaded")
        vg_loaded, vg_hi_ready, vg_split = sem("vg_loaded"), sem("vg_hi_ready"), sem("vg_split")
        h_hi_ready, h_split = sem("h_hi_ready"), sem("h_split")
        small_loaded = sem("small_loaded")
        consts = sem("consts")
        const_dve = sem("const_dve")
        x_loaded = [sem(f"x_loaded{n}") for n in range(XPARTS)]
        pre_dve, pre_h = sem("pre_dve"), sem("pre_h")
        pre_tr, pre_hT, pre_ba, ba_ready = (sem(n) for n in ("pre_tr", "pre_hT", "pre_ba", "ba_ready"))
        hT_stored = [sem(f"hT_stored{n}") for n in range(4)]
        wba_loaded, gate_loaded = sem("wba_loaded"), sem("gate_loaded")
        msc_ready, xln_ready = sem("msc_ready"), sem("xln_ready")
        dec_dve, dec_act, dec_pe = sem("dec_dve"), sem("dec_act"), sem("dec_pe")
        dec_ready = sem("dec_ready")
        hT_loaded = [sem("hT_loaded0"), sem("hT_loaded1")]
        front_filled = [sem("front_filled0"), sem("front_filled1")]
        front_evac = [sem("front_evac0"), sem("front_evac1")]
        sq_ready = sem("sq_ready")
        sc_ready, rhs_ready, ss_ready, rn_ready = (sem(n) for n in ("sc_ready", "rhs_ready", "ss_ready", "rn_ready"))
        norm_pool = sem("norm_pool")
        kn_ready, qn_ready, kb_ready, dtm_ready = (sem(n) for n in ("kn_ready", "qn_ready", "kb_ready", "dtm_ready"))
        vb_ready, kd_ready, gw_ready = (sem(n) for n in ("vb_ready", "kd_ready", "gw_ready"))
        inv_filled = [[sem(f"inv_{n}_filled{g}") for g in range(G)] for n in "ab"]
        x_ready = [sem(f"x_ready{g}") for g in range(G)]
        y_ready = [sem(f"y_ready{g}") for g in range(G)]
        t_ready = [sem(f"t_ready{g}") for g in range(G)]
        y0_pool = sem("y0_pool")
        back_filled = [sem("back_filled0"), sem("back_filled1")]
        back_evac = [sem("back_evac0"), sem("back_evac1")]
        xin_loaded = sem("xin_loaded")
        x1_stored, xf_stored = sem("x1_stored"), sem("xf_stored")
        hid_ready = sem("hid_ready")
        tail_dve, m_pool, x_pool, o_pool = (sem(n) for n in ("tail_dve", "m_pool", "x_pool", "o_pool"))
        so_ready, os_ready, or_ready, og_ready = (sem(n) for n in ("so_ready", "os_ready", "or_ready", "og_ready"))
        mv_ready, mr_ready, m_ready = (sem(n) for n in ("mv_ready", "mr_ready", "m_ready"))
        x1_ready, xv_ready, xr_ready, xf_ready = (sem(n) for n in ("x1_ready", "xv_ready", "xr_ready", "xf_ready"))

        def f_filled(f, u):
            return FU // 2 * f + u // 2 + 1

        def f_evac(f, u):
            return FU // 2 * f + u // 2 + 2

        def b_filled(s, u):
            before = lambda uses, last: sum(1 for n in uses if n % 2 == u % 2 and n <= last)
            if isinstance(s, int) and s == 0:
                return before(STATE_USES, u)
            inner = before(STATE_USES, BU) + before(range(BU), BU) * (s - 1)
            return inner + (before(TAIL_USES, u) if isinstance(s, int) and s == TILES else u // 2 + 1)

        def b_evac(s, u):
            return b_filled(s, u) + 1

        N_NORM, N_ROW, N_O = 13, 8, 13

        hb = [a[:, :].rearrange("p (c d) -> p c d", c=CHUNKS) for a in (v_s, g_s)]
        hTb = [a[:, :].rearrange("p (c k n) -> p c k n", c=CHUNKS, k=KD) for a in (kb, kd, vb, q_s)]
        NB = len(hTb)
        pbst4 = yi[:, 0:6 * CHUNKS].rearrange("p (t n) -> p t n", t=CHUNKS)
        pmv4 = yi[:, 64:64 + 2 * CHUNKS].rearrange("p (t n) -> p t n", t=CHUNKS)
        pmv = yi[:, 256:256 + 2 * TILES].rearrange("p (t n) -> p t n", t=TILES)
        pv, pr, pa, pms, pr2, phs = (r_s[:, n * TILES:(n + 1) * TILES] for n in range(6))
        pmean4, phs4 = r_s[:, 256:256 + CHUNKS], r_s[:, 260:260 + CHUNKS]
        pre_ps = psI

        V3 = lambda a: a.rearrange("p (t e) -> p t e", e=E)
        by_expert = lambda a: a.rearrange("p t e -> p e t")
        over_tiles = lambda s: s.unsqueeze(1).to_broadcast([P, TILES, E])
        TE = TILES * E
        z_b, az_b, tt_b, s_b, s2_b, p_b, den_b = (V3(a[:, 0:TE]) for a in (xi, yi, ti, r_s, u_s, qsg, o_s))
        al1, al2, e1, e2 = (oT[:, n * H:(n + 1) * H] for n in range(4))
        sd, se, pi = V3(xi[:, 0:TE]), V3(yi[:, 0:TE]), V3(pi_t[:, :])
        rowm, rows_, rowl = (r_s[:, n * TILES:(n + 1) * TILES] for n in range(3))
        colm, cmx, cdiag, cols_, coll = r_s[:, 96:104], r_s[0:E, 104:105], r_s[0:E, 112:120], r_s[:, 120:128], r_s[:, 128:136]
        cand, hot, hot2, both = (V3(a[:, 0:TE]) for a in (u_s, qsg, o_s, gw))
        cnt = [V3(hid[:, n * TE:(n + 1) * TE]) for n in range(2)]
        posf = V3(hid[:, 2 * TE:3 * TE])
        need3 = hid[:, 3 * TE:3 * TE + E * MAXT].rearrange("p (e n) -> p e n", e=E)
        need = [r_s[:, 136 + 8 * n:144 + 8 * n] for n in range(4)]
        posk = r_s[:, 256:256 + TILES * TOPK].rearrange("p (t k) -> p t k", k=TOPK)
        tef = r_s[0:1, 384:384 + ETILES]
        PAIRS_B = CHUNKS * TOPK
        pos_col, pos_lane = (r_s[:, n:n + TILES * TOPK] for n in (448, 512))
        lane_hot = [a[:, :].rearrange("p (n l) -> p n l", n=PAIRS_B) for a in (kd, vb)]
        col_hot = [a[:, 0:PAIRS_B * ETILES * RB].rearrange("p (n l) -> p n l", n=PAIRS_B) for a in (kb, v_s)]
        numbers = g_s[:, 0:P]
        tokens = g_s[:, P:P + TILES * TOPK]
        xf_rows = xf_d.rearrange("t p d -> (t p) d")
        te3 = u_s[0:1, 512:512 + ETILES * E].rearrange("p (j e) -> p j e", e=E)
        sk_dve, sk_act, sk_pe = sem("sinkhorn_dve"), sem("sinkhorn_act"), sem("sinkhorn_pe")
        rt_dve, rt_pe, pi_ready = sem("routing_dve"), sem("routing_pe"), sem("pi_ready")
        te_ready, pos_ready = sem("te_ready"), sem("pos_ready")
        pidx_ready = sem("pidx_ready")
        tables_made, pairs_dve, pairs_ready, pairs_used = (sem(n) for n in ("tables_made", "pairs_dve", "pairs_ready", "pairs_used"))
        list_ready, ridx_ready = sem("list_ready"), sem("ridx_ready")
        pool_turn, sp_turn, dve_turn = sem("pool_turn"), sem("sp_turn"), sem("dve_turn")
        QN = E * CHUNKS
        wnat, wst = (weights[:, n * 6 * 2 * D:(n + 1) * 6 * 2 * D].rearrange("p (q w n) -> p q w n", q=2, w=3) for n in range(2))
        wt_banks = (psI[0][0], psI[0][1], psI[1][0])
        wnat_loaded = [sem("wnat_loaded0"), sem("wnat_loaded1")]
        wst_stored = [sem("wst_stored0"), sem("wst_stored1")]
        wt_filled, wst_ready = sem("wt_filled"), sem("wst_ready")
        NPAIR = ETILES // 2
        w_raw = sb("w_raw", [P, 3, KD * F])
        w_hi, w_lo = ([sb(f"w_{n}{p}", [P, 3, KD * F]) for p in range(2)] for n in ("hi", "lo"))
        eh_hi, eh_lo = ([sb(f"eh_{n}{p}", [P, FB, ROWS]) for p in range(2)] for n in ("hi", "lo"))
        eh = sb("eh", [P, 4, ROWS])
        sact = sb("sact", [P, 4, ROWS])
        xT_hi, xT_lo = ([sb(f"xT_{n}{p}", [P, KD, ROWS]) for p in range(2)] for n in ("hi", "lo"))
        xrow = [sb(f"xrow{p}", [P, RB, D]) for p in range(2)]
        ybuf = [sb(f"ybuf{p}", [P, RB * D]) for p in range(2)]
        psG = [psI[0][0], psI[0][1], psI[1][0], psI[1][1]]
        NSLOT = len(psG)
        QUARTERS = 4
        PIECES = 2 * QUARTERS
        EARLY = PIECES - 2
        piece = lambda a, m: a[:, m // QUARTERS, m % QUARTERS * (KD * F // QUARTERS):(m % QUARTERS + 1) * (KD * F // QUARTERS)]
        flat = lambda a: a[:, :, :].rearrange("p a b -> p (a b)")
        expert_loaded = [sem(f"expert_{n}_loaded") for n in ("gate", "up", "down")]
        hi_ready = [sem(f"expert_{n}_hi_ready") for n in ("gate", "up", "down")]
        split = [sem(f"expert_{n}_split") for n in ("gate", "up", "down")]
        xrow_loaded = [sem("xrow_loaded0"), sem("xrow_loaded1")]
        xT_filled, xT_hi_ready, xT_ready = sem("xT_filled"), sem("xT_hi_ready"), sem("xT_ready")
        gu_filled = [sem(f"gu_filled{n}") for n in range(NSLOT)]
        sact_ready = [sem(f"sact_ready{n}") for n in range(NSLOT)]
        eh_ready = [sem(f"eh_ready{n}") for n in range(NSLOT)]
        eh_hi_ready = [sem(f"eh_hi_ready{n}") for n in range(NSLOT)]
        eh_split = [sem(f"eh_split{n}") for n in range(NSLOT)]
        y_filled, y_evac = sem("y_filled"), sem("y_evac")
        y_stored = [sem("y_stored0"), sem("y_stored1")]
        x14_loaded = [sem("x14_loaded0"), sem("x14_loaded1")]
        gathered = [sem("gathered0"), sem("gathered1")]
        mix_dve, mixed = sem("mix_dve"), sem("mixed")
        out_stored = [sem("out_stored0"), sem("out_stored1")]
        xb2 = [a[:, :].rearrange("p (c d) -> p c d", c=CHUNKS) for a in (q_s, k_s)]
        yg = [kbqT[:, n].rearrange("p h a n -> p (h a n)").rearrange("p (c k d) -> p c k d", c=CHUNKS, k=TOPK) for n in range(2)]
        SOFTPLUS_TERMS = [1 / 13, 1 / 11, 1 / 9, 1 / 7, 1 / 5, 1 / 3]
        ND_DEC = 23
        SK_D, SK_A, SK_P = 10, 4, 3

        def dve_decays(dve):
            V = nc.vector
            ch = Chain(dve, dec_dve)
            dve.wait_ge(ba_ready, BATCH + 2)
            dve.wait_ge(small_loaded, 16 * 3)
            ch.link(V.tensor_tensor(z_b, ba[:, :, H:2 * H], over_tiles(dtb[:, :]), ALU.add))
            ch.link(V.scalar_tensor_tensor(az_b, z_b, -1.0, z_b, ALU.mult, ALU.max))
            ch.link(V.tensor_scalar(al1, alog[:, :], 80.0, None, ALU.min))
            ch.link(V.tensor_scalar(al2, alog[:, :], -80.0, 0.0, ALU.add, ALU.max))
            ch.link(V.tensor_scalar(al2, al2, 80.0, None, ALU.min))
            dve.wait_ge(dec_act, 3)
            ch.link(V.tensor_scalar(den_b, tt_b, 2.0, None, ALU.add))
            ch.link(V.reciprocal(den_b, den_b))
            ch.link(V.tensor_tensor(s_b, tt_b, den_b, ALU.mult))
            ch.link(V.tensor_tensor(s2_b, s_b, s_b, ALU.mult))
            ch.link(V.tensor_scalar(p_b, s2_b, 1 / 15, None, ALU.mult))
            for c in SOFTPLUS_TERMS:
                ch.link(V.scalar_tensor_tensor(p_b, p_b, c, s2_b, ALU.add, ALU.mult))
            ch.link(V.scalar_tensor_tensor(p_b, p_b, 1.0, s_b, ALU.add, ALU.mult))
            ch.link(V.tensor_scalar(z_b, z_b, 0.0, None, ALU.max))
            ch.link(V.scalar_tensor_tensor(p_b, p_b, 2.0, z_b, ALU.mult, ALU.add))
            ch.link(V.tensor_tensor(p_b, p_b, over_tiles(e1), ALU.mult))
            ch.link(V.tensor_scalar(p_b, p_b, 1e3, None, ALU.min))
            ch.link(V.tensor_tensor(p_b, p_b, over_tiles(e2), ALU.mult))
            ch.link(V.tensor_scalar(dec[:, :, GLOG:GLOG + H], p_b, -1.0, -DEAD, ALU.mult, ALU.max))
            assert ch.n == ND_DEC
            dve.wait_ge(dec_act, 7)
            ch.link(V.tensor_scalar(dec[:, :, NGAM:NGAM + H], dec[:, :, GAM:GAM + H], -1.0, None, ALU.mult))
            V.memset(dec[:, 0:TILES:CHUNKS, GAM:GTOT + H], 0.0).then_inc(dec_ready, 1)

        def act_decays_in(act):
            A = nc.scalar.activation
            act.wait_ge(dec_dve, 5)
            A(tt_b, az_b, ACT.Exp, scale=-1.0).then_inc(dec_act, 1)
            A(e1, al1, ACT.Exp).then_inc(dec_act, 1)
            A(e2, al2, ACT.Exp).then_inc(dec_act, 1)
            A(dec[:, :, BETA:BETA + H], ba[:, :, 0:H], ACT.Sigmoid).then_inc(dec_act, 1)

        def act_decays_out(act):
            A = nc.scalar.activation
            act.wait_ge(dec_pe, 3)
            for ps, c in ((psI[0][0], GAM), (psI[0][1], GTOT), (psI[1][0], DEND)):
                A(dec[:, :, c:c + H], V3(ps[:, 0:TE]), ACT.Exp).then_inc(dec_act, 1)

        def pe_decays(pe):
            pe.wait_ge(dec_dve, ND_DEC)
            for ps, mask in ((psI[0][0], incl), (psI[0][1], ones), (psI[1][0], lower)):
                nc.tensor.matmul(V3(ps[:, 0:TE]), mask[:, :], dec[:, :, GLOG:GLOG + H], start=True, stop=True).then_inc(dec_pe, 1)
            pe.wait_ge(dec_act, 7)

        def dve_late(dve):
            V = nc.vector
            dve.wait_ge(back_evac[BU_LG % 2], b_evac(TILES, BU_LG))
            with dve.Fori(0, ROUNDS) as r:
                ch = Chain(dve, sk_dve, SK_D * r)
                ch.link(V.tensor_reduce(rowm, la[:, :, :], X, ALU.max))
                ch.link(V.tensor_tensor(sd, la[:, :, :], per_head(rowm, E), ALU.subtract))
                dve.wait_ge(sk_act, SK_A * r + 1)
                ch.link(V.tensor_reduce(rows_, se, X, ALU.add))
                dve.wait_ge(sk_act, SK_A * r + 2)
                ch.link(V.tensor_tensor(la[:, :, :], sd, per_head(rowl, E), ALU.subtract))
                ch.link(V.tensor_reduce(colm, by_expert(la[:, :, :]), X, ALU.max))
                dve.wait_ge(sk_pe, SK_P * r + 1)
                ch.link(V.tensor_reduce(cmx, psF[0][0:E, 0:P], X, ALU.max))
                ch.link(V.tensor_scalar(cdiag, ident[0:E, 0:E], cmx, None, ALU.mult))
                dve.wait_ge(sk_pe, SK_P * r + 2)
                ch.link(V.tensor_tensor(sd, la[:, :, :], over_tiles(psF[1][:, 0:E]), ALU.subtract))
                dve.wait_ge(sk_act, SK_A * r + 3)
                ch.link(V.tensor_reduce(cols_, by_expert(se), X, ALU.add))
                dve.wait_ge(sk_act, SK_A * r + 4)
                ch.link(V.tensor_tensor(la[:, :, :], sd, over_tiles(coll), ALU.subtract))
                assert ch.n == SK_D
            ch = Chain(dve, rt_dve)
            ch.link(V.tensor_scalar(sd, la[:, :, :], EXP_ZERO, None, ALU.max))
            for n, h in enumerate((hot, hot2)):
                ch.link(V.tensor_reduce(rowm, sd, X, ALU.max))
                ch.link(V.tensor_tensor(se, sd, per_head(rowm, E), ALU.is_equal))
                ch.link(V.tensor_tensor(cand, se, over_tiles(rank_w[:, :]), ALU.mult))
                ch.link(V.tensor_reduce(rows_, cand, X, ALU.max))
                ch.link(V.tensor_tensor(h, cand, per_head(rows_, E), ALU.is_equal))
                if n == 0:
                    ch.link(V.scalar_tensor_tensor(sd, h, -1e30, sd, ALU.mult, ALU.add))
            ch.link(V.tensor_tensor(both, hot, hot2, ALU.add))
            assert ch.n == 13
            dve.wait_ge(rt_pe, 2)
            ch.link(V.tensor_copy(cnt[0], V3(psF[1][:, 0:TE])))
            cur = 0
            for s in (1, 2, 4, 8, 16):
                V.tensor_copy(cnt[1 - cur][:, 0:s], cnt[cur][:, 0:s])
                ch.link(V.tensor_tensor(cnt[1 - cur][:, s:], cnt[cur][:, s:], cnt[cur][:, 0:TILES - s], ALU.add))
                cur = 1 - cur
            ch.link(V.tensor_tensor(posf, cnt[cur], V3(psF[1][:, 0:TE]), ALU.subtract))
            ch.link(V.tensor_tensor(posf, posf, V3(psF[0][:, 0:TE]), ALU.add))
            ch.link(V.tensor_tensor(need3, per_head(cnt[cur][:, TILES - 1, :], MAXT), thresholds[:, :].unsqueeze(1).to_broadcast([P, E, MAXT]), ALU.is_gt))
            ch.link(V.tensor_reduce(need[0], need3, X, ALU.add))
            ch.link(V.tensor_copy(need[1], need[0]))
            a, b = need[1], need[2]
            for s in (1, 2, 4):
                V.tensor_copy(b[:, 0:s], a[:, 0:s])
                ch.link(V.tensor_tensor(b[:, s:], a[:, s:], a[:, 0:E - s], ALU.add))
                a, b = b, a
            ch.link(V.tensor_tensor(need[3], a, need[0], ALU.subtract))
            ch.link(V.tensor_scalar(need[3], need[3], float(ROWS), None, ALU.mult))
            ch.link(V.tensor_tensor(posf, posf, over_tiles(need[3]), ALU.add))
            for k, h in enumerate((hot, hot2)):
                ch.link(V.tensor_tensor(cand, h, posf, ALU.mult))
                ch.link(V.tensor_reduce(posk[:, :, k], cand, X, ALU.add))
            V.tensor_copy(posi[:, :, :], posk).then_inc(pos_ready, 1)
            ch.link(V.tensor_tensor(te3, tile_iota[:, :].unsqueeze(2).to_broadcast([1, ETILES, E]), a[0:1, :].unsqueeze(1).to_broadcast([1, ETILES, E]), ALU.is_ge))
            ch.link(V.tensor_reduce(tef, te3, X, ALU.add))
            ch.link(V.tensor_scalar(tef, tef, float(E - 1), None, ALU.min))
            V.tensor_copy(te_i[:, :], tef).then_inc(te_ready, 1)
            pos_all = r_s[:, 256:256 + TILES * TOPK]
            ch.link(V.tensor_scalar(pos_col, pos_all, 1 / P, -(P - 1) / (2 * P), ALU.mult, ALU.add))
            ch.link(V.tensor_scalar(pos_col, pos_col, ROUND, None, ALU.add))
            ch.link(V.tensor_scalar(pos_col, pos_col, -ROUND, None, ALU.add))
            ch.link(V.scalar_tensor_tensor(pos_lane, pos_col, -float(P), pos_all, ALU.mult, ALU.add))
            dve.wait_ge(tables_made, 2)
            def hots(b, p, first):
                if not first:
                    dve.wait_ge(pairs_used, b - 1)
                pairs = bass.ds(b * PAIRS_B, PAIRS_B)
                repeated = lambda a: a.unsqueeze(1).to_broadcast([P, PAIRS_B, a.shape[1]])
                ch = Chain(dve, pairs_dve, b)
                V.tensor_tensor(lane_hot[p], repeated(numbers), per_head(pos_lane[:, pairs], P), ALU.is_equal)
                ch.link(V.tensor_tensor(col_hot[p], repeated(numbers[:, 0:ETILES * RB]), per_head(pos_col[:, pairs], ETILES * RB), ALU.is_equal))
                V.tensor_tensor(col_hot[p], col_hot[p], per_head(tokens[:, pairs], ETILES * RB), ALU.mult).then_inc(pairs_ready, 1)

            for p in range(2):
                hots(p, p, True)
            with dve.Fori(1, BATCH // 2) as i:
                for p in range(2):
                    hots(2 * i + p, p, False)
            dve.wait_ge(pairs_used, BATCH)
            V.tensor_copy(list_i[:, :], psB[1][:, 0:ETILES * RB]).then_inc(list_ready, 1)

            def low(m, j, p):
                n = m // QUARTERS
                dve.wait_ge(hi_ready[n], QUARTERS * j + m % QUARTERS + 1)
                V.tensor_tensor(piece(w_lo[p], m).bitcast(F32R), piece(w_raw, m), piece(w_hi[p], m), ALU.subtract).then_inc(split[n], 1)

            def rows_T(j, p):
                dve.wait_ge(xT_hi_ready, j + 1)
                V.tensor_tensor(flat(xT_lo[p]).bitcast(F32R), psF[p][:, :], flat(xT_hi[p]), ALU.subtract).then_inc(xT_ready, 1)

            def low_h(j, p, fb):
                s, n = fb % NSLOT, FB // NSLOT * j + fb // NSLOT
                dve.wait_ge(eh_hi_ready[s], n + 1)
                V.tensor_tensor(eh_lo[p][:, fb, :].bitcast(F32R), eh[:, s, :], eh_hi[p][:, fb, :], ALU.subtract).then_inc(eh_split[s], 1)

            def expert(j, p, more):
                for fb in range(FB):
                    s, n = fb % NSLOT, FB // NSLOT * j + fb // NSLOT
                    dve.wait_ge(sact_ready[s], n + 1)
                    V.tensor_tensor(eh[:, s, :], sact[:, s, :], psG[s][:, ROWS:2 * ROWS], ALU.mult).then_inc(eh_ready[s], 1)
                    if fb > 0:
                        low_h(j, p, fb - 1)
                    if more and fb < EARLY:
                        low(fb, j + 1, 1 - p)
                low_h(j, p, FB - 1)
                if more:
                    rows_T(j + 1, 1 - p)
                    for m in range(EARLY, PIECES):
                        low(m, j + 1, 1 - p)

            for m in range(PIECES):
                low(m, 0, 0)
            rows_T(0, 0)
            with dve.Fori(0, NPAIR) as i:
                for p in range(2):
                    expert(2 * i + p, p, True)
            expert(ETILES - 1, 0, False)
            def places(b, p):
                V.tensor_copy(pidx[:, p], posi[:, bass.ds(b * CHUNKS, CHUNKS), :]).then_inc(pidx_ready, 1)

            dve.wait_ge(pi_ready, 1)
            dve.wait_ge(pos_ready, 1)
            for p in range(2):
                places(p, p)

            def mix(b, p, i):
                ch = Chain(dve, mix_dve, 2 * b)
                ch.link(V.tensor_copy(pw[:, p], pi[:, bass.ds(b * CHUNKS, CHUNKS), 0:TOPK]))
                dve.wait_ge(x14_loaded[p], 16 * i + 16)
                dve.wait_ge(gathered[p], 128 * i + 128)
                for k in range(TOPK):
                    for c in range(CHUNKS):
                        ins = V.scalar_tensor_tensor(xb2[p][:, c, :], yg[p][:, c, k, :], pw[:, p, c, k:k + 1], xb2[p][:, c, :], ALU.mult, ALU.add)
                    if k == 0:
                        ch.link(ins)
                ins.then_inc(mixed, 1)

            with dve.Fori(0, BATCH // 2 - 1) as i:
                for p in range(2):
                    mix(2 * i + p, p, i)
                    places(2 * i + p + 2, p)
            for p in range(2):
                mix(BATCH - 2 + p, p, BATCH // 2 - 1)

        def act_late(act):
            A = nc.scalar.activation
            act.preload_act_table_set("natural_log_exp_and_others")
            def quarter(n, p, i):
                act.wait_ge(wst_stored[p], 48 * i + 48)
                for w in range(3):
                    act.wait_ge(wt_filled, 3 * n + w + 1)
                    A(wst[:, p, w], wt_banks[w][:, :], ACT.Copy).then_inc(wst_ready, 1)

            def sinkhorn(r, prepare):
                act.wait_ge(sk_dve, SK_D * r + 2)
                A(se, sd, ACT.Exp).then_inc(sk_act, 1)
                act.wait_ge(sk_dve, SK_D * r + 3)
                A(rowl, rows_, ACT.Ln).then_inc(sk_act, 1)
                if prepare:
                    quarter(2 * r, 0, r)
                act.wait_ge(sk_dve, SK_D * r + 8)
                A(se, sd, ACT.Exp).then_inc(sk_act, 1)
                act.wait_ge(sk_pe, SK_P * r + 3)
                A(coll, psB[0][:, 0:E], ACT.Ln).then_inc(sk_act, 1)
                if prepare:
                    quarter(2 * r + 1, 1, r)

            with act.Fori(0, QN // 2) as r:
                sinkhorn(r, True)
            with act.Fori(QN // 2, ROUNDS) as r:
                sinkhorn(r, False)
            act.wait_ge(sk_dve, SK_D * ROUNDS)
            A(pi, la[:, :, :], ACT.Exp).then_inc(pi_ready, 1)

            def rows_T(j, p):
                act.wait_ge(xT_filled, j + 1)
                A(flat(xT_hi[p]).bitcast(F32R), psF[p][:, :], ACT.Copy).then_inc(xT_hi_ready, 1)

            def high(m, j, p, first):
                n = m // QUARTERS
                act.wait_ge(expert_loaded[n], 16 * j + 16)
                if not first:
                    act.wait_ge(y_filled, j - 1)
                A(piece(w_hi[p], m).bitcast(F32R), piece(w_raw, m), ACT.Copy).then_inc(hi_ready[n], 1)

            def high_h(j, p, fb):
                s, n = fb % NSLOT, FB // NSLOT * j + fb // NSLOT
                act.wait_ge(eh_ready[s], n + 2)
                A(eh_hi[p][:, fb, :].bitcast(F32R), eh[:, s, :], ACT.Copy).then_inc(eh_hi_ready[s], 1)

            def expert(j, p, i, more):
                for fb in range(FB):
                    s, n = fb % NSLOT, FB // NSLOT * j + fb // NSLOT
                    act.wait_ge(eh_ready[s], n + 1)
                    act.wait_ge(gu_filled[s], n + 1)
                    A(sact[:, s, :], psG[s][:, 0:ROWS], ACT.Silu).then_inc(sact_ready[s], 1)
                    if fb > 0:
                        high_h(j, p, fb - 1)
                    if more and fb < EARLY:
                        high(fb, j + 1, 1 - p, False)
                high_h(j, p, FB - 1)
                if more:
                    rows_T(j + 1, 1 - p)
                    for m in range(EARLY, PIECES):
                        high(m, j + 1, 1 - p, False)
                act.wait_ge(y_stored[p], 16 * i + 16)
                act.wait_ge(y_filled, j + 1)
                A(ybuf[p][:, :], psB[p][:, :], ACT.Copy).then_inc(y_evac, 1)
                act.wait_ge(y_evac, j + 3)
                act.dma_start(ys_d[bass.ds(j * ROWS, ROWS), :].rearrange("(r p) d -> p r d", p=P), ybuf[p][:, :].rearrange("p (r d) -> p r d", r=RB)).then_inc(y_stored[p], 16)

            for m in range(PIECES):
                high(m, 0, 0, True)
            rows_T(0, 0)
            with act.Fori(0, NPAIR) as i:
                for p in range(2):
                    expert(2 * i + p, p, i, True)
            expert(ETILES - 1, 0, NPAIR, False)

        def exact(MM, out_, w, x, start, stop):
            for n, (a, b) in enumerate(((0, 0), (0, 1), (1, 0))):
                ins = MM(out_, w[a].bitcast(F32R), x[b].bitcast(F32R), start=start and n == 0, stop=stop and n == 2)
            return ins

        def pe_late(pe):
            MM = nc.tensor.matmul
            def quarter(n, p, i):
                pe.wait_ge(wnat_loaded[p], 48 * i + 48)
                for w in range(3):
                    pe.wait_ge(wst_ready, 3 * n + w + 1)
                    for a in range(2):
                        for b in range(2):
                            j = (b * 2 + a) * P
                            last = nc.tensor.transpose(wt_banks[w][:, j:j + P], wnat[:, p, w, a * D + b * P:a * D + (b + 1) * P], ident[:, :])
                    last.then_inc(wt_filled, 1)

            def sinkhorn(r, prepare):
                if prepare:
                    quarter(2 * r, 0, r)
                pe.wait_ge(sk_dve, SK_D * r + 5)
                nc.tensor.transpose(psF[0][0:E, 0:P], colm, ident[:, :]).then_inc(sk_pe, 1)
                pe.wait_ge(sk_dve, SK_D * r + 7)
                MM(psF[1][:, 0:E], ones[0:E, :], cdiag, start=True, stop=True).then_inc(sk_pe, 1)
                pe.wait_ge(sk_dve, SK_D * r + 9)
                MM(psB[0][:, 0:E], ones[:, :], cols_, start=True, stop=True).then_inc(sk_pe, 1)
                if prepare:
                    quarter(2 * r + 1, 1, r)

            with pe.Fori(0, QN // 2) as r:
                sinkhorn(r, True)
            with pe.Fori(QN // 2, ROUNDS) as r:
                sinkhorn(r, False)
            pe.wait_ge(rt_dve, 13)
            MM(V3(psF[0][:, 0:TE]), upper[:, :], both, start=True, stop=True).then_inc(rt_pe, 1)
            MM(V3(psF[1][:, 0:TE]), ones[:, :], both, start=True, stop=True).then_inc(rt_pe, 1)

            def pairs(b, p, first=False, last=False):
                pe.wait_ge(pairs_ready, b + 1)
                for n in range(PAIRS_B):
                    ins = MM(psB[1][:, 0:ETILES * RB], lane_hot[p][:, n, :], col_hot[p][:, n, :], start=first and n == 0, stop=last and n == PAIRS_B - 1)
                ins.then_inc(pairs_used, 1)

            pairs(0, 0, first=True), pairs(1, 1)
            with pe.Fori(1, BATCH // 2 - 1) as i:
                for p in range(2):
                    pairs(2 * i + p, p)
            pairs(BATCH - 2, 0), pairs(BATCH - 1, 1, last=True)

            def rows_T(j, p, i):
                pe.wait_ge(xrow_loaded[p], 16 * RB * (i + 1))
                pe.wait_ge(xT_ready, j + 1)
                for k in range(KD):
                    for r in range(RB):
                        c = (k * RB + r) * P
                        last = nc.tensor.transpose(psF[p][:, c:c + P], xrow[p][:, r, k * P:(k + 1) * P], ident[:, :])
                last.then_inc(xT_filled, 1)

            def expert(j, p, i, more):
                pe.wait_ge(xT_ready, j + 3)
                for w in range(2):
                    pe.wait_ge(split[w], QUARTERS * (j + 1))
                for fb in range(FB):
                    s, n = fb % NSLOT, FB // NSLOT * j + fb // NSLOT
                    pe.wait_ge(eh_ready[s], n + 1)
                    for w in range(2):
                        for k in range(KD):
                            c = k * F + fb * P
                            last = exact(MM, psG[s][:, w * ROWS:(w + 1) * ROWS], [a[p][:, w, c:c + P] for a in (w_hi, w_lo)],
                                         [a[p][:, k, :] for a in (xT_hi, xT_lo)], k == 0, k == KD - 1)
                    last.then_inc(gu_filled[s], 1)
                if more:
                    rows_T(j + 1, 1 - p, i + p)
                pe.wait_ge(split[2], j + 1)
                pe.wait_ge(y_evac, j + 1)
                for r in range(RB):
                    for fb in range(FB):
                        if r == 0:
                            s, n = fb % NSLOT, FB // NSLOT * j + fb // NSLOT
                            pe.wait_ge(eh_split[s], n + 1)
                        last = exact(MM, psB[p][:, r * D:(r + 1) * D], [a[p][:, fb, r * P:(r + 1) * P] for a in (eh_hi, eh_lo)],
                                     [a[p][:, 2, fb * D:(fb + 1) * D] for a in (w_hi, w_lo)], fb == 0, fb == FB - 1)
                last.then_inc(y_filled, 1)

            pe.wait_ge(te_ready, 1)
            rows_T(0, 0, 0)
            with pe.Fori(0, NPAIR) as i:
                for p in range(2):
                    expert(2 * i + p, p, i, True)
            expert(ETILES - 1, 0, NPAIR, False)

        def pool_late(pool):
            for s in eh_ready:
                pool.sem_inc(s, 1)
            pool.sem_inc(xT_ready, 2)
            pool.sem_inc(y_evac, 2)
            for s in y_stored + out_stored:
                pool.sem_inc(s, 16)
            pool.wait_ge(back_evac[BU_LG % 2], b_evac(TILES, BU_LG))
            pool.sem_inc(pool_turn, 1)
            pool.iota(numbers, pattern=[[1, P]], base=0, channel_multiplier=0, allow_small_or_imprecise_dtypes=True).then_inc(tables_made, 1)
            pool.iota(tokens.rearrange("p (t k) -> p t k", k=TOPK), pattern=[[P, TILES], [0, TOPK]], base=0, channel_multiplier=1, allow_small_or_imprecise_dtypes=True).then_inc(tables_made, 1)

            def gather_rows(j, p, first):
                if not first:
                    pool.wait_ge(xT_filled, j - 1)
                    pool.sem_inc(pool_turn, 1)
                pool.tensor_copy(ridx[:, p], list_i[:, bass.ds(j * RB, RB)]).then_inc(ridx_ready, 1)
                pool.wait_ge(ridx_ready, j + 1)
                pool.sem_inc(pool_turn, 1)
                for r in range(RB):
                    pool.indirect_dma_start(xrow[p][:, r, :], None, xf_rows, bass.IndirectOffsetOnAxis(ap=ridx[:, p, r:r + 1], axis=0)).then_inc(xrow_loaded[p], 16)

            def split_down(j, p, first):
                pool.wait_ge(expert_loaded[2], 16 * j + 16)
                pool.sem_inc(pool_turn, 1)
                if not first:
                    pool.wait_ge(y_filled, j - 1)
                    pool.sem_inc(pool_turn, 1)
                pool.tensor_copy(w_hi[p][:, 2].bitcast(F32R), w_raw[:, 2]).then_inc(hi_ready[2], 1)
                pool.wait_ge(hi_ready[2], j + 1)
                pool.tensor_tensor(w_lo[p][:, 2].bitcast(F32R), w_raw[:, 2], w_hi[p][:, 2], ALU.subtract).then_inc(split[2], 1)

            pool.wait_ge(xf_stored, 16 * TILES + 16)
            pool.sem_inc(pool_turn, 1)
            pool.wait_ge(list_ready, 1)
            pool.sem_inc(pool_turn, 1)
            gather_rows(0, 0, True)
            gather_rows(1, 1, True)
            split_down(0, 0, True)
            split_down(1, 1, True)
            with pool.Fori(1, NPAIR) as i:
                for p in range(2):
                    gather_rows(2 * i + p, p, False)
                    split_down(2 * i + p, p, False)
            gather_rows(ETILES - 1, 0, False)
            split_down(ETILES - 1, 0, False)
            pool.wait_ge(y_stored[0], 16 * (NPAIR + 1) + 16)
            pool.wait_ge(y_stored[1], 16 * NPAIR + 16)
            with pool.Fori(0, BATCH // 2) as i:
                for p in range(2):
                    pool.wait_ge(pidx_ready, 2 * i + p + 1)
                    pool.sem_inc(pool_turn, 1)
                    for c in range(CHUNKS):
                        for k in range(TOPK):
                            pool.indirect_dma_start(yg[p][:, c, k, :], None, ys_d[:, :], bass.IndirectOffsetOnAxis(ap=pidx[:, p, c, k:k + 1], axis=0)).then_inc(gathered[p], 16)

        def sp_late(sp):
            def load_quarter(n, p, first):
                if not first:
                    sp.wait_ge(wt_filled, 3 * n - 3)
                    sp.sem_inc(sp_turn, 1)
                e, r0 = n // CHUNKS, n % CHUNKS * (F // CHUNKS)
                for w, W in enumerate((W_gate, W_up)):
                    sp.dma_start(wnat[:, p, w].rearrange("p (f d) -> p f d", f=2), W[e][bass.ds(r0, 2 * P)].rearrange("(f p) d -> p f d", p=P)).then_inc(wnat_loaded[p], 16)
                sp.dma_start(wnat[:, p, 2].rearrange("p (k f) -> p k f", k=KD), W_down[e][:, bass.ds(r0, 2 * P)].rearrange("(k p) f -> p k f", p=P)).then_inc(wnat_loaded[p], 16)

            def store_quarter(n, p):
                sp.wait_ge(wst_ready, 3 * n + 6)
                sp.sem_inc(sp_turn, 1)
                e, c = n // CHUNKS, n % CHUNKS
                for w in range(2):
                    sp.dma_start(wts_d[e][:, w * KD * F:(w + 1) * KD * F].rearrange("p (k f) -> p k f", k=KD)[:, :, bass.ds(c * 2 * P, 2 * P)],
                                 wst[:, p, w].rearrange("p (k f) -> p k f", k=KD)).then_inc(wst_stored[p], 16)
                sp.dma_start(wts_d[e][:, bass.ds(2 * KD * F + c * 2 * D, 2 * D)], wst[:, p, 2]).then_inc(wst_stored[p], 16)

            load_quarter(0, 0, True), load_quarter(1, 1, True)
            with sp.Fori(1, QN // 2) as i:
                for p in range(2):
                    load_quarter(2 * i + p, p, False)
                    store_quarter(2 * i + p - 2, p)
            for p in range(2):
                store_quarter(QN - 2 + p, p)
            for p in range(2):
                sp.wait_ge(wst_stored[p], 48 * (QN // 2) + 48)

            def load_weights(j, first):
                e = sp.value_load(te_i[0:1, bass.ds(j, 1)] if not isinstance(j, int) else te_i[0:1, j:j + 1], min_val=0, max_val=E - 1)
                for n in range(3):
                    if not first:
                        sp.wait_ge(split[n], (QUARTERS if n < 2 else 1) * j)
                        sp.sem_inc(sp_turn, 1)
                    sp.dma_start(w_raw[:, n], wts_d[bass.ds(e, 1), :, n * KD * F:(n + 1) * KD * F].rearrange("a p n -> p (a n)")).then_inc(expert_loaded[n], 16)

            sp.wait_ge(te_ready, 1)
            load_weights(0, True)
            load_weights(1, False)
            with sp.Fori(2, ETILES) as j:
                load_weights(j, False)
            sp.wait_ge(y_stored[0], 16 * (NPAIR + 1) + 16)
            sp.wait_ge(y_stored[1], 16 * NPAIR + 16)

            def load_x1(b, p, i):
                sp.wait_ge(out_stored[p], 16 * i + 16)
                sp.sem_inc(sp_turn, 1)
                sp.dma_start(xb2[p], x1_d[bass.ds(b * CHUNKS, CHUNKS)].rearrange("c p d -> p c d")).then_inc(x14_loaded[p], 16)

            with sp.Fori(0, BATCH // 2) as i:
                for p in range(2):
                    load_x1(2 * i + p, p, i)
                for p in range(2):
                    sp.wait_ge(mixed, 2 * i + p + 1)
                    sp.sem_inc(sp_turn, 1)
                    sp.dma_start(out_tiles[bass.ds((2 * i + p) * CHUNKS, CHUNKS)].rearrange("c p d -> p c d"), xb2[p]).then_inc(out_stored[p], 16)
            for p in range(2):
                sp.wait_ge(out_stored[p], 16 * (BATCH // 2) + 16)

        block = ctx.enter_context(nc.Block())

        @block.sync
        def _(sp):
            sp.dma_start(wba[:, :, 0:H], Wb.rearrange("(k p) n -> p k n", p=P)).then_inc(wba_loaded, 16)
            sp.dma_start(wba[:, :, H:2 * H], Wa.rearrange("(k p) n -> p k n", p=P)).then_inc(wba_loaded, 16)
            for n in range(XPARTS):
                s = slice(n * TILES // XPARTS, (n + 1) * TILES // XPARTS)
                sp.dma_start(x_all[:, s, :], x_tiles[s].rearrange("c p d -> p c d")).then_inc(x_loaded[n], 16)
            sp.dma_start(alog[:, :], A_log.partition_broadcast(P)).then_inc(small_loaded, 16)
            sp.dma_start(dtb[:, :], dt_bias.partition_broadcast(P)).then_inc(small_loaded, 16)
            sp.dma_start(onorm[:, :], o_norm_w.partition_broadcast(P)).then_inc(small_loaded, 16)
            for n, raw in enumerate(wvg_raw):
                sp.dma_start(raw, (Wv, Wg)[n // KD][n % KD * P:(n % KD + 1) * P, :]).then_inc(vg_loaded, 16)
            for n, w in enumerate((Wq, Wk)):
                sp.dma_start(wqk[:, n], w.rearrange("(k p) n -> p k n", p=P)).then_inc(w_loaded, 16)
            with sp.Fori(0, BATCH // NB) as i:
                for p in range(NB):
                    b = NB * i + p
                    sp.wait_ge(pre_hT, 2 * b + 2)
                    sp.sem_inc(sp_turn, 1)
                    sp.dma_start(hT_d[bass.ds(CHUNKS * b, CHUNKS)].rearrange("c p (k n) -> p c k n", k=KD), hTb[p]).then_inc(hT_stored[p], 16)
            for p in range(NB):
                sp.wait_ge(hT_stored[p], 16 * (BATCH // NB) + 16)

            def load_hT(f, q):
                sp.dma_start(hT[:, q], hT_d[f].rearrange("p (k n) -> p k n", k=KD)).then_inc(hT_loaded[q], 16)

            def tail(t):
                sp.wait_ge(x1_ready, t + 1)
                sp.sem_inc(sp_turn, 1)
                sp.dma_start(x1_d[t], x1[:, :]).then_inc(x1_stored, 16)
                sp.wait_ge(xf_ready, t + 1)
                sp.sem_inc(sp_turn, 1)
                sp.dma_start(xf_d[t], xf[:, :]).then_inc(xf_stored, 16)

            def step(t, p, ahead, before):
                if ahead:
                    sp.wait_ge(front_filled[1], f_filled(t, FU_PROJ + 7))
                    sp.sem_inc(sp_turn, 1)
                    load_hT(t + 2, p)
                if before:
                    tail(t - 1)
                sp.dma_start(xin[:, 0, :], x_tiles[t]).then_inc(xin_loaded, 16)

            load_hT(0, 0)
            load_hT(1, 1)
            sp.dma_start(wo, Wo.rearrange("(h p) n -> p h n", p=P)).then_inc(tail_loaded, 16)
            sp.dma_start(wfc, W_fc.rearrange("(k p) n -> p k n", p=P)).then_inc(tail_loaded, 16)
            sp.dma_start(wproj, W_proj.rearrange("(f p) n -> p f n", p=P)).then_inc(tail_loaded, 16)
            with nc.allow_non_contiguous_dma(reason="2048 elements, once"):
                for k in range(KD):
                    sp.dma_start(gwT[:, k, :], gate_W[:, k * P:(k + 1) * P].rearrange("e p -> p e")).then_inc(gate_loaded, 16)
            step(0, 0, True, False)
            with sp.Fori(0, PAIRS - 1) as i:
                for p in range(2):
                    t = 2 * i + p + 1
                    step(t, 1 - p, True, True)
            for t in range(2 * PAIRS - 1, TILES):
                step(t, t % 2, t + 2 < TILES, True)
            tail(TILES - 1)
            sp.wait_ge(x1_stored, 16 * TILES + 16)
            sp.wait_ge(xf_stored, 16 * TILES + 16)
            sp_late(sp)

        @block.gpsimd
        def _(pool):
            pool.memset(ones[:, :], 1.0).then_inc(consts, 1)
            pool.memset(state[:, :], 0.0).then_inc(consts, 1)
            pool.iota(iota_i[:, 0, :], pattern=[[0, P]], base=0, channel_multiplier=1).then_inc(consts, 1)
            pool.iota(iota_i[:, 1, :], pattern=[[1, P]], base=0, channel_multiplier=0).then_inc(consts, 1)
            pool.iota(tile_iota[:, :], pattern=[[1, ETILES]], base=0, channel_multiplier=0, allow_small_or_imprecise_dtypes=True).then_inc(consts, 1)
            pool.iota(thresholds[:, :], pattern=[[ROWS, MAXT]], base=0, channel_multiplier=0, allow_small_or_imprecise_dtypes=True).then_inc(consts, 1)
            pool.iota(rank_w[:, :], pattern=[[-1, E]], base=E, channel_multiplier=0, allow_small_or_imprecise_dtypes=True).then_inc(consts, 1)
            pool.wait_ge(consts, 7)
            pool.affine_select(out=incl[:, :], in_=ones[:, :], compare_op=ALU.is_ge, fill=0.0, base=0,
                               pattern=[[1, P]], channel_multiplier=-1).then_inc(consts, 1)
            pool.affine_select(out=upper[:, :], in_=ones[:, :], compare_op=ALU.is_gt, fill=0.0, base=0,
                               pattern=[[1, P]], channel_multiplier=-1).then_inc(consts, 1)
            pool.affine_select(out=lower[:, :], in_=ones[:, :], compare_op=ALU.is_gt, fill=0.0, base=0,
                               pattern=[[-1, P]], channel_multiplier=1).then_inc(consts, 1)
            pool.affine_select(out=ident[:, :], in_=ones[:, :], compare_op=ALU.is_equal, fill=0.0, base=0,
                               pattern=[[1, P]], channel_multiplier=-1).then_inc(consts, 1)
            for s in front_evac + back_evac:
                pool.sem_inc(s, 1)
            pool.sem_inc(ba_ready, 2)
            pool.sem_inc(pre_tr, 4)
            for s in [x1_stored, xf_stored] + hT_stored:
                pool.sem_inc(s, 16)
            for s in wst_stored:
                pool.sem_inc(s, 48)
            pool.sem_inc(wst_ready, 3)
            for n, raw in enumerate(wvg_raw):
                pool.wait_ge(vg_hi_ready, n + 1)
                pool.tensor_tensor(wvg_lo[:, n // KD, n % KD, :].bitcast(F32R), raw, wvg_hi[:, n // KD, n % KD, :], ALU.subtract).then_inc(vg_split, 1)
            pool.wait_ge(h_hi_ready, 1)
            pool.tensor_tensor(hT_lo[:, :, :].bitcast(F32R), hT[:, 0], hT_hi[:, :, :], ALU.subtract).then_inc(h_split, 1)

            def front_early(f, q, first):
                pool.tensor_copy(sc[:, q, :].unsqueeze(1), dec[:, bass.ds(f, 1), :]).then_inc(sc_ready, 1)
                if not first:
                    pool.wait_ge(front_evac[0], f_evac(f - 1, FU_KKQ + 2))
                    pool.wait_ge(front_evac[1], f_evac(f - 1, FU_KKQ + 3))
                pool.wait_ge(sc_ready, f + 1)
                pool.tensor_tensor(dT[:, :, :], over_heads(incl[:, :], H), per_head(sc[:, q, GLOG:GLOG + H]), ALU.mult).then_inc(rhs_ready, 1)

            def link(ins, chain, n):
                ins.then_inc(chain, 1)
                pool.wait_ge(chain, n)
                pool.sem_inc(pool_turn, 1)

            def first_root(v, r, chain, n):
                link(pool.tensor_scalar(r.bitcast(I32), v.bitcast(I32), -0.5, ROOT_MAGIC, ALU.mult, ALU.add), chain, n)

            def roots(v, r, a, chain, n, ready):
                first_root(v, r, chain, n + 1)
                for k in range(3):
                    m = n + 4 * k + 1
                    link(pool.tensor_tensor(a, r, r, ALU.mult), chain, m + 1)
                    link(pool.tensor_tensor(a, a, v, ALU.mult), chain, m + 2)
                    link(pool.tensor_scalar(a, a, -0.5, 1.5, ALU.mult, ALU.add), chain, m + 3)
                    last = pool.tensor_tensor(r, a, r, ALU.mult)
                    if k < 2:
                        link(last, chain, m + 4)
                last.then_inc(ready, 1)

            def row_root(v, r, a, chain, n, ready):
                first_root(v, r, chain, n + 1)
                c = 1.0
                for k in range(3):
                    m = n + 2 * k + 1
                    link(pool.tensor_scalar(a, r, r, v, ALU.mult, ALU.mult), chain, m + 1)
                    link(pool.tensor_scalar(r, a, -3.0 * c * c, r, ALU.add, ALU.mult), chain, m + 2)
                    c *= -2.0 * c * c
                pool.tensor_scalar(r, r, 1.0 / c, None, ALU.mult).then_inc(ready, 1)

            def norm_roots(f):
                pool.wait_ge(ss_ready, 2 * f + 2)
                pool.sem_inc(pool_turn, 1)
                link(pool.tensor_scalar(nv[:, :], ss[:, :], RMS_EPS, None, ALU.add), norm_pool, N_NORM * f + 1)
                roots(nv[:, :], rn[:, :], na[:, :], norm_pool, N_NORM * f + 1, rn_ready)

            def m_root(t):
                pool.wait_ge(mv_ready, t + 1)
                pool.sem_inc(pool_turn, 1)
                n = N_ROW * t + 1
                link(pool.tensor_scalar(mrow_v[:, 1:2], mrow_v[:, 0:1], 1.0 / D, RMS_EPS, ALU.mult, ALU.add), m_pool, n)
                row_root(mrow_v[:, 1:2], mrow_r[:, 0:1], mrow_r[:, 1:2], m_pool, n, mr_ready)

            def x_root(t):
                pool.wait_ge(xv_ready, t + 1)
                pool.sem_inc(pool_turn, 1)
                n = N_ROW * t + 1
                link(pool.tensor_scalar(xrow_v[:, 0:1], bag[:, 1:2], LN_EPS, None, ALU.add), x_pool, n)
                row_root(xrow_v[:, 0:1], xrow_r[:, 0:1], xrow_r[:, 1:2], x_pool, n, xr_ready)

            def o_roots(t):
                pool.wait_ge(os_ready, t + 1)
                pool.sem_inc(pool_turn, 1)
                link(pool.tensor_scalar(os_[:, 1, :], os_[:, 0, :], 1.0 / DK, RMS_EPS, ALU.mult, ALU.add), o_pool, N_O * t + 1)
                roots(os_[:, 1, :], or_[:, 0, :], or_[:, 1, :], o_pool, N_O * t + 1, or_ready)

            def front_mid(f, q):
                pool.wait_ge(kn_ready, f + 1)
                pool.tensor_tensor(kb[:, :].rearrange("p (h d) -> p h d", h=H), k_s[:, :].rearrange("p (h d) -> p h d", h=H),
                                   per_head(sc[:, q, BETA:BETA + H]), ALU.mult).then_inc(kb_ready, 1)
                for n in range(G):
                    pool.wait_ge(front_evac[n], f_evac(f, FU_D + n))
                    d = dT[:, n * HG:(n + 1) * HG, :]
                    pool.tensor_tensor(d, d, over_heads(incl[:, :]), ALU.mult).then_inc(dtm_ready, 1)

            heads = lambda a: a[:, :].rearrange("p (h d) -> p h d", h=H)

            def inverse_start(f, q, first):
                for g in range(G):
                    y = yi[:, g * GW:(g + 1) * GW].rearrange("p (h n) -> p h n", h=HG)
                    for n in range(2):
                        u = FU_KKQ + 2 * g + n
                        pool.wait_ge(front_evac[u % 2], f_evac(f, u))
                    if not first:
                        pool.wait_ge(back_filled[(BU_U + g) % 2], b_filled(f - 1, BU_U + g))
                    pool.tensor_tensor(y, aP[:, q, g * HG:(g + 1) * HG, 0, :], over_heads(neg_m0t[:, :]), ALU.mult).then_inc(y0_pool, 1)
                    pool.wait_ge(y0_pool, 2 * f + g + 1)
                    pool.tensor_tensor(y, y, over_heads(ident[:, :]), ALU.add).then_inc(y_ready[g], 1)

            def decayed_k(f, q):
                pool.wait_ge(kn_ready, f + 1)
                pool.tensor_tensor(heads(kd), heads(k_s), per_head(sc[:, q, DEND:DEND + H]), ALU.mult).then_inc(kd_ready, 1)

            def beta_v(f, q):
                pool.wait_ge(front_evac[1], f_evac(f, FU_PROJ + 5))
                pool.tensor_tensor(heads(vb), heads(v_s), per_head(sc[:, q, BETA:BETA + H]), ALU.mult).then_inc(vb_ready, 1)

            def front_gate(f):
                pool.wait_ge(front_evac[1], f_evac(f, FU_PROJ + 7))
                pool.tensor_tensor(heads(gw), heads(g_s), over_heads(onorm[:, :], H), ALU.mult).then_inc(gw_ready, 1)

            def step(t, p, more, tail):
                f, q = t + 1, 1 - p
                if more:
                    front_early(f, q, False)
                if tail:
                    m_root(t - 1)
                if more:
                    norm_roots(f)
                    front_mid(f, q)
                if tail:
                    x_root(t - 1)
                if more:
                    inverse_start(f, q, False)
                    pool.wait_ge(back_evac[BU_KDU % 2], b_evac(t, BU_KDU))
                    pool.wait_ge(back_evac[(BU_KDU + 1) % 2], b_evac(t, BU_KDU + 1))
                    decayed_k(f, q)
                o_roots(t)
                if more:
                    beta_v(f, q)
                    pool.wait_ge(og_ready, t + 1)
                    front_gate(f)

            pool.wait_ge(dec_ready, 1)
            pool.wait_ge(small_loaded, 16 * 3)
            front_early(0, 0, True)
            norm_roots(0)
            front_mid(0, 0)
            decayed_k(0, 0)
            beta_v(0, 0)
            front_gate(0)
            inverse_start(0, 0, True)
            step(0, 0, True, False)
            with pool.Fori(0, PAIRS) as i:
                for p in range(2):
                    step(2 * i + p + 1, 1 - p, True, True)
            step(TILES - 1, 1, False, True)
            m_root(TILES - 1)
            x_root(TILES - 1)
            pool_late(pool)

        @block.scalar
        def _(act):
            A = nc.scalar.activation
            act.wait_ge(vg_loaded, 16 * 2 * KD)
            for n, raw in enumerate(wvg_raw):
                A(wvg_hi[:, n // KD, n % KD, :].bitcast(F32R), raw, ACT.Copy).then_inc(vg_hi_ready, 1)
            with act.Fori(0, BATCH // NB) as i:
                for p in range(NB + 1):
                    if p < NB:
                        b = NB * i + p
                        act.wait_ge(hT_stored[p], 16 * i + 16)
                        for n in range(2):
                            act.wait_ge(pre_tr, 2 * b + n + 5)
                            A(hTb[p][:, 2 * n:2 * n + 2].rearrange("p c k n -> p (c k n)"), pre_ps[p % 2][n][:, :], ACT.Copy).then_inc(pre_hT, 1)
                    if p > 0:
                        b = NB * i + p - 1
                        act.wait_ge(pre_ba, b + 1)
                        A(ba[:, bass.ds(CHUNKS * b, CHUNKS), :], psB[(p - 1) % 2][:, 0:CHUNKS * 2 * H].rearrange("p (c n) -> p c n", c=CHUNKS), ACT.Copy).then_inc(ba_ready, 1)
            act_decays_in(act)

            def silu(f, n, first):
                u = FU_PROJ + n
                if not first and n in (2, 4, 6):
                    act.wait_ge({2: kd_ready, 4: vb_ready, 6: gw_ready}[n], f)
                act.wait_ge(front_filled[u % 2], f_filled(f, u))
                A((q_s, k_s, v_s, g_s)[n // 2][:, n % 2 * GW:(n % 2 + 1) * GW], psF[u % 2][:, :], ACT.Silu).then_inc(front_evac[u % 2], 1)

            def hT_high(f, q, turn):
                act.wait_ge(hT_loaded[q], 16 * turn + 16)
                A(hT_hi[:, :, :].bitcast(F32R), hT[:, q], ACT.Copy).then_inc(h_hi_ready, 1)

            def square(f, n):
                if n == 1:
                    act.wait_ge(ss_ready, 2 * f + 1)
                act.wait_ge(front_evac[0], f_evac(f, FU_PROJ + 2 * n))
                act.wait_ge(front_evac[1], f_evac(f, FU_PROJ + 2 * n + 1))
                A(kb[:, :], (q_s, k_s)[n][:, :], ACT.Square).then_inc(sq_ready, 1)

            def decay_exp(f):
                for n in range(G):
                    u = FU_D + n
                    act.wait_ge(front_filled[u % 2], f_filled(f, u))
                    A(dT[:, n * HG:(n + 1) * HG, :].rearrange("p h n -> p (h n)"), psF[u % 2][:, :], ACT.Exp).then_inc(front_evac[u % 2], 1)

            def copy_T(f, u0, dst):
                for n in range(G):
                    u = u0 + n
                    act.wait_ge(front_filled[u % 2], f_filled(f, u))
                    A(dst[:, n * HG:(n + 1) * HG, :], psF[u % 2][:, :].rearrange("p (h n) -> p h n", h=HG), ACT.Copy).then_inc(front_evac[u % 2], 1)

            def copy_x(t):
                for g in range(G):
                    act.wait_ge(inv_filled[0][g], 7 * t + 1)
                    A(xi[:, g * GW:(g + 1) * GW], psI[0][g][:, :], ACT.Copy).then_inc(x_ready[g], 1)

            def copy_y(t, l):
                for g in range(G):
                    act.wait_ge(inv_filled[1][g], 11 * t + 2 * l)
                    A(yi[:, g * GW:(g + 1) * GW], psI[1][g][:, :], ACT.Copy).then_inc(y_ready[g], 1)

            def evac(s, u, dst, func=ACT.Copy):
                act.wait_ge(back_filled[u % 2], b_filled(s, u))
                A(dst, psB[u % 2][:, 0:dst.shape[1]], func).then_inc(back_evac[u % 2], 1)

            def back(t, p):
                act.wait_ge(sc_ready, t + 1)
                for g in range(G):
                    u = BU_QS + g
                    act.wait_ge(back_filled[u % 2], b_filled(t, u))
                    for h in range(HG):
                        c = g * HG + h
                        last = A(qsg[:, c * DK:(c + 1) * DK], psB[u % 2][:, h * DK:(h + 1) * DK], ACT.Copy, scale=sc[:, p, GAM + c:GAM + c + 1])
                    last.then_inc(back_evac[u % 2], 1)
                for g in range(G):
                    evac(t, BU_U + g, u_s[:, g * GW:(g + 1) * GW])
                for g in range(G):
                    u = BU_PU + g
                    act.wait_ge(back_evac[u % 2], b_evac(t, u))
                    s = slice(g * GW, (g + 1) * GW)
                    A(r_s[:, s], o_s[:, s], ACT.Square).then_inc(so_ready, 1)

            def tail_o(t):
                for g in range(G):
                    evac(t + 1, BU_OT + g, oT[:, g * GW:(g + 1) * GW])

            def tail_m(t):
                evac(t + 1, BU_MT, mT[:, :])

            def tail_fc(t):
                for n in range(2):
                    evac(t + 1, BU_FC + n, hid[:, n * GW:(n + 1) * GW], ACT.Relu)

            def tail_x(t):
                evac(t + 1, BU_XT, xfT[:, :])

            def step(t, p, more, tail, turn):
                f, q = t + 1, 1 - p
                if more:
                    silu(f, 0, False)
                copy_x(t)
                if more:
                    silu(f, 1, False)
                    hT_high(f, q, turn)
                for l in range(1, LEVELS):
                    if more and l <= 3:
                        silu(f, 2 * l, False)
                    if tail and l == 2:
                        tail_o(t - 1)
                    if more and l <= 3:
                        silu(f, 2 * l + 1, False)
                    if more and l <= 2:
                        square(f, l - 1)
                    if more and l == 4:
                        decay_exp(f)
                    if tail and l == 4:
                        tail_m(t - 1)
                    if more and l == 4:
                        copy_T(f, FU_K, kT)
                    if tail and l == 4:
                        tail_fc(t - 1)
                    if more and l == 5:
                        copy_T(f, FU_KB, kbqT[:, q, :, 0, :])
                        copy_T(f, FU_Q, kbqT[:, q, :, 1, :])
                    if l < LEVELS - 1:
                        copy_y(t, l)
                back(t, p)
                if tail:
                    tail_x(t - 1)

            hT_high(0, 0, 0)
            for n in range(8):
                silu(0, n, True)
            act_decays_out(act)
            square(0, 0), square(0, 1)
            decay_exp(0)
            copy_T(0, FU_K, kT)
            copy_T(0, FU_KB, kbqT[:, 0, :, 0, :])
            copy_T(0, FU_Q, kbqT[:, 0, :, 1, :])
            step(0, 0, True, False, 0)
            with act.Fori(0, PAIRS) as i:
                for p in range(2):
                    step(2 * i + p + 1, 1 - p, True, True, i + 1)
            step(TILES - 1, 1, False, True, 0)
            for part in (tail_o, tail_m, tail_fc, tail_x):
                part(TILES - 1)
            act_late(act)

        @block.vector
        def _(dve):
            V = nc.vector
            ch = Chain(dve, const_dve)
            dve.wait_ge(consts, 11)
            ch.link(V.tensor_tensor(iota_i[:, 0, :], iota_i[:, 0, :], iota_i[:, 1, :], ALU.bitwise_xor))
            ch.link(V.tensor_copy(xor[:, :], iota_i[:, 0, :]))
            wide = xi[:, 0:LEVELS * P].rearrange("p (l n) -> p l n", l=LEVELS)
            for l in range(LEVELS):
                ins = V.scalar_tensor_tensor(wide[:, l, :], xor[:, :], float(1 << l), lower[:, :], ALU.is_ge, ALU.mult)
            ch.link(ins)
            for l in range(LEVELS - 1):
                ins = V.tensor_tensor(left(level_mask[:, l, :], l, 1), left(wide[:, l, :], l), left(wide[:, l + 1, :], l), ALU.subtract)
            ins = V.tensor_copy(level_mask[:, l + 1, :], left(wide[:, l + 1, :], l + 1)[:, 0, :])
            ch.link(ins)
            ch.link(V.scalar_tensor_tensor(neg_m0t[:, :], xor[:, :], 1.0, upper[:, :], ALU.is_equal, ALU.mult))
            ch.link(V.tensor_scalar(neg_m0t[:, :], neg_m0t[:, :], -1.0, None, ALU.mult))

            def root(ch, v, r, a):
                ch.link(V.tensor_scalar(r.bitcast(I32), v.bitcast(I32), -0.5, ROOT_MAGIC, ALU.mult, ALU.add))
                for _ in range(3):
                    ch.link(V.scalar_tensor_tensor(a, r, -0.5, r, ALU.mult, ALU.mult))
                    ch.link(V.tensor_tensor(a, a, v, ALU.mult))
                    ch.link(V.scalar_tensor_tensor(r, a, 1.5, r, ALU.add, ALU.mult))

            for n in range(XPARTS):
                dve.wait_ge(x_loaded[n], 16)
                with dve.Fori(n * BATCH // XPARTS, (n + 1) * BATCH // XPARTS) as b:
                    ch = Chain(dve, pre_dve, 3 * b)
                    for c in range(CHUNKS):
                        ins = V.bn_stats(pbst4[:, c, :], x_all[:, bass.ds(CHUNKS * b + c, 1), :].rearrange("p t d -> p (t d)"))
                    ch.link(ins)
                    dve.sem_inc(dve_turn, 1)
                    for c in range(CHUNKS):
                        ins = V.bn_aggr(pmv4[:, c, :], pbst4[:, c, :])
                    ch.link(ins)
                    ch.link(V.tensor_copy(pmv[:, bass.ds(CHUNKS * b, CHUNKS), :], pmv4))
            ch = Chain(dve, pre_dve, 3 * BATCH)
            V.tensor_copy(dec[:, :, MEAN], pmv[:, :, 0])
            ch.link(V.tensor_scalar(pv, pmv[:, :, 1], LN_EPS, None, ALU.add))
            root(ch, pv, pr, pa)
            V.tensor_copy(dec[:, :, RINV], pr)
            ch.link(V.tensor_tensor(pms, pmv[:, :, 1], pr, ALU.mult))
            ch.link(V.tensor_tensor(pms, pms, pr, ALU.mult))
            ch.link(V.tensor_scalar(pms, pms, RMS_EPS, None, ALU.add))
            root(ch, pms, pr2, pa)
            ch.link(V.tensor_tensor(phs, pr, pr2, ALU.mult))
            n0 = 3 * BATCH + ch.n
            with dve.Fori(0, BATCH // 2) as i:
                for p in range(2):
                    b = 2 * i + p
                    V.tensor_copy(pmean4, pmv[:, bass.ds(CHUNKS * b, CHUNKS), 0])
                    Chain(dve, pre_dve, n0 + b).link(V.tensor_copy(phs4, phs[:, bass.ds(CHUNKS * b, CHUNKS)]))
                    dve.wait_ge(pre_tr, 2 * b + 2)
                    for c in range(CHUNKS):
                        ins = V.tensor_scalar(hb[p][:, c, :], x_all[:, bass.ds(CHUNKS * b + c, 1), :].rearrange("p t d -> p (t d)"), pmean4[:, c:c + 1], phs4[:, c:c + 1], ALU.subtract, ALU.mult)
                    ins.then_inc(pre_h, 1)
                    dve.wait_ge(pre_h, b + 1)
            dve_decays(dve)

            H3 = lambda a: a[:, :].rearrange("p (h d) -> p h d", h=H)

            def norm_sum(f, n):
                dve.wait_ge(sq_ready, 2 * f + n + 1)
                V.tensor_reduce(ss[:, n * H:(n + 1) * H], H3(kb), X, ALU.add).then_inc(ss_ready, 1)

            def norms(f):
                dve.wait_ge(rn_ready, f + 1)
                V.tensor_tensor(H3(k_s), H3(k_s), per_head(rn[:, H:2 * H]), ALU.mult).then_inc(kn_ready, 1)
                V.scalar_tensor_tensor(H3(q_s), H3(q_s), DK ** -0.5, per_head(rn[:, 0:H]), ALU.mult, ALU.mult).then_inc(qn_ready, 1)

            def delta_products(f, q, n):
                u = FU_KKQ + n
                if n % 2 == 0:
                    dve.wait_ge(dtm_ready, 2 * f + n // 2 + 1)
                dve.wait_ge(front_filled[u % 2], f_filled(f, u))
                d = dT[:, 2 * n:2 * n + 2, :].unsqueeze(2).to_broadcast([P, 2, 2, P])
                V.tensor_tensor(aP[:, q, 2 * n:2 * n + 2], psF[u % 2][:, :].rearrange("p (h a n) -> p h a n", h=2, a=2), d, ALU.mult).then_inc(front_evac[u % 2], 1)

            GV = lambda a, g: a[:, g * GW:(g + 1) * GW].rearrange("p (h n) -> p h n", h=HG)

            HW = GW // 2
            half = lambda a, g: a[:, g * HW:(g + 1) * HW]

            def level_t(t, l):
                for g in range(G):
                    dve.wait_ge(inv_filled[0][g], 7 * t + l + 1)
                    V.tensor_tensor(half(ti, g).rearrange("p (h n) -> p h n", h=HG), psI[0][g][:, 0:HW].rearrange("p (h n) -> p h n", h=HG),
                                    over_heads(level_mask[:, l, :]), ALU.mult).then_inc(t_ready[g], 1)

            def level_x(t, l):
                for g in range(G):
                    dve.wait_ge(inv_filled[1][g], 11 * t + 2 * l - 1)
                    if l < LEVELS - 1:
                        a = left(xi[:, g * GW:(g + 1) * GW], l)
                        V.tensor_tensor(a, a, left(psI[1][g][:, 0:HW], l, 1), ALU.subtract).then_inc(x_ready[g], 1)
                    else:
                        a = GV(yi, g)[0:P // 2, :, P // 2:P]
                        V.tensor_tensor(a, a, psI[1][g][0:P // 2, 0:HW].rearrange("p (h n) -> p h n", h=HG), ALU.subtract).then_inc(y_ready[g], 1)

            def state_in(t, p):
                dve.wait_ge(vb_ready, t + 1)
                dve.wait_ge(sc_ready, t + 1)
                for g in range(G):
                    u = BU_KBS + g
                    dve.wait_ge(back_filled[u % 2], b_filled(t, u))
                    for h in range(HG):
                        c = g * HG + h
                        s = slice(c * DK, (c + 1) * DK)
                        ins = V.scalar_tensor_tensor(r_s[:, s], psB[u % 2][:, h * DK:(h + 1) * DK], sc[:, p, NGAM + c:NGAM + c + 1], vb[:, s], ALU.mult, ALU.add)
                    ins.then_inc(back_evac[u % 2], 1)

            def state_out(t, p):
                for g in range(G):
                    u = BU_PU + g
                    dve.wait_ge(back_evac[(BU_QS + g) % 2], b_evac(t, BU_QS + g))
                    dve.wait_ge(back_filled[u % 2], b_filled(t, u))
                    s = slice(g * GW, (g + 1) * GW)
                    V.tensor_tensor(o_s[:, s], qsg[:, s], psB[u % 2][:, :], ALU.add).then_inc(back_evac[u % 2], 1)
                for g in range(G):
                    u = BU_KDU + g
                    dve.wait_ge(back_filled[u % 2], b_filled(t, u))
                    for h in range(HG):
                        c = g * HG + h
                        s = slice(c * DK, (c + 1) * DK)
                        ins = V.scalar_tensor_tensor(state[:, s], state[:, s], sc[:, p, GTOT + c:GTOT + c + 1], psB[u % 2][:, h * DK:(h + 1) * DK], ALU.mult, ALU.add)
                    ins.then_inc(back_evac[u % 2], 1)

            def tail_xln(t):
                dve.wait_ge(msc_ready, t + 1)
                dve.wait_ge(xin_loaded, 16 * t + 16)
                V.tensor_scalar(xin[:, 1, :], xin[:, 0, :], msc[:, 0:1], msc[:, 1:2], ALU.subtract, ALU.mult).then_inc(xln_ready, 1)

            def square_sums(t, p):
                V.tensor_copy(msc[:, :], sc[:, p, MEAN:MEAN + 2]).then_inc(msc_ready, 1)
                dve.wait_ge(so_ready, 2 * t + 2)
                V.tensor_reduce(os_[:, 0, :], H3(r_s), X, ALU.add).then_inc(os_ready, 1)

            def tail_o(t):
                dve.wait_ge(or_ready, t + 1)
                dve.wait_ge(gw_ready, t + 1)
                for h in range(H):
                    s = slice(h * DK, (h + 1) * DK)
                    ins = V.scalar_tensor_tensor(o_s[:, s], o_s[:, s], or_[:, 0, h:h + 1], gw[:, s], ALU.mult, ALU.mult)
                ins.then_inc(og_ready, 1)

            def tail_x2(t):
                dve.wait_ge(xln_ready, t + 1)
                b = BU_WO % 2
                dve.wait_ge(back_filled[b], b_filled(t + 1, BU_WO))
                V.tensor_tensor(x2[:, :], xin[:, 1, :], psB[b][:, 0:D], ALU.add).then_inc(back_evac[b], 1)
                dve.wait_ge(back_evac[b], b_evac(t + 1, BU_WO))
                V.tensor_tensor_reduce(out=m_s[:, :], in0=x2[:, :], in1=x2[:, :], scale=1.0, scalar=0.0, op0=ALU.mult, op1=ALU.add,
                                       accum_out=mrow_v[:, 0:1]).then_inc(mv_ready, 1)

            def tail_m(t):
                dve.wait_ge(mr_ready, t + 1)
                V.tensor_scalar(m_s[:, :], x2[:, :], mrow_r[:, 0:1], None, ALU.mult).then_inc(m_ready, 1)

            def tail_fc(t):
                for n in range(2):
                    u = BU_FC + n
                    dve.wait_ge(back_evac[u % 2], b_evac(t + 1, u))
                    s = slice(n * GW, (n + 1) * GW)
                    V.tensor_tensor(hid[:, s], hid[:, s], hid[:, s], ALU.mult).then_inc(hid_ready, 1)

            def tail_x1(t):
                b = BU_PROJ % 2
                dve.wait_ge(x1_stored, 16 * t + 16)
                dve.wait_ge(back_filled[b], b_filled(t + 1, BU_PROJ))
                V.tensor_tensor(x1[:, :], x2[:, :], psB[b][:, 0:D], ALU.add).then_inc(back_evac[b], 1)
                dve.wait_ge(back_evac[b], b_evac(t + 1, BU_PROJ))
                V.tensor_tensor(x1[:, :], x1[:, :], xin[:, 0, :], ALU.add).then_inc(x1_ready, 1)
                dve.wait_ge(x1_ready, t + 1)
                Chain(dve, tail_dve, t).link(V.bn_stats(bst[:, :], x1[:, :]))
                dve.sem_inc(dve_turn, 1)
                V.bn_aggr(bag[:, :], bst[:, :]).then_inc(xv_ready, 1)

            def tail_xf(t):
                dve.wait_ge(xr_ready, t + 1)
                dve.wait_ge(xf_stored, 16 * t + 16)
                V.tensor_scalar(xf[:, :], x1[:, :], bag[:, 0:1], xrow_r[:, 0:1], ALU.subtract, ALU.mult).then_inc(xf_ready, 1)

            def tail_logits(t):
                b = BU_LG % 2
                dve.wait_ge(back_filled[b], b_filled(t + 1, BU_LG))
                V.tensor_scalar(la[:, bass.ds(t, 1), :], psB[b][:, 0:E].unsqueeze(1), -1.0 / EPSILON, None, ALU.mult).then_inc(back_evac[b], 1)

            def step(t, p, more, tail):
                f, q = t + 1, 1 - p
                for l in range(1, LEVELS):
                    level_t(t, l)
                    if more and l == 1:
                        dve.wait_ge(h_hi_ready, f + 1)
                        V.tensor_tensor(hT_lo[:, :, :].bitcast(F32R), hT[:, q], hT_hi[:, :, :], ALU.subtract).then_inc(h_split, 1)
                    if tail and l == 3:
                        tail_x2(t - 1)
                    if more and l in (2, 3):
                        norm_sum(f, l - 2)
                    if more and l == 4:
                        norms(f)
                    if tail and l == 5:
                        tail_fc(t - 1)
                    if more and l == 6:
                        delta_products(f, q, 0), delta_products(f, q, 1)
                    level_x(t, l)
                    if tail and l == 1:
                        tail_o(t - 1)
                        tail_xln(t - 1)
                    if tail and l == 3:
                        tail_m(t - 1)
                    if l == 5:
                        state_in(t, p)
                        if tail:
                            tail_x1(t - 1)
                if more:
                    delta_products(f, q, 2), delta_products(f, q, 3)
                if tail:
                    tail_xf(t - 1)
                state_out(t, p)
                square_sums(t, p)
                if tail:
                    tail_logits(t - 1)

            norm_sum(0, 0), norm_sum(0, 1)
            norms(0)
            for n in range(4):
                delta_products(0, 0, n)
            step(0, 0, True, False)
            with dve.Fori(0, PAIRS) as i:
                for p in range(2):
                    step(2 * i + p + 1, 1 - p, True, True)
            step(TILES - 1, 1, False, True)
            for part in (tail_o, tail_xln, tail_x2, tail_m, tail_fc, tail_x1, tail_xf, tail_logits):
                part(TILES - 1)
            dve_late(dve)

        @block.tensor
        def _(pe):
            MM = nc.tensor.matmul
            pe.wait_ge(const_dve, 6)
            pe.wait_ge(wba_loaded, 16 * 2)
            def pre_transposes(b, p):
                pe.wait_ge(pre_h, b + 1)
                for n in range(2):
                    for c in range(2):
                        for k in range(KD):
                            j = (c * KD + k) * P
                            last = nc.tensor.transpose(pre_ps[p % 2][n][:, j:j + P], hb[p % 2][:, 2 * n + c, k * P:(k + 1) * P], ident[:, :])
                    last.then_inc(pre_tr, 1)

            def pre_small(b, p):
                pe.wait_ge(pre_hT, 2 * b + 2)
                pe.wait_ge(ba_ready, b + 1)
                for c in range(CHUNKS):
                    for k in range(KD):
                        last = MM(psB[p % 2][:, c * 2 * H:(c + 1) * 2 * H], hTb[p][:, c, k, :], wba[:, k, :], start=k == 0, stop=k == KD - 1)
                last.then_inc(pre_ba, 1)

            with pe.Fori(0, BATCH // NB) as i:
                for p in range(NB + 1):
                    if p < NB:
                        pre_transposes(NB * i + p, p)
                    if p > 0:
                        pre_small(NB * i + p - 1, p - 1)

            def front_bank(f, u):
                pe.wait_ge(front_evac[u % 2], f_evac(f, u) - 1)
                return psF[u % 2], front_filled[u % 2]

            def back_bank(t, u):
                pe.wait_ge(back_evac[u % 2], b_evac(t, u) - 1)
                return psB[u % 2], back_filled[u % 2]

            def project(f, q, n):
                ps, filled = front_bank(f, FU_PROJ + n)
                s = slice(n % 2 * GW, (n % 2 + 1) * GW)
                if n == 4:
                    pe.wait_ge(h_split, f + 1)
                for k in range(KD):
                    if n < 4:
                        last = MM(ps[:, :], hT[:, q, k, :], wqk[:, n // 2, k, s], start=k == 0, stop=k == KD - 1)
                    else:
                        last = exact(MM, ps[:, :], [a[:, k, :] for a in (hT_hi, hT_lo)], [a[:, n // 2 - 2, k, s] for a in (wvg_hi, wvg_lo)], k == 0, k == KD - 1)
                last.then_inc(filled, 1)

            def decay_sums(f, n):
                ps, filled = front_bank(f, FU_D + n)
                MM(ps[:, :], lower[:, :], dT[:, n * HG:(n + 1) * HG, :].rearrange("p h n -> p (h n)"), start=True, stop=True).then_inc(filled, 1)

            def transposes(f, u0, src):
                for n in range(G):
                    ps, filled = front_bank(f, u0 + n)
                    for h in range(HG):
                        c = n * HG + h
                        last = nc.tensor.transpose(ps[:, h * P:(h + 1) * P], src[:, c * DK:(c + 1) * DK], ident[:, :])
                    last.then_inc(filled, 1)

            def delta_products(f, q, n):
                ps, filled = front_bank(f, FU_KKQ + n)
                for h in range(2):
                    c = 2 * n + h
                    last = MM(ps[:, h * 2 * P:(h + 1) * 2 * P], kT[:, c, :], kbqT[:, q, c].rearrange("p a n -> p (a n)"), start=True, stop=True)
                last.then_inc(filled, 1)

            cols = lambda a, c: a[:, c * DK:(c + 1) * DK]
            HP = P // 2

            def start_x(t):
                for g in range(G):
                    pe.wait_ge(y_ready[g], 7 * t + 1)
                    for h in range(HG):
                        last = nc.tensor.transpose(psI[0][g][:, h * P:(h + 1) * P], cols(yi, g * HG + h), ident[:, :])
                    last.then_inc(inv_filled[0][g], 1)

            def level_t(t, p, l):
                for g in range(G):
                    pe.wait_ge(x_ready[g], 6 * t + l)
                    for h in range(HG):
                        last = MM(left(psI[0][g][:, h * HP:(h + 1) * HP], l, 1), aP[:, p, g * HG + h, 0, :], left(cols(xi, g * HG + h), l), start=True, stop=True)
                    last.then_inc(inv_filled[0][g], 1)

            def level_x(t, l):
                for g in range(G):
                    pe.wait_ge(t_ready[g], 6 * t + l)
                    pe.wait_ge(y_ready[g], 7 * t + l)
                    for h in range(HG):
                        c = g * HG + h
                        tm, out_ = ti[:, c * HP:(c + 1) * HP], psI[1][g][:, h * HP:(h + 1) * HP]
                        if l < LEVELS - 1:
                            last = MM(out_, cols(yi, c), tm, start=True, stop=True)
                        else:
                            last = MM(out_[0:HP, :], tm, cols(yi, c)[:, HP:P], start=True, stop=True)
                    last.then_inc(inv_filled[1][g], 1)

            def level_y(t, l):
                for g in range(G):
                    pe.wait_ge(x_ready[g], 6 * t + l + 1)
                    for h in range(HG):
                        last = nc.tensor.transpose(psI[1][g][:, h * P:(h + 1) * P], cols(xi, g * HG + h), ident[:, :])
                    last.then_inc(inv_filled[1][g], 1)

            def heads(t, u, g, left, right):
                ps, filled = back_bank(t, u)
                for h in range(HG):
                    last = MM(ps[:, h * DK:(h + 1) * DK], left(g * HG + h), right(g * HG + h), start=True, stop=True)
                last.then_inc(filled, 1)

            def state_in(t, p):
                for g in range(G):
                    heads(t, BU_KBS + g, g, lambda c: kbqT[:, p, c, 0, :], lambda c: cols(state, c))

            def state_u(t, p):
                for g in range(G):
                    pe.wait_ge(y_ready[g], 7 * t + 7)
                    heads(t, BU_U + g, g, lambda c: cols(yi, c), lambda c: cols(r_s, c))

            def state_q(t, p):
                for g in range(G):
                    heads(t, BU_QS + g, g, lambda c: kbqT[:, p, c, 1, :], lambda c: cols(state, c))

            def state_out(t, p):
                for g in range(G):
                    heads(t, BU_PU + g, g, lambda c: aP[:, p, c, 1, :], lambda c: cols(u_s, c))
                pe.wait_ge(kd_ready, t + 1)
                for g in range(G):
                    heads(t, BU_KDU + g, g, lambda c: cols(kd, c), lambda c: cols(u_s, c))

            def tail_o(t):
                pe.wait_ge(og_ready, t + 1)
                for g in range(G):
                    ps, filled = back_bank(t + 1, BU_OT + g)
                    for h in range(HG):
                        last = nc.tensor.transpose(ps[:, h * P:(h + 1) * P], cols(o_s, g * HG + h), ident[:, :])
                    last.then_inc(filled, 1)

            def tail_wo(t):
                ps, filled = back_bank(t + 1, BU_WO)
                for h in range(H):
                    if h == HG:
                        pe.wait_ge(back_evac[(BU_OT + 1) % 2], b_evac(t + 1, BU_OT + 1))
                    last = MM(ps[:, 0:D], cols(oT, h), wo[:, h, :], start=h == 0, stop=h == H - 1)
                last.then_inc(filled, 1)

            def tail_m(t):
                pe.wait_ge(m_ready, t + 1)
                ps, filled = back_bank(t + 1, BU_MT)
                for k in range(KD):
                    last = nc.tensor.transpose(ps[:, k * P:(k + 1) * P], m_s[:, k * P:(k + 1) * P], ident[:, :])
                last.then_inc(filled, 1)

            def tail_fc(t):
                pe.wait_ge(back_evac[BU_MT % 2], b_evac(t + 1, BU_MT))
                for n in range(2):
                    ps, filled = back_bank(t + 1, BU_FC + n)
                    for fb in range(FB // 2):
                        for k in range(KD):
                            c = (n * (FB // 2) + fb) * P
                            last = MM(ps[:, fb * P:(fb + 1) * P], wfc[:, k, c:c + P], mT[:, k * P:(k + 1) * P], start=k == 0, stop=k == KD - 1)
                    last.then_inc(filled, 1)

            def tail_proj(t):
                ps, filled = back_bank(t + 1, BU_PROJ)
                for fb in range(FB):
                    if fb % (FB // 2) == 0:
                        pe.wait_ge(hid_ready, 2 * t + fb // (FB // 2) + 1)
                    last = MM(ps[:, 0:D], hid[:, fb * P:(fb + 1) * P], wproj[:, fb, :], start=fb == 0, stop=fb == FB - 1)
                last.then_inc(filled, 1)

            def tail_xf(t):
                pe.wait_ge(xf_ready, t + 1)
                ps, filled = back_bank(t + 1, BU_XT)
                for k in range(KD):
                    last = nc.tensor.transpose(ps[:, k * P:(k + 1) * P], xf[:, k * P:(k + 1) * P], ident[:, :])
                last.then_inc(filled, 1)

            def tail_logits(t):
                pe.wait_ge(back_evac[BU_XT % 2], b_evac(t + 1, BU_XT))
                ps, filled = back_bank(t + 1, BU_LG)
                for k in range(KD):
                    last = MM(ps[:, 0:E], xfT[:, k * P:(k + 1) * P], gwT[:, k, :], start=k == 0, stop=k == KD - 1)
                last.then_inc(filled, 1)

            def front_k(f):
                pe.wait_ge(kn_ready, f + 1)
                transposes(f, FU_K, k_s)

            def front_kb(f):
                pe.wait_ge(kb_ready, f + 1)
                transposes(f, FU_KB, kb)

            def front_q(f):
                pe.wait_ge(qn_ready, f + 1)
                transposes(f, FU_Q, q_s)

            def step(t, p, more, tail, turn):
                f, q = t + 1, 1 - p
                if more:
                    pe.wait_ge(hT_loaded[q], 16 * turn + 16)
                    project(f, q, 0), project(f, q, 1)
                for l in range(1, LEVELS):
                    level_t(t, p, l)
                    if more and l <= 3:
                        project(f, q, 2 * l)
                    if tail and l == 2:
                        tail_o(t - 1)
                    if more and l == 4:
                        pe.wait_ge(rhs_ready, f + 1)
                        decay_sums(f, 0), decay_sums(f, 1)
                    if tail and l == 4:
                        tail_m(t - 1)
                    if more and l == 5:
                        front_kb(f)
                    if l == 5:
                        state_in(t, p)
                    if more and l == 6:
                        delta_products(f, q, 0), delta_products(f, q, 1)
                    level_x(t, l)
                    if more and l <= 3:
                        project(f, q, 2 * l + 1)
                    if tail and l == 2:
                        tail_wo(t - 1)
                    if more and l == 4:
                        front_k(f)
                    if tail and l == 4:
                        tail_fc(t - 1)
                    if more and l == 5:
                        front_q(f)
                    if l < LEVELS - 1:
                        level_y(t, l)
                    if tail and l == 5:
                        tail_proj(t - 1)
                state_q(t, p)
                if more:
                    delta_products(f, q, 2)
                state_u(t, p)
                if more:
                    delta_products(f, q, 3)
                state_out(t, p)
                if tail:
                    tail_xf(t - 1)
                if more:
                    start_x(t + 1)
                if tail:
                    tail_logits(t - 1)

            pe.wait_ge(w_loaded, 16 * 2)
            pe.wait_ge(vg_split, 2 * KD)
            pe.wait_ge(hT_loaded[0], 16)
            for n in range(8):
                project(0, 0, n)
            pe_decays(pe)
            pe.wait_ge(rhs_ready, 1)
            decay_sums(0, 0), decay_sums(0, 1)
            front_k(0)
            front_kb(0)
            front_q(0)
            for n in range(4):
                delta_products(0, 0, n)
            start_x(0)
            step(0, 0, True, False, 0)
            pe.wait_ge(tail_loaded, 16 * 3)
            pe.wait_ge(gate_loaded, 16 * 2)
            with pe.Fori(0, PAIRS) as i:
                for p in range(2):
                    step(2 * i + p + 1, 1 - p, True, True, i + 1)
            step(TILES - 1, 1, False, True, 0)
            for part in (tail_o, tail_wo, tail_m, tail_fc, tail_proj, tail_xf, tail_logits):
                part(TILES - 1)
            pe_late(pe)


_INS = ["L0_attn_x", "L0_attn_Wq", "L0_attn_Wk", "L0_attn_Wv", "L0_attn_Wb", "L0_attn_Wa", "L0_attn_A_log",
        "L0_attn_dt_bias", "L0_attn_Wg", "L0_attn_o_norm_w", "L0_attn_Wo", "L0_attn_W_fc", "L0_attn_W_proj",
        "L0_ffn_gate_W", "L0_ffn_W_gate", "L0_ffn_W_up", "L0_ffn_W_down"]


def kernel(**inputs):
    import concourse.bacc as _bacc
    from concourse.bass_utils import run_bass_kernel_spmd as _run

    nc = _bacc.Bacc("TRN2", target_bir_lowering=False, num_devices=1)
    arrays, args = {}, []
    for name in _INS:
        a = np.ascontiguousarray(inputs[name])
        arrays[f"{name}_dram"] = a
        args.append(nc.dram_tensor(f"{name}_dram", a.shape, mybir.dt.from_np(a.dtype), kind="ExternalInput").ap())
    o = nc.dram_tensor("out_dram", (BATCH, SEQ, D), F32, kind="ExternalOutput").ap()
    program(nc, *args, o)
    r = _run(nc, [arrays], core_ids=[0])
    return r.results[0]["out_dram"]
```
